# Optimizing a Trainium2 kernel written in Bass

```python
import numpy as np
import jax
import jax.numpy as jnp

def _softmax(x, axis=-1):
    return jax.nn.softmax(x, axis=axis)

def _gelu(x):
    return jax.nn.gelu(x, approximate=True)

def _silu(x):
    return jax.nn.silu(x)

def _sigmoid(x):
    return jax.nn.sigmoid(x)

def _layernorm(x, axis=-1, eps=1e-05):
    m = jnp.mean(x, axis=axis, keepdims=True)
    v = jnp.var(x, axis=axis, keepdims=True)
    return (x - m) / jnp.sqrt(v + eps)

def _scatter_add(tgt, idx, src, axis=0):
    return tgt.at[idx].add(src)

def _segment_sum(src, seg, n):
    return jax.ops.segment_sum(src, seg, n)
kernel_name = 'mk_vit_tower_d1_tok_img768_r4_95c473'

def setup_inputs(seed: int=0):
    np.random.seed(seed)
    _w = jnp.asarray

    def _rec_inputs():
        import jax
        import jax.numpy as jnp
        _rk = jax.random.key(seed)
        x = -0.00016672 + 0.999947 * jax.random.normal(jax.random.fold_in(_rk, 1), (64, 3, 96, 96), jnp.float32)
        return x
    x = _rec_inputs()

    def _L0_tok_setup():
        import jax, jax.numpy as jnp
        import numpy as np
        PATCH = 16

        def _patchify(x):
            B, C, H, W = x.shape
            Hp, Wp = (H // PATCH, W // PATCH)
            x = x.reshape(B, C, Hp, PATCH, Wp, PATCH)
            x = x.transpose(0, 2, 4, 1, 3, 5)
            return x.reshape(B, Hp * Wp, C * PATCH * PATCH)
        key = jax.random.key(seed)
        k1, k2, k3 = jax.random.split(key, 3)
        B, C, H, W = (64, 3, 96, 96)
        feat = 192
        in_dim = C * PATCH * PATCH
        x = jax.random.normal(k1, (B, C, H, W), dtype=jnp.float32)
        bound = 1.0 / np.sqrt(in_dim)
        W_proj = jax.random.uniform(k2, (feat, in_dim), minval=-bound, maxval=bound, dtype=jnp.float32)
        b_proj = jax.random.uniform(k3, (feat,), minval=-bound, maxval=bound, dtype=jnp.float32)
        return {'x': x, 'W_proj': W_proj, 'b_proj': b_proj}
    _L0_tok_all = _L0_tok_setup()
    _L0_tok_in = {k: v for k, v in _L0_tok_all.items() if k in ('W_proj', 'b_proj')}
    del _L0_tok_all

    def _L0_attn_setup():
        import jax, jax.numpy as jnp
        import numpy as np
        import math
        B, N, DIM = (8, 1024, 192)
        H, D = (12, 64)
        STAGES = 3
        LN_EPS = 1e-05

        def _ln(x, g, b):
            mu = jnp.mean(x, axis=-1, keepdims=True)
            var = jnp.mean(jnp.square(x - mu), axis=-1, keepdims=True)
            return (x - mu) * jax.lax.rsqrt(var + LN_EPS) * g + b

        def _mlp(x, W, b, g, be):
            return jax.nn.gelu(_ln(x @ W + b, g, be), approximate=False)
        key = jax.random.key(seed)
        ks = jax.random.split(key, 16)
        s = lambda i, shape, sc: jax.random.normal(ks[i], shape, jnp.float32) * sc
        return {'x': s(0, (B, N, DIM), 1.0), 'Wq': s(1, (DIM, H * D), DIM ** (-0.5)), 'Wk': s(2, (DIM, H * D), DIM ** (-0.5)), 'Wv': s(3, (DIM, H * D), DIM ** (-0.5)), 'pool_W': s(4, (STAGES, D, D), D ** (-0.5)), 'pool_b': jnp.zeros((STAGES, D), jnp.float32), 'pool_g': jnp.ones((STAGES, D), jnp.float32), 'pool_be': jnp.zeros((STAGES, D), jnp.float32), 'exp_W': s(5, (STAGES, D, D), D ** (-0.5)), 'exp_b': jnp.zeros((STAGES, D), jnp.float32), 'exp_g': jnp.ones((STAGES, D), jnp.float32), 'exp_be': jnp.zeros((STAGES, D), jnp.float32), 'Wo': s(6, (H * D, DIM), (H * D) ** (-0.5)), 'bo': jnp.zeros((DIM,), jnp.float32)}
    _L0_attn_all = _L0_attn_setup()
    _L0_attn_in = {k: v for k, v in _L0_attn_all.items() if k in ('Wq', 'Wk', 'Wv', 'pool_W', 'pool_b', 'pool_g', 'pool_be', 'exp_W', 'exp_b', 'exp_g', 'exp_be', 'Wo', 'bo')}
    del _L0_attn_all

    def _L0_ffn_setup():
        import jax, jax.numpy as jnp
        import numpy as np
        D = 192
        I = 768
        E = 8
        K = 2
        LIMIT = 10.0
        VOCAB = 8192

        def _expert(xf, W1, W2, W3):
            gate = jnp.minimum(xf @ W1, LIMIT)
            up = jnp.clip(xf @ W3, -LIMIT, LIMIT)
            return jax.nn.silu(gate) * up @ W2
        key = jax.random.key(seed)
        ks = jax.random.split(key, 10)
        s = 0.02
        return {'x': jax.random.normal(ks[0], (1, 512, D), dtype=jnp.float32), 'input_ids': jax.random.randint(ks[1], (1, 512), 0, VOCAB, dtype=jnp.int64), 'gate_w': jax.random.normal(ks[2], (D, E), dtype=jnp.float32) * s, 'gate_bias': jnp.zeros((E,), dtype=jnp.float32), 'w1': jax.random.normal(ks[3], (E, D, I), dtype=jnp.float32) * s, 'w2': jax.random.normal(ks[4], (E, I, D), dtype=jnp.float32) * s, 'w3': jax.random.normal(ks[5], (E, D, I), dtype=jnp.float32) * s, 'w1s': jax.random.normal(ks[6], (D, I), dtype=jnp.float32) * s, 'w2s': jax.random.normal(ks[7], (I, D), dtype=jnp.float32) * s, 'w3s': jax.random.normal(ks[8], (D, I), dtype=jnp.float32) * s}
    _L0_ffn_all = _L0_ffn_setup()
    _L0_ffn_in = {k: v for k, v in _L0_ffn_all.items() if k in ('input_ids', 'gate_w', 'gate_bias', 'w1', 'w2', 'w3', 'w1s', 'w2s', 'w3s')}
    del _L0_ffn_all
    return {'x': x, 'L0_tok_W_proj': _L0_tok_in['W_proj'], 'L0_tok_b_proj': _L0_tok_in['b_proj'], 'L0_attn_Wq': _L0_attn_in['Wq'], 'L0_attn_Wk': _L0_attn_in['Wk'], 'L0_attn_Wv': _L0_attn_in['Wv'], 'L0_attn_pool_W': _L0_attn_in['pool_W'], 'L0_attn_pool_b': _L0_attn_in['pool_b'], 'L0_attn_pool_g': _L0_attn_in['pool_g'], 'L0_attn_pool_be': _L0_attn_in['pool_be'], 'L0_attn_exp_W': _L0_attn_in['exp_W'], 'L0_attn_exp_b': _L0_attn_in['exp_b'], 'L0_attn_exp_g': _L0_attn_in['exp_g'], 'L0_attn_exp_be': _L0_attn_in['exp_be'], 'L0_attn_Wo': _L0_attn_in['Wo'], 'L0_attn_bo': _L0_attn_in['bo'], 'L0_ffn_input_ids': _L0_ffn_in['input_ids'], 'L0_ffn_gate_w': _L0_ffn_in['gate_w'], 'L0_ffn_gate_bias': _L0_ffn_in['gate_bias'], 'L0_ffn_w1': _L0_ffn_in['w1'], 'L0_ffn_w2': _L0_ffn_in['w2'], 'L0_ffn_w3': _L0_ffn_in['w3'], 'L0_ffn_w1s': _L0_ffn_in['w1s'], 'L0_ffn_w2s': _L0_ffn_in['w2s'], 'L0_ffn_w3s': _L0_ffn_in['w3s']}

def reference(x, L0_tok_W_proj, L0_tok_b_proj, L0_attn_Wq, L0_attn_Wk, L0_attn_Wv, L0_attn_pool_W, L0_attn_pool_b, L0_attn_pool_g, L0_attn_pool_be, L0_attn_exp_W, L0_attn_exp_b, L0_attn_exp_g, L0_attn_exp_be, L0_attn_Wo, L0_attn_bo, L0_ffn_input_ids, L0_ffn_gate_w, L0_ffn_gate_bias, L0_ffn_w1, L0_ffn_w2, L0_ffn_w3, L0_ffn_w1s, L0_ffn_w2s, L0_ffn_w3s):
    import jax
    import jax.numpy as jnp

    def _L0_tok_ref(x, W_proj, b_proj):
        import jax, jax.numpy as jnp
        import numpy as np
        PATCH = 16

        def _patchify(x):
            B, C, H, W = x.shape
            Hp, Wp = (H // PATCH, W // PATCH)
            x = x.reshape(B, C, Hp, PATCH, Wp, PATCH)
            x = x.transpose(0, 2, 4, 1, 3, 5)
            return x.reshape(B, Hp * Wp, C * PATCH * PATCH)
        patches = _patchify(x)
        return jnp.einsum('bnk,fk->bnf', patches, W_proj) + b_proj

    def _L0_attn_ref(x, Wq, Wk, Wv, pool_W, pool_b, pool_g, pool_be, exp_W, exp_b, exp_g, exp_be, Wo, bo):
        import jax, jax.numpy as jnp
        import numpy as np
        import math
        B, N, DIM = (8, 1024, 192)
        H, D = (12, 64)
        STAGES = 3
        LN_EPS = 1e-05

        def _ln(x, g, b):
            mu = jnp.mean(x, axis=-1, keepdims=True)
            var = jnp.mean(jnp.square(x - mu), axis=-1, keepdims=True)
            return (x - mu) * jax.lax.rsqrt(var + LN_EPS) * g + b

        def _mlp(x, W, b, g, be):
            return jax.nn.gelu(_ln(x @ W + b, g, be), approximate=False)
        b, n, _ = x.shape

        def heads(y):
            return y.reshape(b, n, H, D).transpose(0, 2, 1, 3)
        q = heads(x @ Wq)
        k = heads(x @ Wk)
        v = heads(x @ Wv)
        fmap = lambda t: jax.nn.elu(t) + 1.0
        q = fmap(q)
        k = fmap(k)
        kc, vc = (k, v)
        for i in range(STAGES):
            s = kc.shape[2]
            if s > 1:
                pad = -s % 2
                if pad:
                    kc = jnp.pad(kc, ((0, 0), (0, 0), (0, pad), (0, 0)))
                    vc = jnp.pad(vc, ((0, 0), (0, 0), (0, pad), (0, 0)))
                kc = kc.reshape(b, H, -1, 2, D).mean(axis=3)
                kc = _mlp(kc, pool_W[i], pool_b[i], pool_g[i], pool_be[i])
                vc = vc.reshape(b, H, -1, 2, D).mean(axis=3)
        kc = kc / math.sqrt(kc.shape[2])
        kv = jnp.einsum('bhnd,bhne->bhde', kc, vc)
        out = jnp.einsum('bhnd,bhde->bhne', q, kv)
        k_sum = kc.sum(axis=2, keepdims=True)
        q_k_sum = jnp.sum(q * k_sum, axis=-1, keepdims=True)
        out = out / (q_k_sum + 1e-06)
        for i in reversed(range(STAGES)):
            out = _mlp(out, exp_W[i], exp_b[i], exp_g[i], exp_be[i])
        out = out.transpose(0, 2, 1, 3).reshape(b, n, H * D)
        return out @ Wo + bo

    def _L0_ffn_ref(x, input_ids, gate_w, gate_bias, w1, w2, w3, w1s, w2s, w3s):
        import jax, jax.numpy as jnp
        import numpy as np
        D = 192
        I = 768
        E = 8
        K = 2
        LIMIT = 10.0
        VOCAB = 8192

        def _expert(xf, W1, W2, W3):
            gate = jnp.minimum(xf @ W1, LIMIT)
            up = jnp.clip(xf @ W3, -LIMIT, LIMIT)
            return jax.nn.silu(gate) * up @ W2
        B, T, _ = x.shape
        flat = x.reshape(-1, D)
        N = flat.shape[0]
        scores = jnp.sqrt(jax.nn.softplus(flat @ gate_w))
        routed_scores = scores + gate_bias
        _, indices = jax.lax.top_k(routed_scores, K)
        weights = jnp.take_along_axis(scores, indices, axis=1)
        weights = weights / jnp.clip(weights.sum(axis=-1, keepdims=True), 1e-06)
        combine = jnp.zeros((N, E), dtype=weights.dtype)
        combine = combine.at[jnp.arange(N)[:, None], indices].add(weights)
        y = _expert(flat, w1s, w2s, w3s)
        gate_h = jnp.minimum(jnp.einsum('td,edi->eti', flat, w1), LIMIT)
        up_h = jnp.clip(jnp.einsum('td,edi->eti', flat, w3), -LIMIT, LIMIT)
        h = jax.nn.silu(gate_h) * up_h
        out_e = jnp.einsum('eti,eid->etd', h, w2)
        routed = jnp.einsum('etd,te->td', out_e, combine)
        return (y + routed).reshape(B, T, D)
    h = _L0_tok_ref(x, L0_tok_W_proj, L0_tok_b_proj)
    h = h + _L0_attn_ref(_layernorm(h, axis=-1), L0_attn_Wq, L0_attn_Wk, L0_attn_Wv, L0_attn_pool_W, L0_attn_pool_b, L0_attn_pool_g, L0_attn_pool_be, L0_attn_exp_W, L0_attn_exp_b, L0_attn_exp_g, L0_attn_exp_be, L0_attn_Wo, L0_attn_bo)
    h = h + _L0_ffn_ref(_layernorm(h, axis=-1), L0_ffn_input_ids, L0_ffn_gate_w, L0_ffn_gate_bias, L0_ffn_w1, L0_ffn_w2, L0_ffn_w3, L0_ffn_w1s, L0_ffn_w2s, L0_ffn_w3s)
    return h

_drawn_inputs = setup_inputs


def setup_inputs(seed=0):
    import zlib

    import numpy as np

    out = dict(_drawn_inputs(seed))
    spreads = {'L0_attn_pool_b': (0.0, 0.8),
     'L0_attn_pool_g': (1.0, 0.6),
     'L0_attn_pool_be': (0.0, 0.8),
     'L0_attn_exp_b': (0.0, 0.1),
     'L0_attn_exp_g': (1.0, 0.2),
     'L0_attn_exp_be': (0.0, 0.1),
     'L0_attn_bo': (0.0, 0.1),
     'L0_ffn_gate_bias': (0.0, 0.498)}
    factors = {'L0_ffn_gate_w': 4.918,
     'L0_ffn_w1': 3.313,
     'L0_ffn_w2': 3.303,
     'L0_ffn_w3': 3.307,
     'L0_ffn_w1s': 2.873,
     'L0_ffn_w2s': 2.884,
     'L0_ffn_w3s': 2.877}
    for name, (base, spread) in spreads.items():
        noise = np.random.default_rng([zlib.crc32(name.encode()), seed]).standard_normal(out[name].shape)
        drawn = base * np.exp(spread * noise) if base else spread * noise
        out[name] = jnp.asarray(drawn.astype(out[name].dtype))
    for name, factor in factors.items():
        out[name] = (out[name] * factor).astype(out[name].dtype)
    return out
```

```python
from contextlib import ExitStack

import concourse.bass as bass
from concourse import mybir

F32 = mybir.dt.float32
BF16 = mybir.dt.bfloat16
I32 = mybir.dt.int32
U32 = mybir.dt.uint32
ALU = mybir.AluOpType
ACT = mybir.ActivationFunctionType
AX = mybir.AxisListType
ds = bass.ds

IMAGES, TOKENS_PER_IMAGE = 64, 36
TOKENS = IMAGES * TOKENS_PER_IMAGE
PATCH_DIM, DIM, HEADS, HEAD_DIM = 768, 192, 12, 64
HALF = DIM // 2
STAGES = 3
PAIRS = HEADS // 2
TILE = 128
TILES = TOKENS // TILE
CHUNK = 384
CHUNKS = TOKENS // CHUNK
GROUP_IMAGES = 4
GROUP = GROUP_IMAGES * TOKENS_PER_IMAGE
GROUPS = IMAGES // GROUP_IMAGES
POOLED = 5
GROUP_ROWS = GROUP_IMAGES * POOLED
K1, K2, K3 = TOKENS // 2, TOKENS // 4, IMAGES * POOLED
LN_EPS = 1e-5
DEN_EPS = 1e-6
QUADS = HEADS // 4
EXPERTS, HIDDEN = 8, 768
LIMIT = 10.0
LN_EXP_TABLES = "natural_log_exp_and_others"
SILU_LIMIT = 9.999546021312976
UNITS = 3
UNIT = HIDDEN // UNITS
W13 = 2 * 2 * HIDDEN
W2 = (HIDDEN // 128) * DIM
SHARED = EXPERTS - 1
ROUTED_TILES = 44
N144 = TILES * EXPERTS


def build(nc, dram, out):
    ctx = ExitStack()
    with ctx:
        def sb(name, shape, dt=F32):
            return ctx.enter_context(nc.sbuf_tensor(name, shape, dt))

        def sem(name):
            return ctx.enter_context(nc.semaphore(name))

        resid = sb("resid", [128, TILES, DIM])
        arena = sb("arena", [128, EXPERTS * (W13 + W2)])
        arena_b = sb("arena_b", [128, 8256])
        w13_cols = EXPERTS * W13
        w13_all = arena[0:HALF, 0:w13_cols]
        w2_all = arena[:, w13_cols:w13_cols + EXPERTS * W2]
        PREP, SMALL_LOADS, N_CONST = 7, 6, 49

        def view(base, start, shape):
            n = 1
            for s in shape:
                n *= s
            v = base[:, start:start + n]
            if len(shape) == 1:
                return v
            names = "abc"[:len(shape)]
            return v.rearrange(f"p ({' '.join(names)}) -> p {' '.join(names)}",
                               **{names[i]: shape[i] for i in range(1, len(shape))})

        q_y = view(arena, 0, [PAIRS, TOKENS])
        kp1 = view(arena, 0, [PAIRS, K1])
        kp2 = view(arena, PAIRS * K1, [PAIRS, K2])
        o = PAIRS * TOKENS
        x1T = view(arena, o, [2, TOKENS]); o += 2 * TOKENS
        wo = view(arena, PAIRS * TOKENS, [PAIRS, DIM])
        wq = view(arena, o, [2, HEADS * HEAD_DIM]); o += 2 * HEADS * HEAD_DIM
        wk = view(arena, o, [2, HEADS * HEAD_DIM])
        vw = view(arena, o, [2, PAIRS, 128]); o += 2 * HEADS * HEAD_DIM
        wv = view(arena, o, [2, HEADS * HEAD_DIM])
        vblk = view(arena, o, [2, PAIRS, 128]); o += 2 * HEADS * HEAD_DIM
        patches = view(arena, o, [2, PATCH_DIM // 128, TILE])
        kblk = view(arena, o, [2, PAIRS, 128]); o += 2 * PATCH_DIM
        assert o <= EXPERTS * W13
        o = w13_cols
        var = arena[0:96, o:o + TOKENS]; o += TOKENS
        rstd = arena[0:96, o:o + TOKENS]; o += TOKENS
        rsplit = arena[0:96, o:o + TOKENS // 2].bitcast(BF16); o += TOKENS // 2
        ind = arena[:, o:o + (PAIRS + 1) * 96]; o += (PAIRS + 1) * 96
        wbd = view(arena, o, [2 * STAGES, 128]); o += 2 * STAGES * 128
        kc3_at = w13_cols + EXPERTS * W2 - PAIRS * K3
        assert o <= kc3_at <= w13_cols + (EXPERTS - 1) * W2
        kc3 = view(arena, kc3_at, [PAIRS, K3])
        gath = view(arena, 0, [3, 2, DIM])
        o = 0
        vcT = view(arena_b, o, [PAIRS, K3]); o += PAIRS * K3
        xp = view(arena_b, o, [2 * IMAGES, POOLED]); o += 2 * IMAGES * POOLED
        sqb = view(arena_b, o, [3, CHUNK]); o += 3 * CHUNK
        zb = view(arena_b, o, [3, CHUNK]); o += 3 * CHUNK
        gb = view(arena_b, o, [3, CHUNK]); o += 3 * CHUNK
        wp = view(arena_b, o, [PATCH_DIM // 128, DIM]); o += (PATCH_DIM // 128) * DIM
        sm = view(arena_b, PAIRS * K3 + 2 * IMAGES * POOLED, [2, QUADS, GROUP])
        sn = view(arena_b, PAIRS * K3 + 2 * IMAGES * POOLED + 3 * CHUNK, [2, QUADS, GROUP])
        sq = view(arena_b, PAIRS * K3 + 2 * IMAGES * POOLED + 6 * CHUNK, [PAIRS, GROUP])
        o = 0
        x2r = view(arena_b, o, [TILES, DIM]); o += TILES * DIM
        sgate = view(arena_b, o, [3, UNIT]); o += 3 * UNIT
        sup = view(arena_b, o, [3, UNIT]); o += 3 * UNIT
        hid = view(arena_b, o, [3, UNIT]); o += 3 * UNIT
        zrow = arena_b[:, o - 3 * UNIT:o + 3 * UNIT]
        hidT = view(arena_b, o, [3, 2, 128]); o += 3 * UNIT
        rt = view(arena_b, o, [12, N144]); o += 12 * N144
        assert o <= 8256

        vecs = sb("vecs", [128, 6 * STAGES])
        bcen = sb("bcen", [128, 2 * STAGES])
        wsum = sb("wsum", [128, 2 * STAGES])
        wmean = sb("wmean", [128, 2 * STAGES])
        bproj = sb("bproj", [128, DIM])
        bo = sb("bo", [128, DIM])
        bboth = sb("bboth", [128, DIM])
        gbias = sb("gbias", [128, EXPERTS])
        gatew = sb("gatew", [HALF, 2, EXPERTS])
        ident = sb("ident", [128, 128])
        ones = sb("ones", [128, 128])
        upper = sb("upper", [128, 128])
        blk64 = sb("blk64", [128, 128])
        ind_den = sb("ind_den", [128, QUADS * 96 + 96])
        sel = sb("sel", [96, PAIRS, 128], BF16)
        sel_den = sb("sel_den", [96, QUADS, 128], BF16)
        mask = sb("mask", [128, GROUP])
        eps = sb("eps", [128, 1])
        hrow = sb("hrow", [128, 2, DIM])
        xrow = sb("xrow", [128, 2, DIM])
        xT = sb("xT", [HALF, 2, 2, TILE])
        stats = sb("stats", [128, 2, 6])
        mv1 = sb("mv1", [128, 2, 2])
        lnv = sb("lnv", [128, 2])
        rs1 = sb("rs1", [128, 2])
        mv2 = sb("mv2", [128, TILES, 2])
        ln2 = sb("ln2", [128, TILES])
        rs2 = sb("rs2", [128, TILES])
        den = sb("den", [96, GROUP])
        rden = sb("rden", [96, GROUP])
        dsplit = sb("dsplit", [96, GROUP], BF16)
        tab = sb("tab", [1, ROUTED_TILES + 1], I32)
        small = sb("small", [128, 12, TILES])
        iota_e = sb("iota_e", [128, N144])
        iota_tok = sb("iota_tok", [128, N144])
        iota_tile = sb("iota_tile", [1, ROUTED_TILES, EXPERTS])
        cmp_tile = sb("cmp_tile", [1, ROUTED_TILES, EXPERTS])
        tile_expert = sb("tile_expert", [1, ROUTED_TILES])
        ecount = sb("ecount", [128, 6, EXPERTS])
        slot = sb("slot", [128, 2, TILES], U32)
        orow = sb("orow", [128, 3, DIM])

        bank = [ctx.enter_context(nc.psum_tensor(f"bank{i}", [128, 512], F32)) for i in range(8)]

        consts_set = sem("consts_set")
        small_in = sem("small_in")
        wqkv_in = sem("wqkv_in")
        wbd_in = sem("wbd_in")
        prep = sem("prep")
        bmean_ready = sem("bmean_ready")
        wo_in = sem("wo_in")
        blocks_zero = sem("blocks_zero")
        last_in = sem("last_in")
        shared_in = sem("shared_in")
        experts_in = sem("experts_in")
        block = ctx.enter_context(nc.Block())

        patch_in = [sem(f"patch_in{b}") for b in range(2)]
        embedded = sem("embedded")
        emb_read = sem("emb_read")
        ln1_dve = sem("ln1_dve")
        ln1_stat = sem("ln1_stat")
        ln1_act = sem("ln1_act")
        x1_ready = sem("x1_ready")
        x1T_ps = sem("x1T_ps")
        x1T_ready = sem("x1T_ready")

        class Pass:
            def __init__(self, name):
                self.y_ps = sem(f"{name}_y_ps")
                self.y_sq = sem(f"{name}_y_sq")
                self.y_out = sem(f"{name}_y_out")
                self.sums = sem(f"{name}_sums")
                self.var_out = sem(f"{name}_var_out")
                self.rb_ps = sem(f"{name}_rb_ps")
                self.z_out = sem(f"{name}_z_out")
                self.g_out = sem(f"{name}_g_out")
                self.next_out = sem(f"{name}_next_out")

        k_f = sem("k_proj_ps"), sem("k_exp"), sem("k_min"), sem("k_map"), sem("k_pooled")
        q_f = sem("q_proj_ps"), sem("q_exp"), sem("q_min"), sem("q_map")
        ks = [Pass(f"k{i}") for i in range(3)]
        es = [Pass(f"e{i}") for i in range(3)]
        rchain = sem("rchain")
        r_ready = sem("r_ready")
        r_log = sem("r_log")
        r_exp = sem("r_exp")
        k_main = sem("k_main")
        v_ps = sem("v_ps")
        v_out = sem("v_out")
        xp_out = sem("xp_out")
        vfree = sem("vfree")

        def bias_of(s):
            return bcen[:, s:s + 1]

        def gain_of(s):
            return vecs[:, 6 + s:7 + s]

        def shift_of(s):
            return vecs[:, 12 + s:13 + s]


        def f_pe(pe, P, src, w, n, c, p, first_wait):
            first_wait()
            pe.wait_ge(P.y_out, c * PAIRS + p + 1)
            pe.wait_ge(P.y_sq, c * PAIRS + p + 1)
            pe.matmul(bank[3 + p % 3][:, 0:n], w, src, start=True, stop=True).then_inc(P.y_ps, 1)

        def s_pe(pe, P, n, c, p):
            pe.wait_ge(P.y_sq, c * PAIRS + p + 4)
            if p == 0:
                pe.wait_ge(P.var_out, c + 1)
            pe.matmul(bank[6][0:96, 0:n], ind[:, 96 * p:96 * p + 96], sqb[:, p % 3, 0:n],
                      start=(p == 0), stop=(p == PAIRS - 1)).then_inc(P.sums, 1)

        def f_act(act, P, s, n, c, p):
            act.wait_ge(P.y_ps, c * PAIRS + p + 1)
            act.wait_ge(P.sums, c * PAIRS + p + 1)
            act.activation(sqb[:, p % 3, 0:n], bank[3 + p % 3][:, 0:n], ACT.Square,
                           bias=bias_of(s)).then_inc(P.y_sq, 1)

        def f_dve(dve, P, s, dst, n, c, p):
            dve.wait_ge(P.y_sq, c * PAIRS + p + 4)
            dve.tensor_scalar(dst, bank[3 + p % 3][:, 0:n], bias_of(s), None,
                              ALU.add).then_inc(P.y_out, 1)

        def var_dve(dve, P, n, c):
            dve.wait_ge(P.sums, c * PAIRS + PAIRS + 3)
            dve.tensor_copy(var[:, ds(c * n, n)], bank[6][0:96, 0:n]).then_inc(P.var_out, 1)

        def r_act(act, P, chunks, length, n):
            act.preload_act_table_set(LN_EXP_TABLES)
            act.wait_ge(P.var_out, chunks + 1)
            act.activation(var[:, 0:length], var[:, 0:length], ACT.Ln, bias=eps[0:96, :]).then_inc(r_log, 1)
            act.wait_ge(r_log, n + 1)
            act.activation(rstd[:, 0:length], var[:, 0:length], ACT.Exp, scale=-0.5).then_inc(r_exp, 1)

        def split_dve(dve, src, dst, length, chain, n):
            dve.tensor_copy(dst[:, 0:length], src[:, 0:length]).then_inc(chain, 1)
            dve.wait_ge(chain, n + 1)
            dve.tensor_tensor(src[:, 0:length], src[:, 0:length], dst[:, 0:length],
                              ALU.subtract).then_inc(chain, 1)
            dve.wait_ge(chain, n + 2)
            dve.tensor_copy(dst[32:64, 0:length], src[32:64, 0:length]).then_inc(chain, 1)
            dve.tensor_copy(dst[64:96, 0:length], src[64:96, 0:length]).then_inc(chain, 1)
            dve.wait_ge(chain, n + 4)
            return dve.tensor_tensor(dst[64:96, 0:length], src[64:96, 0:length], dst[64:96, 0:length],
                                     ALU.subtract)

        def r_dve(dve, length, n):
            dve.wait_ge(r_exp, n + 1)
            split_dve(dve, rstd, rsplit, length, rchain, 4 * n).then_inc(r_ready, 1)

        def b_pe(pe, P, n, c, p):
            pe.wait_ge(P.z_out, c * PAIRS + p + 1)
            pe.matmul(bank[p % 3][:, 0:n], sel[:, p, :], rsplit[:, ds(c * n, n)],
                      start=True, stop=True).then_inc(P.rb_ps, 1)

        def z_dve(dve, P, src, n, c, p):
            dve.wait_ge(P.rb_ps, c * PAIRS + p + 1)
            dve.wait_ge(P.g_out, c * PAIRS + p + 1)
            dve.tensor_tensor(zb[:, p % 3, 0:n], src, bank[p % 3][:, 0:n], ALU.mult).then_inc(P.z_out, 1)

        def g_act(act, P, s, n, c, p, consumed=True):
            act.wait_ge(P.z_out, c * PAIRS + p + 4)
            if consumed:
                act.wait_ge(P.next_out, c * PAIRS + p + 1)
            act.activation(gb[:, p % 3, 0:n], zb[:, p % 3, 0:n], ACT.Gelu, bias=shift_of(s),
                           scale=gain_of(s)).then_inc(P.g_out, 1)

        KSTAGE = [(kp1, CHUNK, K1 // CHUNK), (kp2, K2 // 2, 2), (kc3, K3, 1)]

        def loop(eng, n, body):
            if n == 1:
                body(0)
            else:
                with eng.Fori(0, n) as c:
                    body(c)

        core_kv = sem("core_kv")
        core_vw = sem("core_vw")
        core_vw_out = sem("core_vw_out")
        core_s = sem("core_s")
        core_sm = sem("core_sm")
        core_den = sem("core_den")
        core_chain = sem("core_chain")
        core_r = sem("core_r")
        core_rb = sem("core_rb")
        core_sn = sem("core_sn")
        core_y = sem("core_y")
        core_sq = sem("core_sq")
        core_y_out = sem("core_y_out")
        core_sum = sem("core_sum")
        core_var = sem("core_var")

        mv_out = sem("mv_out")
        wo_read = sem("wo_read")
        ln2_chain = sem("ln2_chain")
        ln2_log = sem("ln2_log")
        ln2_r = sem("ln2_r")
        x2_out = sem("x2_out")
        x2T_ps = sem("x2T_ps")
        x2T_out = sem("x2T_out")
        logit_ps = sem("logit_ps")
        logit_out = sem("logit_out")
        rt_step = sem("rt_step")
        zrow_set = sem("zrow_set")
        rt_abs = sem("rt_abs")
        rt_exp = sem("rt_exp")
        rt_ln = sem("rt_ln")
        rt_sp = sem("rt_sp")
        rt_sqrt = sem("rt_sqrt")
        rt_masks = sem("rt_masks")
        rt_prefix = sem("rt_prefix")
        prefix_read = sem("prefix_read")
        tab_ready = sem("tab_ready")
        slots_ready = sem("slots_ready")
        scattered = sem("scattered")
        zeroed = sem("zeroed")
        row_in = [sem(f"row_in{b}") for b in range(2)]
        row_used = sem("row_used")
        xT_ps = sem("xT_ps")
        xT_out = sem("xT_out")
        gu_ps = sem("gu_ps")
        silu_out = sem("silu_out")
        up_out = sem("up_out")
        hid_out = sem("hid_out")
        hidT_ps = sem("hidT_ps")
        hidT_out = sem("hidT_out")
        y_ps = sem("y_ps")
        y_read = sem("y_read")
        y_stored = [sem(f"y_stored{b}") for b in range(2)]
        gathered = [sem(f"gathered{b}") for b in range(3)]
        comb = sem("comb")
        comb_step = sem("comb_step")
        stored = [sem(f"stored{b}") for b in range(3)]

        KB = PATCH_DIM // 128

        @block.sync
        def _(sp):
            def load_patch(t, b):
                sp.dma_start(patches[:, b], dram["patches"][ds(t, 1)].rearrange("a p k n -> p (a k) n")
                             ).then_inc(patch_in[b], 16)
            load_patch(0, 0)
            load_patch(1, 1)
            with sp.Fori(0, TILES // 2 - 1) as it:
                for b in range(2):
                    sp.wait_ge(embedded, it * 2 + b + 1)
                    load_patch(it * 2 + 2 + b, b)
            sp.wait_ge(q_f[3], CHUNKS * PAIRS + 3)
            sp.dma_start(wo, dram["wo"]).then_inc(wo_in, 16)
            sp.wait_ge(core_y_out, 2 * GROUPS + 2)
            sp.dma_start(w13_all[:, SHARED * W13:(SHARED + 1) * W13], dram["w13"][EXPERTS]).then_inc(shared_in, 16)
            sp.dma_start(w2_all[:, SHARED * W2:(SHARED + 1) * W2], dram["w2"][EXPERTS]).then_inc(shared_in, 16)

            sp.wait_ge(x2_out, 2 * TILES)
            def load_row(src, b):
                sp.dma_start(xrow[:, b, :], src).then_inc(row_in[b], 16)
            sp.wait_ge(x2T_ps, TILES)
            for b in range(2):
                load_row(x2r[:, b, :], b)
            with sp.Fori(0, TILES // 2 - 1) as it:
                for b in range(2):
                    sp.wait_ge(row_used, it * 2 + b + 1)
                    load_row(x2r[:, ds(it * 2 + 2 + b, 1), :], b)
            for n in range(2):
                sp.wait_ge(scattered, 16 * 2 * TILES) if n == 0 else None
                sp.wait_ge(row_used, TILES - 1 + n)
                load_row(dram["slots"][n * TILE:(n + 1) * TILE, :], n)
            with sp.Fori(0, ROUTED_TILES // 2 - 1) as it:
                for b in range(2):
                    sp.wait_ge(row_used, it * 2 + b + 1 + TILES)
                    load_row(dram["slots"][ds((it * 2 + 2 + b) * TILE, TILE), :], b)

        @block.gpsimd
        def _(pool):
            n_const = [0]

            def const(ins):
                ins.then_inc(consts_set, 1)
                n_const[0] += 1
                pool.wait_ge(consts_set, n_const[0])

            const(pool.memset(ident[:, :], 0.0))
            const(pool.memset(ones[:, :], 1.0))
            const(pool.memset(blk64[:, :], 0.0))
            const(pool.memset(eps[:, :], LN_EPS))
            const(pool.memset(wbd[:, :, :], 0.0))
            const(pool.memset(ind[:, :], 0.0))
            const(pool.memset(ind_den[:, :], 0.0))
            const(pool.memset(sel[:, :, :], 0.0))
            const(pool.memset(sel_den[:, :, :], 0.0))
            const(pool.memset(mask[:, :], float(POOLED) ** -0.5))
            const(pool.affine_select(out=ident[:, :], in_=ident[:, :], compare_op=ALU.not_equal, fill=1.0,
                                     base=0, pattern=[[-1, 128]], channel_multiplier=1))
            const(pool.affine_select(out=upper[:, :], in_=ones[:, :], compare_op=ALU.is_ge, fill=0.0,
                                     base=-1, pattern=[[1, 128]], channel_multiplier=-1))
            for a in range(2):
                rows = slice(64 * a, 64 * a + 64)
                const(pool.memset(blk64[rows, 64 * a:64 * a + 64], 1.0 / HEAD_DIM))
                for r in range(3):
                    first = 32 * r + a
                    const(pool.memset(ind[rows, first:first + 98 * (PAIRS - 1) + 1:98], 1.0 / HEAD_DIM))
            for j in range(4):
                for r in range(3):
                    first = 32 * r + j
                    const(pool.memset(ind_den[32 * j:32 * j + 32, first:first + 100 * (QUADS - 1) + 1:100], 1.0))
            for r in range(3):
                rows = slice(32 * r, 32 * r + 32)
                v = sel[rows, :, :].rearrange("k p (h j) -> k p h j", h=2)
                const(pool.affine_select(out=v, in_=v, compare_op=ALU.not_equal, fill=1.0, base=0,
                                         pattern=[[-2, PAIRS], [-1, 2], [0, 64]], channel_multiplier=1))
                v = sel_den[rows, :, :].rearrange("k q (h j) -> k q h j", h=4)
                const(pool.affine_select(out=v, in_=v, compare_op=ALU.not_equal, fill=1.0, base=0,
                                         pattern=[[-4, QUADS], [-1, 4], [0, 32]], channel_multiplier=1))
            for j in range(4):
                m = mask[32 * j:32 * j + 32, :].rearrange("k (i t) -> k i t", i=GROUP_IMAGES)
                const(pool.affine_select(out=m, in_=m, compare_op=ALU.is_ge, fill=0.0, base=0,
                                         pattern=[[-POOLED, GROUP_IMAGES], [0, TOKENS_PER_IMAGE]], channel_multiplier=1))
            for j in range(4):
                m = mask[32 * j:32 * j + 32, :].rearrange("k (i t) -> k i t", i=GROUP_IMAGES)
                const(pool.affine_select(out=m, in_=m, compare_op=ALU.is_ge, fill=0.0, base=POOLED - 1,
                                         pattern=[[POOLED, GROUP_IMAGES], [0, TOKENS_PER_IMAGE]], channel_multiplier=-1))
            const(pool.iota(iota_e[:, :], [[0, TILES], [1, EXPERTS]], base=0, channel_multiplier=0,
                            allow_small_or_imprecise_dtypes=True))
            const(pool.iota(iota_tok[:, :], [[0, EXPERTS], [TILE, TILES]], base=0, channel_multiplier=0,
                            allow_small_or_imprecise_dtypes=True))
            const(pool.iota(iota_tile[:, :, :], [[1, ROUTED_TILES], [0, EXPERTS]], base=0, channel_multiplier=0,
                            allow_small_or_imprecise_dtypes=True))
            assert n_const[0] == N_CONST, n_const[0]
            pool.wait_ge(v_out, PAIRS)
            pool.wait_ge(ks[0].y_ps, 1)
            for blocks in (kblk, vblk, vw):
                pool.memset(blocks, 0.0).then_inc(blocks_zero, 1)
            pool.wait_ge(blocks_zero, 3)
            pool.wait_ge(ks[2].g_out, PAIRS + 3)
            with pool.Fori(0, GROUPS // 2) as it:
                for b in range(2):
                    g = it * 2 + b
                    pool.wait_ge(core_s, g + 1)
                    for src, dst in ((kc3, kblk), (vcT, vblk)):
                        for odd in range(2):
                            for a in range(2):
                                rows = slice(64 * a, 64 * a + 64)
                                first = 64 * odd + 32 * a
                                pool.tensor_copy(
                                    dst[rows, b, odd::2, first:first + GROUP_ROWS],
                                    src[rows, odd::2, ds(g * GROUP_ROWS, GROUP_ROWS)]).then_inc(core_kv, 1)
            pool.wait_ge(wo_read, TILES + 3)
            pool.memset(zrow, 0.0).then_inc(zrow_set, 1)
            pool.wait_ge(zrow_set, 1)
            for e in range(EXPERTS - 1):
                pool.dma_start(w13_all[:, e * W13:(e + 1) * W13], dram["w13"][e]).then_inc(experts_in, 16)
                pool.dma_start(w2_all[:, e * W2:(e + 1) * W2], dram["w2"][e]).then_inc(experts_in, 16)
            n0 = 8 * TILE
            for z in range(6):
                lo, hi = z * n0, min((z + 1) * n0, ROUTED_TILES * TILE)
                k = (hi - lo) // TILE
                pool.dma_start(dram["slots"][lo:hi, :].rearrange("(p a) d -> p (a d)", p=128),
                               zrow[:, 0:k * DIM]).then_inc(zeroed, 16)
            pool.wait_ge(zeroed, 16 * 6)
            pool.wait_ge(slots_ready, 1)
            for t in range(TILES):
                for k in range(2):
                    pool.indirect_dma_start(dram["slots"][:, :], bass.IndirectOffsetOnAxis(slot[:, k, t:t + 1], 0),
                                            x2r[:, t, :], None).then_inc(scattered, 16)
            pool.wait_ge(y_ps, TILES * UNITS)
            pool.dma_start(w13_all[:, SHARED * W13:(SHARED + 1) * W13], dram["w13"][SHARED]).then_inc(last_in, 16)
            pool.dma_start(w2_all[:, SHARED * W2:(SHARED + 1) * W2], dram["w2"][SHARED]).then_inc(last_in, 16)
            with pool.Fori(0, ROUTED_TILES // 2) as it:
                for b in range(2):
                    m = it * 2 + b
                    pool.wait_ge(y_read, m + TILES + 2)
                    pool.dma_start(dram["expert_out"][ds(m * TILE, TILE), :], orow[:, b, :]).then_inc(y_stored[b], 16)
            for b in range(2):
                pool.wait_ge(y_stored[b], 16 * (ROUTED_TILES // 2))
            for t in range(TILES):
                b = t % 3
                if t >= 3:
                    pool.wait_ge(comb, t - 2)
                for k in range(2):
                    pool.indirect_dma_start(gath[:, b, k, :], None, dram["expert_out"][:, :],
                                            bass.IndirectOffsetOnAxis(slot[:, k, t:t + 1], 0)).then_inc(gathered[b], 16)

        @block.tensor
        def _(pe):
            pe.wait_ge(consts_set, N_CONST)
            pe.wait_ge(small_in, 16 * SMALL_LOADS)
            pe.matmul(bank[7][:, 0:2 * STAGES], blk64[:, :], vecs[:, 0:2 * STAGES], start=True,
                      stop=True).then_inc(bmean_ready, 1)

            def embed(it, b):
                t = it * 2 + b
                pe.wait_ge(patch_in[b], (it + 1) * 16)
                pe.wait_ge(emb_read, t + 1)
                for k in range(KB):
                    mm = pe.matmul(bank[b][:, 0:DIM], patches[:, b, k, :], wp[:, k, :],
                                   start=(k == 0), stop=(k == KB - 1))
                mm.then_inc(embedded, 1)

            def turn_x1(it, b):
                t = it * 2 + b
                pe.wait_ge(x1_ready, t + 1)
                pe.wait_ge(x1T_ready, t + 1)
                for h in range(2):
                    mm = pe.transpose(bank[2 + b][0:HALF, h * TILE:(h + 1) * TILE],
                                      xrow[:, b, h * HALF:(h + 1) * HALF], ident[:, :])
                mm.then_inc(x1T_ps, 1)

            embed(0, 0)
            with pe.Fori(0, TILES // 2 - 1) as it:
                embed(it, 1)
                turn_x1(it, 0)
                embed(it + 1, 0)
                turn_x1(it, 1)
            embed(TILES // 2 - 1, 1)
            turn_x1(TILES // 2 - 1, 0)
            turn_x1(TILES // 2 - 1, 1)

            pe.wait_ge(x1T_ready, TILES + 2)
            pe.wait_ge(wqkv_in, 48)
            pe.wait_ge(xp_out, 2)
            xpf = xp.rearrange("p (h i) r -> p h (i r)", h=2)
            for p in range(PAIRS):
                if p >= 2:
                    pe.wait_ge(v_out, p - 1)
                for h in range(2):
                    mm = pe.matmul(bank[4 + p % 2][:, 0:K3], wv[0:HALF, h, p * 128:(p + 1) * 128],
                                   xpf[0:HALF, h, :], start=(h == 0), stop=(h == 1))
                mm.then_inc(v_ps, 1)
            def project(w, ps_sem, free_sem, c, p):
                pe.wait_ge(free_sem, c * PAIRS + p + 1)
                for h in range(2):
                    mm = pe.matmul(bank[p % 3][:, 0:CHUNK], w[0:HALF, h, p * 128:(p + 1) * 128],
                                   x1T[0:HALF, h, ds(c * CHUNK, CHUNK)], start=(h == 0), stop=(h == 1))
                mm.then_inc(ps_sem, 1)
            pe.wait_ge(emb_read, TILES + 2)
            with pe.Fori(0, CHUNKS) as c:
                for p in range(PAIRS):
                    project(wk, k_f[0], k_f[3], c, p)
            pe.wait_ge(prep, PREP)
            for i in range(STAGES):
                buf, n, chunks = KSTAGE[i]
                if i == 0:
                    pe.wait_ge(k_f[4], CHUNKS * PAIRS + 3)
                    pe.wait_ge(v_out, PAIRS)
                else:
                    pe.wait_ge(ks[i - 1].next_out, 3 + KSTAGE[i - 1][2] * PAIRS)

                def f_body(c):
                    for p in range(PAIRS):
                        f_pe(pe, ks[i], buf[:, p, ds(c * n, n)], wbd[:, i, :], n, c, p, lambda: None)
                        if p:
                            s_pe(pe, ks[i], n, c, p - 1)
                    s_pe(pe, ks[i], n, c, PAIRS - 1)
                loop(pe, chunks, f_body)
                pe.wait_ge(r_ready, i + 1)

                def g_body(c):
                    for p in range(PAIRS):
                        b_pe(pe, ks[i], n, c, p)
                loop(pe, chunks, g_body)
            pe.wait_ge(ks[2].z_out, 3 + PAIRS)
            with pe.Fori(0, CHUNKS) as c:
                for p in range(PAIRS):
                    project(wq, q_f[0], q_f[3], c, p)
            pe.wait_ge(q_f[3], 3 + CHUNKS * PAIRS)

            def core_a(it, b):
                g = it * 2 + b
                pe.wait_ge(core_kv, (g + 1) * 8)
                pe.wait_ge(core_vw_out, g * 2 + 2)
                for p in range(PAIRS):
                    mm = pe.matmul(bank[0][:, (p // 2) * 128:(p // 2) * 128 + 128], vblk[:, b, p, :],
                                   wbd[:, 2 * STAGES - 1, :], start=(p % 2 == 0), stop=(p % 2 == 1))
                mm.then_inc(core_vw, 1)
                pe.wait_ge(core_sm, g + 1)
                for p in range(PAIRS):
                    mm = pe.matmul(bank[1][:, (p // 2) * GROUP:(p // 2 + 1) * GROUP], kblk[:, b, p, :],
                                   q_y[:, p, ds(g * GROUP, GROUP)], start=(p % 2 == 0), stop=(p % 2 == 1))
                mm.then_inc(core_s, 1)

            def core_d(it, b):
                g = it * 2 + b
                pe.wait_ge(core_sm, g + 2)
                pe.wait_ge(core_chain, g * 6 + 1)
                for q in range(QUADS):
                    mm = pe.matmul(bank[2][0:96, 0:GROUP], ind_den[:, 96 * q:96 * q + 96], sm[:, b, q, :],
                                   start=(q == 0), stop=(q == QUADS - 1))
                mm.then_inc(core_den, 1)

            def core_b(it, b):
                g = it * 2 + b
                pe.wait_ge(core_r, g + 1)
                pe.wait_ge(core_sn, g + 1)
                for q in range(QUADS):
                    mm = pe.matmul(bank[3][:, q * GROUP:(q + 1) * GROUP], sel_den[:, q, :], dsplit[:, :],
                                   start=True, stop=True)
                mm.then_inc(core_rb, 1)

            def core_yy(it, b):
                g = it * 2 + b
                pe.wait_ge(core_sn, g + 2)
                pe.wait_ge(core_vw_out, g * 2 + 4)
                pe.wait_ge(core_y_out, g * 2 + 2)
                pe.wait_ge(core_sq, g * 2 + 2)
                for p in range(PAIRS):
                    mm = pe.matmul(bank[4 + p // 3][:, (p % 3) * GROUP:(p % 3 + 1) * GROUP],
                                   vw[:, b, p, :], sn[:, b, p // 2, :], start=True, stop=True)
                mm.then_inc(core_y, 1)

            def core_st(it, b):
                g = it * 2 + b
                pe.wait_ge(core_sq, g * 2 + 4)
                pe.wait_ge(core_var, g + 1)
                for p in range(PAIRS):
                    mm = pe.matmul(bank[6][0:96, 0:GROUP], ind[:, 96 * p:96 * p + 96], sq[:, p, :],
                                   start=(p == 0), stop=(p == PAIRS - 1))
                mm.then_inc(core_sum, 1)

            def core_step(it, b, last=False):
                core_b(it, b)
                if not last:
                    core_a(it + b, 1 - b)
                core_yy(it, b)
                if not last:
                    core_d(it + b, 1 - b)
                core_st(it, b)
            core_a(0, 0)
            core_d(0, 0)
            with pe.Fori(0, GROUPS // 2 - 1) as it:
                core_step(it, 0)
                core_step(it, 1)
            core_step(GROUPS // 2 - 1, 0)
            core_step(GROUPS // 2 - 1, 1, last=True)

            for i in range(STAGES - 1):
                G, Fn = es[i], es[i + 1]
                pe.wait_ge(r_ready, STAGES + i + 1)

                def gf_body(c, more):
                    for p in range(PAIRS):
                        if p + 2 < PAIRS:
                            b_pe(pe, G, CHUNK, c, p + 2)
                        elif more:
                            b_pe(pe, G, CHUNK, c + 1, p + 2 - PAIRS)
                        f_pe(pe, Fn, gb[:, p % 3, :], wbd[:, 2 * STAGES - 2 - i, :], CHUNK, c, p,
                             lambda: pe.wait_ge(G.g_out, c * PAIRS + p + 4))
                        if p:
                            s_pe(pe, Fn, CHUNK, c, p - 1)
                    s_pe(pe, Fn, CHUNK, c, PAIRS - 1)
                b_pe(pe, G, CHUNK, 0, 0)
                b_pe(pe, G, CHUNK, 0, 1)
                with pe.Fori(0, CHUNKS - 1) as c:
                    gf_body(c, True)
                gf_body(CHUNKS - 1, False)
            pe.wait_ge(r_ready, 2 * STAGES)
            G = es[2]
            pe.wait_ge(wo_in, 16)
            pe.wait_ge(G.y_out, 3 + CHUNKS * PAIRS)

            def go_body(c, more):
                for p in range(PAIRS):
                    if p + 2 < PAIRS:
                        b_pe(pe, G, CHUNK, c, p + 2)
                    elif more:
                        b_pe(pe, G, CHUNK, c + 1, p + 2 - PAIRS)
                    pe.wait_ge(G.g_out, c * PAIRS + p + 4)
                    for j in range(3):
                        if p == 0:
                            pe.wait_ge(wo_read, c * 3 + j + 1)
                        mm = pe.matmul(bank[3 + j][:, 0:DIM], gb[:, p % 3, j * TILE:(j + 1) * TILE], wo[:, p, :],
                                       start=(p == 0), stop=(p == PAIRS - 1))
                    mm.then_inc(G.next_out, 1)
            b_pe(pe, G, CHUNK, 0, 0)
            b_pe(pe, G, CHUNK, 0, 1)
            with pe.Fori(0, CHUNKS - 1) as c:
                go_body(c, True)
            go_body(CHUNKS - 1, False)

            pe.wait_ge(G.z_out, 3 + CHUNKS * PAIRS)
            pe.wait_ge(wo_read, 3 + TILES)
            with pe.Fori(0, TILES // 2) as it:
                for b in range(2):
                    t = it * 2 + b
                    pe.wait_ge(x2_out, t * 2 + 2)
                    pe.wait_ge(x2T_out, t + 1)
                    for h in range(2):
                        mm = pe.transpose(bank[b][0:HALF, h * TILE:(h + 1) * TILE],
                                          xrow[:, b, h * HALF:(h + 1) * HALF], ident[:, :])
                    mm.then_inc(x2T_ps, 1)
                    pe.wait_ge(x2T_out, t + 3)
                    pe.wait_ge(logit_out, t + 1)
                    for h in range(2):
                        mm = pe.matmul(bank[2 + b][:, 0:EXPERTS], xT[:, b, h, :], gatew[:, h, :],
                                       start=(h == 0), stop=(h == 1))
                    mm.then_inc(logit_ps, 1)
            pe.wait_ge(rt_masks, 1)
            pe.matmul(bank[0][:, 0:N144], upper[:, :], rt[:, 7, :], start=True, stop=True)
            pe.matmul(bank[1][:, 0:N144], ones[:, :], rt[:, 7, :], start=True, stop=True).then_inc(rt_prefix, 1)

            def turn_row(n, b, k):
                pe.wait_ge(row_in[b], k * 16)
                for h in range(2):
                    mm = pe.transpose(bank[7][0:HALF, h * TILE:(h + 1) * TILE],
                                      xrow[:, b, h * HALF:(h + 1) * HALF], ident[:, :])
                mm.then_inc(row_used, 1)

            def gate_up(n, b, u, e):
                if u == 0:
                    pe.wait_ge(xT_out, n + 1)
                pe.wait_ge(up_out, n * UNITS + u + 1)
                for h in range(2):
                    mm = pe.matmul(bank[u][:, :], xT[:, b, h, :],
                                   w13_all[:, ds(e * W13 + h * 2 * HIDDEN + u * 512, 512)],
                                   start=(h == 0), stop=(h == 1))
                mm.then_inc(gu_ps, 1)

            def turn_hid(n, u):
                pe.wait_ge(hid_out, n * UNITS + u + 1)
                pe.wait_ge(hidT_out, n * UNITS + u + 1)
                for j in range(2):
                    mm = pe.transpose(bank[3 + u][:, j * 128:(j + 1) * 128], hid[:, u, j * 128:(j + 1) * 128],
                                      ident[:, :])
                mm.then_inc(hidT_ps, 1)

            def down(n, u, e):
                pe.wait_ge(hidT_out, n * UNITS + u + 4)
                if u == 0:
                    pe.wait_ge(y_read, n + 1)
                for j in range(2):
                    mm = pe.matmul(bank[6][:, 0:DIM], hidT[:, u, j, :],
                                   w2_all[:, ds(e * W2 + (2 * u + j) * DIM, DIM)],
                                   start=(u == 0 and j == 0), stop=(u == UNITS - 1 and j == 1))
                mm.then_inc(y_ps, 1)

            def two_tiles(n, k, ea, eb, before, more=True):
                for u in range(UNITS):
                    gate_up(n, 0, u, ea)
                    if u == 0:
                        turn_row(n + 1, 1, k + 1)
                    if u > 0 or before is not None:
                        turn_hid(n - 1 if u == 0 else n, (u - 1) % UNITS)
                    if u > 1 or before is not None:
                        down(n - 1 if u < 2 else n, (u - 2) % UNITS, before if u < 2 else ea)
                for u in range(UNITS):
                    gate_up(n + 1, 1, u, eb)
                    if u == 0 and more:
                        turn_row(n + 2, 0, k + 2)
                    turn_hid(n if u == 0 else n + 1, (u - 1) % UNITS)
                    down(n if u < 2 else n + 1, (u - 2) % UNITS, ea if u < 2 else eb)

            pe.wait_ge(shared_in, 32)
            pe.wait_ge(prefix_read, 1)
            turn_row(0, 0, 1)
            two_tiles(0, 0, SHARED, SHARED, None)
            with pe.Fori(1, TILES // 2) as it:
                two_tiles(it * 2, it, SHARED, SHARED, SHARED)
            pe.wait_ge(tab_ready, 1)
            pe.wait_ge(experts_in, 16 * 2 * (EXPERTS - 1))

            def expert_of(j):
                return pe.value_load(tab[0:1, ds(j, 1)], min_val=0, max_val=EXPERTS - 1)
            two_tiles(TILES, TILES // 2, expert_of(1), expert_of(2), SHARED)
            pe.wait_ge(last_in, 32)
            half = TILES // 2
            with pe.Fori(half + 1, half + ROUTED_TILES // 2 - 1) as it:
                n = it * 2
                two_tiles(n, it, expert_of(n - TILES + 1), expert_of(n - TILES + 2), expert_of(n - TILES))
            n = TILES + ROUTED_TILES - 2
            e_last = expert_of(ROUTED_TILES)
            two_tiles(n, n // 2, expert_of(ROUTED_TILES - 1), e_last, expert_of(ROUTED_TILES - 2), more=False)
            down(n + 1, 1, e_last)
            turn_hid(n + 1, 2)
            down(n + 1, 2, e_last)

        @block.scalar
        def _(act):
            act.dma_start(wp, dram["wp"]).then_inc(small_in, 16)
            for dst, name in ((bproj, "bproj"), (bo, "bo"), (vecs, "vecs"), (gbias, "gbias")):
                act.dma_start(dst[:, :], dram[name]).then_inc(small_in, 16)
            act.dma_start(gatew[:, :, :], dram["gatew"]).then_inc(small_in, 16)
            act.dma_start(wv[0:HALF], dram["wv"]).then_inc(wqkv_in, 16)
            act.dma_start(wk[0:HALF], dram["wk"]).then_inc(wqkv_in, 16)
            act.dma_start(wq[0:HALF], dram["wq"]).then_inc(wqkv_in, 16)
            act.wait_ge(consts_set, N_CONST)
            for a in range(2):
                act.dma_start(wbd[64 * a:64 * a + 64, :, 64 * a:64 * a + 64], dram["maps"]).then_inc(wbd_in, 16)
            act.sem_inc(x1T_ready, 2)
            act.sem_inc(core_vw_out, 2)
            act.sem_inc(core_sq, 2)
            for P in ks + es:
                act.sem_inc(P.y_sq, 3)
                act.sem_inc(P.g_out, 3)
            act.sem_inc(x2T_out, 2)
            act.sem_inc(hidT_out, 3)
            act.sem_inc(silu_out, 3)

            act.preload_act_table_set(LN_EXP_TABLES)

            def norm1(t, b):
                act.wait_ge(ln1_stat, t + 1)
                act.activation(lnv[:, b:b + 1], mv1[:, b, 1:2], ACT.Ln, bias=eps[:, :]).then_inc(ln1_act, 1)
                act.wait_ge(ln1_act, t * 2 + 1)
                act.activation(rs1[:, b:b + 1], lnv[:, b:b + 1], ACT.Exp, scale=-0.5).then_inc(ln1_act, 1)

            with act.Fori(0, TILES // 2) as it:
                for b in range(2):
                    t = it * 2 + b
                    norm1(t, b)
                    act.wait_ge(x1T_ps, t + 1)
                    act.activation(x1T[0:HALF, :, ds(t * TILE, TILE)],
                                   bank[2 + b][0:HALF, 0:2 * TILE].rearrange("p (h t) -> p h t", h=2),
                                   ACT.Copy).then_inc(x1T_ready, 1)
            for p in range(PAIRS):
                act.wait_ge(v_ps, p + 1)
                act.activation(vcT[:, p, :], bank[4 + p % 2][:, 0:K3], ACT.Copy, scale=1.0 / 8).then_inc(v_out, 1)

            def exp_unit(S, used, c, p):
                act.wait_ge(S[0], c * PAIRS + p + 1)
                act.wait_ge(used, c * PAIRS + p + 1)
                act.activation(gb[:, p % 3, :], bank[p % 3][:, 0:CHUNK], ACT.Exp).then_inc(S[1], 1)
            with act.Fori(0, CHUNKS) as c:
                for p in range(PAIRS):
                    exp_unit(k_f, k_f[4], c, p)
            for i in range(STAGES):
                buf, n, chunks = KSTAGE[i]
                act.wait_ge(prep, PREP)
                act.preload_act_table(ACT.Gelu)

                def f_body(c):
                    for p in range(PAIRS):
                        f_act(act, ks[i], i, n, c, p)
                loop(act, chunks, f_body)
                r_act(act, ks[i], chunks, n * chunks, i)
                act.preload_act_table(ACT.Gelu)

                def g_body(c):
                    for p in range(PAIRS):
                        if i < 2:
                            g_act(act, ks[i], i, n, c, p)
                        else:
                            act.wait_ge(ks[i].z_out, c * PAIRS + p + 4)
                            act.activation(kc3[:, p, :], zb[:, p % 3, 0:n], ACT.Gelu, bias=shift_of(i),
                                           scale=gain_of(i)).then_inc(ks[i].g_out, 1)
                loop(act, chunks, g_body)
            act.preload_act_table(ACT.Exp)
            with act.Fori(0, CHUNKS) as c:
                for p in range(PAIRS):
                    exp_unit(q_f, q_f[3], c, p)

            act.wait_ge(blocks_zero, 3)

            def vw_copy(it, b):
                g = it * 2 + b
                act.wait_ge(core_vw, g + 1)
                act.wait_ge(core_y, g + 1)
                for odd in range(2):
                    rows = slice(64 * odd, 64 * odd + 64)
                    act.activation(vw[rows, b, odd::2, :],
                                   bank[0][rows, 0:QUADS * 128].rearrange("p (q e) -> p q e", q=QUADS),
                                   ACT.Copy).then_inc(core_vw_out, 1)

            def square(it, b):
                g = it * 2 + b
                act.wait_ge(core_y, g + 3)
                act.wait_ge(core_sum, g + 1)
                for q in range(2):
                    act.activation(sq[:, 3 * q:3 * q + 3, :],
                                         bank[4 + q][:, 0:3 * GROUP].rearrange("p (a t) -> p a t", a=3),
                                         ACT.Square, bias=bias_of(2 * STAGES - 1)).then_inc(core_sq, 1)
            vw_copy(0, 0)
            with act.Fori(0, GROUPS // 2 - 1) as it:
                vw_copy(it, 1)
                square(it, 0)
                vw_copy(it + 1, 0)
                square(it, 1)
            vw_copy(GROUPS // 2 - 1, 1)
            square(GROUPS // 2 - 1, 0)
            square(GROUPS // 2 - 1, 1)
            act.preload_act_table_set(LN_EXP_TABLES)
            act.wait_ge(core_var, GROUPS + 1)
            act.activation(var[:, :], var[:, :], ACT.Ln, bias=eps[0:96, :]).then_inc(r_log, 1)
            act.wait_ge(r_log, STAGES + 1)
            act.activation(rstd[:, :], var[:, :], ACT.Exp, scale=-0.5).then_inc(r_exp, 1)
            for i in range(STAGES):
                G = es[i]
                s = 2 * STAGES - 1 - i
                act.preload_act_table(ACT.Gelu)

                def gf_body(c):
                    for p in range(PAIRS):
                        g_act(act, G, s, CHUNK, c, p, consumed=(i == STAGES - 1))
                        if i < STAGES - 1:
                            if p:
                                f_act(act, es[i + 1], s - 1, CHUNK, c, p - 1)
                    if i < STAGES - 1:
                        f_act(act, es[i + 1], s - 1, CHUNK, c, PAIRS - 1)
                loop(act, CHUNKS, gf_body)
                if i < STAGES - 1:
                    r_act(act, es[i + 1], CHUNKS, TOKENS, STAGES + 1 + i)

            act.preload_act_table_set(LN_EXP_TABLES)
            act.wait_ge(mv_out, TILES)
            act.activation(ln2[:, :], mv2[:, :, 1], ACT.Ln, bias=eps[:, :]).then_inc(ln2_log, 1)
            act.wait_ge(ln2_log, 1)
            act.activation(rs2[:, :], ln2[:, :], ACT.Exp, scale=-0.5).then_inc(ln2_r, 1)
            with act.Fori(0, TILES // 2) as it:
                for b in range(2):
                    t = it * 2 + b
                    act.wait_ge(x2T_ps, t + 1)
                    act.wait_ge(logit_ps, t + 1)
                    act.activation(xT[:, b, :, :],
                                   bank[b][0:HALF, 0:2 * TILE].rearrange("p (h t) -> p h t", h=2),
                                   ACT.Copy).then_inc(x2T_out, 1)
            act.wait_ge(rt_abs, 1)
            act.activation(rt[:, 2, :], rt[:, 1, :], ACT.Exp, scale=-1.0).then_inc(rt_exp, 1)
            act.wait_ge(rt_exp, 1)
            act.activation(rt[:, 3, :], rt[:, 2, :], ACT.Ln, bias=1.0).then_inc(rt_ln, 1)
            act.wait_ge(rt_sp, 1)
            act.activation(rt[:, 2, :], rt[:, 1, :], ACT.Sqrt).then_inc(rt_sqrt, 1)

            def turned(n, b):
                act.wait_ge(row_used, n + 1)
                act.wait_ge(gu_ps, n * UNITS - 3) if not isinstance(n, int) or n >= 2 else None
                act.activation(xT[:, b, :, :],
                               bank[7][0:HALF, 0:2 * TILE].rearrange("p (h t) -> p h t", h=2),
                               ACT.Copy).then_inc(xT_out, 1)

            def silu(n, u):
                act.wait_ge(gu_ps, n * UNITS + u + 1)
                act.wait_ge(hid_out, n * UNITS + u - 2) if not isinstance(n, int) or n >= 1 else None
                act.activation(sgate[:, u, :], bank[u][:, 0:UNIT], ACT.Silu).then_inc(silu_out, 1)

            def hid_copy(n, u):
                act.wait_ge(hidT_ps, n * UNITS + u + 1)
                act.wait_ge(y_ps, n * UNITS + u - 2) if not isinstance(n, int) or n >= 1 else None
                act.activation(hidT[:, u, :, :], bank[3 + u][:, 0:UNIT].rearrange("p (j t) -> p j t", j=2),
                               ACT.Copy).then_inc(hidT_out, 1)

            def two_tiles(n, first=False, more=True):
                for b in range(2):
                    for u in range(UNITS):
                        silu(n + b, u)
                        if u == 0 and (b == 0 or more):
                            turned(n + b + 1, 1 - b)
                        if u > 0 or b > 0 or not first:
                            hid_copy(n + b if u else n + b - 1, (u - 1) % UNITS)
            turned(0, 0)
            two_tiles(0, first=True)
            with act.Fori(1, (TILES + ROUTED_TILES) // 2 - 1) as it:
                two_tiles(it * 2)
            two_tiles(TILES + ROUTED_TILES - 2, more=False)
            hid_copy(TILES + ROUTED_TILES - 1, UNITS - 1)

            for t in range(TILES):
                act.wait_ge(comb, t + 1)
                act.dma_start(out[t * TILE:(t + 1) * TILE, :], orow[:, t % 3, :]).then_inc(stored[t % 3], 16)
            for b in range(3):
                act.wait_ge(stored[b], 16 * (TILES // 3))

        @block.vector
        def _(dve):
            def routing():
                count = [0]

                def step(ins, signal=None):
                    if signal is None:
                        count[0] += 1
                        ins.then_inc(rt_step, 1)
                        dve.wait_ge(rt_step, count[0])
                    else:
                        ins.then_inc(signal, 1)
                        dve.wait_ge(signal, 1)

                def by_token(x):
                    return x.rearrange("p (t e) -> p t e", t=TILES)

                def over_experts(x):
                    return x.unsqueeze(2).to_broadcast([128, TILES, EXPERTS])

                L, A, E, LN, SC, R, TMP, M, M1, M2, SA, SB = (rt[:, k, :] for k in range(12))
                s1, s2, w1, w2, inv, pos = (small[:, k, :] for k in range(6))
                step(dve.scalar_tensor_tensor(out=A, in0=L, scalar=-1.0, in1=L, op0=ALU.mult, op1=ALU.max), rt_abs)
                dve.wait_ge(rt_ln, 1)
                step(dve.tensor_scalar(SC, E, -1.0 / 6, None, ALU.mult))
                for c in (1.0 / 5, -1.0 / 4, 1.0 / 3, -1.0 / 2, 1.0):
                    step(dve.scalar_tensor_tensor(out=SC, in0=SC, scalar=c, in1=E, op0=ALU.add, op1=ALU.mult))
                step(dve.tensor_tensor(SC, SC, LN, ALU.subtract))
                step(dve.scalar_tensor_tensor(out=SC, in0=E, scalar=0.06, in1=SC, op0=ALU.is_lt, op1=ALU.mult))
                step(dve.tensor_tensor(LN, LN, SC, ALU.add))
                step(dve.scalar_tensor_tensor(out=A, in0=L, scalar=0.0, in1=LN, op0=ALU.max, op1=ALU.add))
                step(dve.tensor_scalar(A, A, 1e-30, None, ALU.max), rt_sp)
                dve.wait_ge(rt_sqrt, 1)
                step(dve.reciprocal(LN, E))
                step(dve.scalar_tensor_tensor(out=LN, in0=A, scalar=0.5, in1=LN, op0=ALU.mult, op1=ALU.mult))
                step(dve.scalar_tensor_tensor(out=SC, in0=E, scalar=0.5, in1=LN, op0=ALU.mult, op1=ALU.add))
                step(dve.tensor_tensor(by_token(R), by_token(SC),
                                       gbias[:, :].unsqueeze(1).to_broadcast([128, TILES, EXPERTS]), ALU.add))
                for mk in (M1, M2):
                    step(dve.tensor_reduce(s1, by_token(R), AX.X, ALU.max))
                    step(dve.tensor_tensor(by_token(TMP), by_token(R), over_experts(s1), ALU.is_equal))
                    step(dve.scalar_tensor_tensor(out=TMP, in0=TMP, scalar=-100.0, in1=iota_e[:, :], op0=ALU.mult,
                                                  op1=ALU.add))
                    step(dve.tensor_reduce(s2, by_token(TMP), AX.X, ALU.min))
                    step(dve.tensor_scalar(TMP, iota_e[:, :], -100.0, None, ALU.add))
                    step(dve.tensor_tensor(by_token(mk), by_token(TMP), over_experts(s2), ALU.is_equal))
                    if mk is M1:
                        step(dve.scalar_tensor_tensor(out=R, in0=M1, scalar=-1e30, in1=R, op0=ALU.mult, op1=ALU.add))
                step(dve.tensor_tensor(M, M1, M2, ALU.add), rt_masks)
                for mk, s in ((M1, s1), (M2, s2)):
                    step(dve.tensor_tensor(TMP, mk, SC, ALU.mult))
                    step(dve.tensor_reduce(s, by_token(TMP), AX.X, ALU.add))
                step(dve.tensor_tensor(inv, s1, s2, ALU.add))
                step(dve.tensor_scalar(inv, inv, 1e-6, None, ALU.max))
                step(dve.reciprocal(pos, inv))
                step(dve.tensor_tensor(w1, s1, pos, ALU.mult))
                step(dve.tensor_tensor(w2, s2, pos, ALU.mult))
                dve.wait_ge(rt_prefix, 1)
                step(dve.tensor_copy(L, bank[1][:, 0:N144]))
                step(dve.tensor_copy(A, bank[0][:, 0:N144]), prefix_read)
                src, dst = L, SA
                shift = 1
                while shift < TILES:
                    n = shift * EXPERTS
                    step(dve.tensor_copy(dst[:, 0:n], src[:, 0:n]))
                    step(dve.tensor_tensor(dst[:, n:N144], src[:, n:N144], src[:, 0:N144 - n], ALU.add))
                    src, dst = dst, (SB if dst is SA else SA)
                    shift *= 2
                total = ecount[:, 0, :]
                step(dve.tensor_copy(total, src[:, N144 - EXPERTS:N144]))
                step(dve.tensor_tensor(TMP, src, L, ALU.subtract))
                step(dve.tensor_tensor(TMP, TMP, A, ALU.add))
                tiles = ecount[:, 1, :]
                by_expert = SA.rearrange("p (e j) -> p e j", e=EXPERTS)
                step(dve.tensor_tensor(by_expert, iota_tok[:, :].rearrange("p (e j) -> p e j", e=EXPERTS),
                                       total.unsqueeze(2).to_broadcast([128, EXPERTS, TILES]), ALU.is_lt))
                step(dve.tensor_reduce(tiles, by_expert, AX.X, ALU.add))
                step(dve.tensor_copy(ecount[:, 2, :], tiles))
                src, dst = ecount[:, 2, :], ecount[:, 3, :]
                for n in (1, 2, 4):
                    step(dve.tensor_copy(dst[:, 0:n], src[:, 0:n]))
                    step(dve.tensor_tensor(dst[:, n:EXPERTS], src[:, n:EXPERTS], src[:, 0:EXPERTS - n], ALU.add))
                    src, dst = dst, src
                ends = src
                step(dve.tensor_tensor(cmp_tile[:, :, :], iota_tile[:, :, :],
                                       ends[0:1, :].unsqueeze(1).to_broadcast([1, ROUTED_TILES, EXPERTS]), ALU.is_ge))
                step(dve.tensor_reduce(tile_expert[:, :], cmp_tile[:, :, :], AX.X, ALU.add))
                step(dve.memset(tab[:, 0:1], SHARED))
                step(dve.tensor_scalar(tab[:, 1:1 + ROUTED_TILES], tile_expert[:, :], float(EXPERTS - 1), None,
                                       ALU.min), tab_ready)
                step(dve.tensor_tensor(dst, ends, tiles, ALU.subtract))
                step(dve.tensor_scalar(dst, dst, float(TILE), None, ALU.mult))
                step(dve.tensor_tensor(by_token(TMP), by_token(TMP),
                                       dst.unsqueeze(1).to_broadcast([128, TILES, EXPERTS]), ALU.add))
                for k, mk in enumerate((M1, M2)):
                    step(dve.tensor_tensor(R, mk, TMP, ALU.mult))
                    step(dve.tensor_reduce(pos, by_token(R), AX.X, ALU.add))
                    step(dve.tensor_copy(slot[:, k, :], pos), slots_ready if k else None)

            dve.sem_inc(emb_read, 2)
            for P in ks + es:
                dve.sem_inc(P.y_out, 3)
                dve.sem_inc(P.var_out, 1)
                dve.sem_inc(P.z_out, 3)
                dve.sem_inc(P.sums, 3)
                dve.sem_inc(P.next_out, 3)
            for s in (k_f[3], q_f[3], k_f[4]):
                dve.sem_inc(s, 3)
            dve.sem_inc(core_s, 2)
            dve.sem_inc(core_sm, 1)
            dve.sem_inc(core_chain, 1)
            dve.sem_inc(core_sn, 1)
            dve.sem_inc(core_y, 2)
            dve.sem_inc(core_y_out, 2)
            dve.sem_inc(core_sum, 1)
            dve.sem_inc(core_var, 1)
            dve.sem_inc(wo_read, 3)
            dve.sem_inc(logit_out, 2)
            dve.sem_inc(logit_ps, 2)
            dve.sem_inc(up_out, 3)
            dve.sem_inc(y_read, 1)
            dve.wait_ge(small_in, 16 * SMALL_LOADS)
            dve.tensor_tensor(bboth[:, :], bproj[:, :], bo[:, :], ALU.add).then_inc(prep, 1)
            dve.wait_ge(wbd_in, 32)
            dve.tensor_reduce(wsum[:, :], wbd[:, :, :], AX.X, ALU.add).then_inc(prep, 1)
            dve.wait_ge(prep, 2)
            dve.tensor_scalar(wmean[:, :], wsum[:, :], 1.0 / HEAD_DIM, None, ALU.mult).then_inc(prep, 1)
            dve.wait_ge(prep, 3)
            for a in range(2):
                rows, cols = slice(64 * a, 64 * a + 64), slice(64 * a, 64 * a + 64)
                dve.tensor_tensor(wbd[rows, :, cols], wbd[rows, :, cols],
                                  wmean[rows, :].unsqueeze(2).to_broadcast([64, 2 * STAGES, 64]),
                                  ALU.subtract).then_inc(prep, 1)
            dve.wait_ge(prep, 5)
            dve.tensor_scalar(wbd[:, 0:STAGES, :], wbd[:, 0:STAGES, :], 0.5, None, ALU.mult).then_inc(prep, 1)
            dve.wait_ge(bmean_ready, 1)
            dve.tensor_tensor(bcen[:, :], vecs[:, 0:2 * STAGES], bank[7][:, 0:2 * STAGES],
                              ALU.subtract).then_inc(prep, 1)
            dve.wait_ge(prep, PREP)

            with dve.Fori(0, TILES // 2) as it:
                for b in range(2):
                    t = it * 2 + b
                    dve.wait_ge(embedded, t + 1)
                    dve.tensor_tensor(hrow[:, b, :], bank[b][:, 0:DIM], bproj[:, :], ALU.add).then_inc(ln1_dve, 1)
                    dve.wait_ge(ln1_dve, t * 2 + 1)
                    dve.bn_stats(stats[:, b, :], hrow[:, b, :]).then_inc(ln1_dve, 1)
                    dve.wait_ge(ln1_dve, t * 2 + 2)
                    dve.tensor_tensor(resid[:, ds(t, 1), :], bank[b][:, 0:DIM].unsqueeze(1), bboth[:, :].unsqueeze(1),
                                      ALU.add).then_inc(emb_read, 1)
                    dve.bn_aggr(mv1[:, b, :], stats[:, b, :]).then_inc(ln1_stat, 1)
                    dve.wait_ge(ln1_act, t * 2 + 2)
                    dve.wait_ge(ln1_stat, t + 1)
                    dve.tensor_scalar(xrow[:, b, :], hrow[:, b, :], mv1[:, b, 0:1], rs1[:, b:b + 1],
                                      ALU.subtract, ALU.mult).then_inc(x1_ready, 1)
            dve.wait_ge(x1T_ready, TILES + 2)
            xv = x1T[0:HALF].rearrange("p h (i t) -> p (h i) t", t=TOKENS_PER_IMAGE)
            dve.tensor_reduce(xp[0:HALF, :, 0:4], xv[:, :, 0:32].rearrange("p i (r t) -> p i r t", t=8), AX.X,
                              ALU.add).then_inc(xp_out, 1)
            dve.tensor_reduce(xp[0:HALF, :, 4:5], xv[:, :, 32:36].unsqueeze(2), AX.X, ALU.add).then_inc(xp_out, 1)

            def feature_map(S, dst, c, p):
                dve.wait_ge(S[1], c * PAIRS + p + 1)
                dve.tensor_scalar(gb[:, p % 3, :], gb[:, p % 3, :], 1.0, None, ALU.min).then_inc(S[2], 1)
                dve.wait_ge(S[2], c * PAIRS + p + 1)
                dve.scalar_tensor_tensor(out=dst, in0=bank[p % 3][:, 0:CHUNK], scalar=1.0, in1=gb[:, p % 3, :],
                                         op0=ALU.add, op1=ALU.max).then_inc(S[3], 1)
            with dve.Fori(0, CHUNKS) as c:
                for p in range(PAIRS):
                    feature_map(k_f, gb[:, p % 3, :], c, p)
                    dve.wait_ge(k_f[3], c * PAIRS + p + 4)
                    dve.tensor_tensor(kp1[:, p, ds(c * (CHUNK // 2), CHUNK // 2)], gb[:, p % 3, 0::2],
                                      gb[:, p % 3, 1::2], ALU.add).then_inc(k_f[4], 1)
            for i in range(STAGES):
                buf, n, chunks = KSTAGE[i]
                P = ks[i]

                def f_body(c):
                    for p in range(PAIRS):
                        f_dve(dve, P, i, buf[:, p, ds(c * n, n)], n, c, p)
                    var_dve(dve, P, n, c)
                loop(dve, chunks, f_body)
                r_dve(dve, n * chunks, i)

                def g_body(c):
                    def pool_pair(p):
                        dve.wait_ge(P.g_out, c * PAIRS + p + 4)
                        if i == 0:
                            dve.tensor_tensor(kp2[:, p, ds(c * (n // 2), n // 2)], gb[:, p % 3, 0:n:2],
                                              gb[:, p % 3, 1:n:2], ALU.add).then_inc(P.next_out, 1)
                        elif i == 1:
                            rows = gb[:, p % 3, 0:n].rearrange("p (i r) -> p i r", r=9)
                            dst = kc3[:, p, ds(c * (K3 // 2), K3 // 2)].rearrange("p (i r) -> p i r", r=POOLED)
                            dve.tensor_tensor(dst[:, :, 0:4], rows[:, :, 0:8:2], rows[:, :, 1:8:2],
                                              ALU.add).then_inc(k_main, 1)
                            dve.wait_ge(k_main, c * PAIRS + p + 1)
                            dve.tensor_copy(dst[:, :, 4:5], rows[:, :, 8:9]).then_inc(P.next_out, 1)
                    for p in range(PAIRS):
                        z_dve(dve, P, buf[:, p, ds(c * n, n)], n, c, p)
                        if p and i < 2:
                            pool_pair(p - 1)
                    if i < 2:
                        pool_pair(PAIRS - 1)
                loop(dve, chunks, g_body)
            with dve.Fori(0, CHUNKS) as c:
                for p in range(PAIRS):
                    feature_map(q_f, q_y[:, p, ds(c * CHUNK, CHUNK)], c, p)

            def masked(it, b):
                g = it * 2 + b
                dve.wait_ge(core_s, g + 3)
                dve.tensor_tensor(sm[:, b, :, :], bank[1][:, 0:QUADS * GROUP].rearrange("p (q t) -> p q t", q=QUADS),
                                  mask[:, :].unsqueeze(1).to_broadcast([128, QUADS, GROUP]), ALU.mult).then_inc(core_sm, 1)

            def inverse(it, b):
                g = it * 2 + b
                dve.wait_ge(core_den, g + 1)
                dve.wait_ge(core_rb, g) if not isinstance(g, int) or g > 0 else None
                dve.tensor_scalar(den[:, :], bank[2][0:96, 0:GROUP], DEN_EPS, None, ALU.add).then_inc(core_chain, 1)
                dve.wait_ge(core_chain, g * 6 + 2)
                dve.reciprocal(rden[:, :], den[:, :]).then_inc(core_chain, 1)
                dve.wait_ge(core_chain, g * 6 + 3)
                split_dve(dve, rden, dsplit, GROUP, core_chain, g * 6 + 3).then_inc(core_r, 1)

            def normalised(it, b):
                g = it * 2 + b
                dve.wait_ge(core_rb, g + 1)
                dve.tensor_tensor(sn[:, b, :, :], sm[:, b, :, :],
                                  bank[3][:, 0:QUADS * GROUP].rearrange("p (q t) -> p q t", q=QUADS),
                                  ALU.mult).then_inc(core_sn, 1)

            def y_copy(it, b):
                g = it * 2 + b
                dve.wait_ge(core_sq, g * 2 + 4)
                for q in range(2):
                    dve.tensor_scalar(q_y[:, 3 * q:3 * q + 3, ds(g * GROUP, GROUP)],
                                            bank[4 + q][:, 0:3 * GROUP].rearrange("p (a t) -> p a t", a=3),
                                            bias_of(2 * STAGES - 1), None, ALU.add).then_inc(core_y_out, 1)
                dve.wait_ge(core_sum, g + 2)
                dve.tensor_copy(var[:, ds(g * GROUP, GROUP)], bank[6][0:96, 0:GROUP]).then_inc(core_var, 1)

            def core_step(it, b, last=False):
                normalised(it, b)
                if not last:
                    masked(it + b, 1 - b)
                    inverse(it + b, 1 - b)
                y_copy(it, b)
            masked(0, 0)
            inverse(0, 0)
            with dve.Fori(0, GROUPS // 2 - 1) as it:
                core_step(it, 0)
                core_step(it, 1)
            core_step(GROUPS // 2 - 1, 0)
            core_step(GROUPS // 2 - 1, 1, last=True)
            r_dve(dve, TOKENS, STAGES)
            for i in range(STAGES):
                G = es[i]
                s = 2 * STAGES - 1 - i

                def z(c, p):
                    z_dve(dve, G, q_y[:, p, ds(c * CHUNK, CHUNK)], CHUNK, c, p)

                def gf_body(c, more):
                    for p in range(PAIRS):
                        if p + 1 < PAIRS:
                            z(c, p + 1)
                        elif more:
                            z(c + 1, 0)
                        if i < STAGES - 1:
                            if p:
                                f_dve(dve, es[i + 1], s - 1, q_y[:, p - 1, ds(c * CHUNK, CHUNK)], CHUNK, c, p - 1)
                    if i < STAGES - 1:
                        f_dve(dve, es[i + 1], s - 1, q_y[:, PAIRS - 1, ds(c * CHUNK, CHUNK)], CHUNK, c, PAIRS - 1)
                        var_dve(dve, es[i + 1], CHUNK, c)
                    else:
                        for j in range(3):
                            t = c * 3 + j
                            dve.wait_ge(G.next_out, c * PAIRS + PAIRS + 3)
                            dve.tensor_tensor(hrow[:, j % 2, :], bank[3 + j][:, 0:DIM],
                                              resid[:, ds(t, 1), :].rearrange("p a d -> p (a d)"),
                                              ALU.add).then_inc(ln2_chain, 1)
                            dve.wait_ge(ln2_chain, t * 3 + 1)
                            dve.bn_stats(stats[:, 0, :], hrow[:, j % 2, :]).then_inc(ln2_chain, 1)
                            dve.wait_ge(ln2_chain, t * 3 + 2)
                            dve.tensor_tensor(resid[:, ds(t, 1), :], bank[3 + j][:, 0:DIM].unsqueeze(1),
                                              resid[:, ds(t, 1), :], ALU.add).then_inc(wo_read, 1)
                            dve.bn_aggr(mv1[:, j % 2, :], stats[:, 0, :]).then_inc(ln2_chain, 1)
                            dve.wait_ge(ln2_chain, t * 3 + 3)
                            dve.tensor_scalar(mv2[:, ds(t, 1), :], mv1[:, j % 2, :].unsqueeze(1), 1.0, None,
                                              ALU.mult).then_inc(mv_out, 1)
                z(0, 0)
                with dve.Fori(0, CHUNKS - 1) as c:
                    gf_body(c, True)
                gf_body(CHUNKS - 1, False)
                if i < STAGES - 1:
                    r_dve(dve, TOKENS, STAGES + 1 + i)
            dve.wait_ge(ln2_r, 1)
            def x2(it, b):
                t = it * 2 + b
                for dst in (xrow[:, b, :].unsqueeze(1), x2r[:, ds(t, 1), :]):
                    dve.tensor_scalar(dst, resid[:, ds(t, 1), :], mv2[:, ds(t, 1), 0], rs2[:, ds(t, 1)],
                                      ALU.subtract, ALU.mult).then_inc(x2_out, 1)

            def logits(it, b):
                t = it * 2 + b
                dve.wait_ge(logit_ps, t + 3)
                dve.tensor_copy(rt[:, 0, ds(t * EXPERTS, EXPERTS)], bank[2 + b][:, 0:EXPERTS]).then_inc(logit_out, 1)
            x2(0, 0)
            with dve.Fori(0, TILES // 2 - 1) as it:
                x2(it, 1)
                logits(it, 0)
                x2(it + 1, 0)
                logits(it, 1)
            x2(TILES // 2 - 1, 1)
            logits(TILES // 2 - 1, 0)
            logits(TILES // 2 - 1, 1)
            dve.wait_ge(logit_out, TILES + 2)
            routing()

            def up(n, u):
                dve.wait_ge(silu_out, n * UNITS + u + 4)
                dve.tensor_scalar(sup[:, u, :], bank[u][:, UNIT:2 * UNIT], LIMIT, -LIMIT, ALU.min,
                                  ALU.max).then_inc(up_out, 1)
                dve.wait_ge(up_out, n * UNITS + u + 4)
                dve.wait_ge(hidT_ps, n * UNITS + u - 2) if not isinstance(n, int) or n >= 1 else None
                dve.scalar_tensor_tensor(out=hid[:, u, :], in0=sgate[:, u, :], scalar=SILU_LIMIT, in1=sup[:, u, :],
                                         op0=ALU.min, op1=ALU.mult).then_inc(hid_out, 1)

            def finish(n, b, shared, m=None):
                dve.wait_ge(y_ps, (n + 1) * UNITS)
                if shared:
                    dve.tensor_tensor(resid[:, ds(n, 1), :], bank[6][:, 0:DIM].unsqueeze(1), resid[:, ds(n, 1), :],
                                      ALU.add).then_inc(y_read, 1)
                else:
                    dve.wait_ge(y_stored[b], m * 16) if not isinstance(m, int) or m > 0 else None
                    dve.tensor_copy(orow[:, b, :], bank[6][:, 0:DIM]).then_inc(y_read, 1)

            def two_tiles(n, shared, first=False, shared_before=True, m=None):
                for b in range(2):
                    for u in range(UNITS):
                        up(n + b, u)
                        if u == 1 and b == 1:
                            finish(n, 0, shared, m)
                        if u == 1 and b == 0 and not first:
                            finish(n - 1, 1, shared_before, None if m is None else m - 1)
            dve.wait_ge(zeroed, 16 * 6)
            two_tiles(0, True, first=True)
            with dve.Fori(1, TILES // 2) as it:
                two_tiles(it * 2, True)
            two_tiles(TILES, False, shared_before=True, m=0)
            two_tiles(TILES + 2, False, shared_before=False, m=1)
            with dve.Fori(2, ROUTED_TILES // 2) as it:
                two_tiles(it * 2 + TILES, False, shared_before=False, m=it)
            finish(TILES + ROUTED_TILES - 1, 1, False, ROUTED_TILES // 2 - 1)

            for b in range(2):
                dve.wait_ge(y_stored[b], 16 * (ROUTED_TILES // 2))
            for t in range(TILES):
                b = t % 3
                dve.wait_ge(gathered[b], 32 * (t // 3 + 1))
                if t >= 3:
                    dve.wait_ge(stored[b], 16 * (t // 3))
                dve.scalar_tensor_tensor(out=resid[:, t, :], in0=gath[:, b, 0, :], scalar=small[:, 2, t:t + 1],
                                         in1=resid[:, t, :], op0=ALU.mult, op1=ALU.add).then_inc(comb_step, 1)
                dve.wait_ge(comb_step, t + 1)
                dve.scalar_tensor_tensor(out=orow[:, b, :], in0=gath[:, b, 1, :], scalar=small[:, 3, t:t + 1],
                                         in1=resid[:, t, :], op0=ALU.mult, op1=ALU.add).then_inc(comb, 1)


def kernel(**inputs):
    import numpy as np
    import concourse.bacc as bacc
    from concourse.bass_utils import run_bass_kernel_spmd as run

    a = {k: np.asarray(v) for k, v in inputs.items()}
    P = 16
    x = a["x"].reshape(IMAGES, 3, 6, P, 6, P).transpose(0, 2, 4, 1, 3, 5).reshape(TILES, TILE, PATCH_DIM // 128, 128)

    def halves(w):
        return w.reshape(2, HALF, -1).transpose(1, 0, 2)

    w1 = np.concatenate([a["L0_ffn_w1"], a["L0_ffn_w1s"][None]])
    w3 = np.concatenate([a["L0_ffn_w3"], a["L0_ffn_w3s"][None]])
    w2 = np.concatenate([a["L0_ffn_w2"], a["L0_ffn_w2s"][None]])
    w13 = np.stack([w1.reshape(EXPERTS + 1, 2, HALF, UNITS, UNIT), w3.reshape(EXPERTS + 1, 2, HALF, UNITS, UNIT)], 4)
    vecs = np.concatenate([a["L0_attn_" + k + v] for v in ("_b", "_g", "_be") for k in ("pool", "exp")])
    arrays = {
        "patches": x.transpose(0, 3, 2, 1),
        "wp": a["L0_tok_W_proj"].reshape(DIM, PATCH_DIM // 128, 128).transpose(2, 1, 0),
        "bproj": np.broadcast_to(a["L0_tok_b_proj"], (128, DIM)),
        "bo": np.broadcast_to(a["L0_attn_bo"], (128, DIM)),
        "vecs": np.concatenate([vecs.T, vecs.T]),
        "gbias": np.broadcast_to(a["L0_ffn_gate_bias"], (128, EXPERTS)),
        "gatew": halves(a["L0_ffn_gate_w"]),
        "wq": halves(a["L0_attn_Wq"]),
        "wk": halves(a["L0_attn_Wk"]),
        "wv": halves(a["L0_attn_Wv"]),
        "wo": a["L0_attn_Wo"].reshape(PAIRS, 128, DIM).transpose(1, 0, 2),
        "maps": np.concatenate([a["L0_attn_pool_W"], a["L0_attn_exp_W"]]).transpose(1, 0, 2),
        "w13": w13.transpose(0, 2, 1, 3, 4, 5).reshape(EXPERTS + 1, HALF, W13),
        "w2": w2.reshape(EXPERTS + 1, HIDDEN // 128, 128, DIM).transpose(0, 2, 1, 3).reshape(EXPERTS + 1, 128, W2),
    }
    nc = bacc.Bacc("TRN2", target_bir_lowering=False, num_devices=1)
    arrays = {k: np.ascontiguousarray(v) for k, v in arrays.items()}
    dram = {k: nc.dram_tensor(f"in_{k}", v.shape, F32, kind="ExternalInput").ap() for k, v in arrays.items()}
    dram["slots"] = nc.dram_tensor("slots", (ROUTED_TILES * TILE, DIM), F32).ap()
    dram["expert_out"] = nc.dram_tensor("expert_out", (ROUTED_TILES * TILE, DIM), F32).ap()
    out = nc.dram_tensor("out", (TOKENS, DIM), F32, kind="ExternalOutput").ap()
    build(nc, dram, out)
    r = run(nc, [{f"in_{k}": v for k, v in arrays.items()}], core_ids=[0])
    return r.results[0]["out"].reshape(IMAGES, TOKENS_PER_IMAGE, DIM)
```

```python
from contextlib import ExitStack

import concourse.bass as bass
from concourse import mybir

F32 = mybir.dt.float32
BF16 = mybir.dt.bfloat16
F16 = mybir.dt.float16
I32 = mybir.dt.int32
U32 = mybir.dt.uint32
ALU = mybir.AluOpType
ACT = mybir.ActivationFunctionType
AX = mybir.AxisListType
ds = bass.ds

IMAGES, TOKENS_PER_IMAGE = 64, 36
TOKENS = IMAGES * TOKENS_PER_IMAGE
PATCH_DIM, DIM, HEADS, HEAD_DIM = 768, 192, 12, 64
HALF = DIM // 2
STAGES = 3
PAIRS = HEADS // 2
TILE = 128
TILES = TOKENS // TILE
CHUNK = 384
CHUNKS = TOKENS // CHUNK
GROUP_IMAGES = 4
GROUP = GROUP_IMAGES * TOKENS_PER_IMAGE
GROUPS = IMAGES // GROUP_IMAGES
POOLED = 5
GROUP_ROWS = GROUP_IMAGES * POOLED
K1, K2, K3 = TOKENS // 2, TOKENS // 4, IMAGES * POOLED
LN_EPS = 1e-5
DEN_EPS = 1e-6
QUADS = HEADS // 4
EXPERTS, HIDDEN = 8, 768
LIMIT = 10.0
LN_EXP_TABLES = "natural_log_exp_and_others"
SILU_LIMIT = 9.999546021312976
UNITS = 3
UNIT = HIDDEN // UNITS
W13 = 2 * 2 * HIDDEN
W2 = (HIDDEN // 128) * DIM
SCALE = 16.0
STAGE = 512
STAGE2 = 384
C13, C2 = W13 // STAGE, W2 // STAGE2
CHUNKS_W = C13 + C2
SHARED = EXPERTS - 1
ROUTED_TILES = 44
N144 = TILES * EXPERTS


def build(nc, dram, out):
    ctx = ExitStack()
    with ctx:
        def sb(name, shape, dt=F32):
            return ctx.enter_context(nc.sbuf_tensor(name, shape, dt))

        def sem(name):
            return ctx.enter_context(nc.semaphore(name))

        resid = sb("resid", [128, TILES, DIM])
        arena = sb("arena", [128, EXPERTS * (W13 + W2)])
        ARENA_B = 8256
        arena_b = sb("arena_b", [128, ARENA_B])
        w13_cols = EXPERTS * W13
        w13_all = arena[0:HALF, 0:w13_cols].bitcast(F16)
        w2_all = arena[:, w13_cols:w13_cols + EXPERTS * W2].bitcast(F16)
        PREP, SMALL_LOADS, N_CONST = 7, 5, 51

        def view(base, start, shape):
            n = 1
            for s in shape:
                n *= s
            v = base[:, start:start + n]
            if len(shape) == 1:
                return v
            names = "abc"[:len(shape)]
            return v.rearrange(f"p ({' '.join(names)}) -> p {' '.join(names)}",
                               **{names[i]: shape[i] for i in range(1, len(shape))})

        q_y = view(arena, 0, [PAIRS, TOKENS])
        kp1 = view(arena, 0, [PAIRS, K1])
        kp2 = view(arena, PAIRS * K1, [PAIRS, K2])
        o = PAIRS * TOKENS
        x1T = view(arena, o, [2, TOKENS]); o += 2 * TOKENS
        wo = view(arena, PAIRS * TOKENS, [PAIRS, DIM])
        wq = view(arena, o, [2, HEADS * HEAD_DIM]); o += 2 * HEADS * HEAD_DIM
        wk = view(arena, o, [2, HEADS * HEAD_DIM])
        vw = view(arena, o, [2, PAIRS, 128]); o += 2 * HEADS * HEAD_DIM
        wv = view(arena, o, [2, HEADS * HEAD_DIM])
        vblk = view(arena, o, [2, PAIRS, 128]); o += 2 * HEADS * HEAD_DIM
        patches = view(arena, o, [2, PATCH_DIM // 128, TILE])
        kblk = view(arena, o, [2, PAIRS, 128]); o += 2 * PATCH_DIM
        assert o <= EXPERTS * W13
        o = w13_cols
        var = arena[0:96, o:o + TOKENS]; o += TOKENS
        rstd = arena[0:96, o:o + TOKENS]; o += TOKENS
        rsplit = arena[0:96, o:o + TOKENS // 2].bitcast(BF16); o += TOKENS // 2
        ind = arena[:, o:o + (PAIRS + 1) * 96]; o += (PAIRS + 1) * 96
        wbd = view(arena, o, [2 * STAGES, 128]); o += 2 * STAGES * 128
        kc3_at = w13_cols + EXPERTS * W2 - PAIRS * K3
        assert o <= kc3_at <= w13_cols + (EXPERTS - 1) * W2
        kc3 = view(arena, kc3_at, [PAIRS, K3])
        gath = view(arena, 0, [3, 2, DIM])
        o = 0
        vcT = view(arena_b, o, [PAIRS, K3]); o += PAIRS * K3
        xp = view(arena_b, o, [2 * IMAGES, POOLED]); o += 2 * IMAGES * POOLED
        sqb = view(arena_b, o, [3, CHUNK]); o += 3 * CHUNK
        zb = view(arena_b, o, [3, CHUNK]); o += 3 * CHUNK
        gb = view(arena_b, o, [3, CHUNK]); o += 3 * CHUNK
        wp = view(arena_b, o, [PATCH_DIM // 128, DIM]); o += (PATCH_DIM // 128) * DIM
        ind_den = arena_b[:, o:o + (QUADS + 1) * 96]; o += (QUADS + 1) * 96
        mask = arena_b[:, o:o + GROUP]; o += GROUP
        den = arena_b[0:96, o:o + GROUP]; o += GROUP
        rden = arena_b[0:96, o:o + GROUP]; o += GROUP
        dsplit = arena_b[0:96, o:o + GROUP // 2].bitcast(BF16); o += GROUP // 2
        sel_den = arena_b[0:96, o:o + QUADS * 64].bitcast(BF16).rearrange("p (q n) -> p q n", q=QUADS)
        o += QUADS * 64
        assert o <= ARENA_B
        sm = view(arena_b, PAIRS * K3 + 2 * IMAGES * POOLED, [2, QUADS, GROUP])
        sn = view(arena_b, PAIRS * K3 + 2 * IMAGES * POOLED + 3 * CHUNK, [2, QUADS, GROUP])
        sq = view(arena_b, PAIRS * K3 + 2 * IMAGES * POOLED + 6 * CHUNK, [PAIRS, GROUP])
        o = 0
        x2c = arena_b[:, o:o + TILES * DIM].bitcast(F16).rearrange("p (t a d) -> p t a d", t=TILES, a=2)
        o += TILES * DIM
        sgate = view(arena_b, o, [3, UNIT]); o += 3 * UNIT
        sup = view(arena_b, o, [3, UNIT]); o += 3 * UNIT
        hid = view(arena_b, o, [3, UNIT]); o += 3 * UNIT
        zrow = arena_b[:, o - 3 * UNIT:o + 3 * UNIT]
        hsplit = arena_b[:, o:o + 3 * UNIT].bitcast(F16).rearrange("p (u a n) -> p u a n", u=3, a=2)
        o += 3 * UNIT
        rt = view(arena_b, o, [12, N144]); o += 12 * N144
        assert o <= ARENA_B

        vecs = sb("vecs", [128, 6 * STAGES])
        bcen = sb("bcen", [128, 2 * STAGES])
        wsum = sb("wsum", [128, 2 * STAGES])
        wmean = sb("wmean", [128, 2 * STAGES])
        bproj = sb("bproj", [128, DIM])
        bo = sb("bo", [128, DIM])
        bboth = sb("bboth", [128, DIM])
        gbias = sb("gbias", [128, EXPERTS])
        gatew = sb("gatew", [HALF, 2, EXPERTS])
        ident = sb("ident", [128, 128])
        ones = sb("ones", [128, 128])
        upper = sb("upper", [128, 128])
        blk64 = sb("blk64", [128, 128])
        sel = sb("sel", [96, PAIRS, 128], BF16)
        eps = sb("eps", [128, 1])
        hrow = sb("hrow", [128, 2, DIM])
        xrow = sb("xrow", [128, 2, DIM])
        xT = sb("xT", [HALF, 2, 2, TILE])
        xrow16 = xrow[:, :, :].bitcast(F16)
        xT16 = xT[:, :, :, :].rearrange("p b h t -> p (b h t)").bitcast(F16).rearrange(
            "p (b k t) -> p b k t", b=2, k=4)
        hidT = sb("hidT", [128, 3, 4, 128], F16)
        stage = sb("stage", [128, 3, STAGE])
        scale16 = sb("scale16", [128, 1])
        values = hidT[:, :, :, :].rearrange("p u k t -> p u (k t)")
        rests = stage[:, :, :].rearrange("p b n -> p (b n)").bitcast(F16).rearrange(
            "p (b n) -> p b n", b=3)
        ident16 = sb("ident16", [128, 128], F16)
        stats = sb("stats", [128, 3, 6])
        mv1 = sb("mv1", [128, 3, 2])
        lnv = sb("lnv", [128, 2])
        rs1 = sb("rs1", [128, 2])
        mv2 = sb("mv2", [128, TILES, 2])
        ln2 = sb("ln2", [128, TILES])
        rs2 = sb("rs2", [128, TILES])
        tab = sb("tab", [1, ROUTED_TILES + 1], I32)
        small = sb("small", [128, 12, TILES])
        iota_e = sb("iota_e", [128, N144])
        iota_tok = sb("iota_tok", [128, N144])
        iota_tile = sb("iota_tile", [1, ROUTED_TILES, EXPERTS])
        cmp_tile = sb("cmp_tile", [1, ROUTED_TILES, EXPERTS])
        tile_expert = sb("tile_expert", [1, ROUTED_TILES])
        ecount = sb("ecount", [128, 6, EXPERTS])
        slot = sb("slot", [128, 2, TILES], U32)
        orow = sb("orow", [128, 3, DIM])

        bank = [ctx.enter_context(nc.psum_tensor(f"bank{i}", [128, 512], F32)) for i in range(8)]
        bank16 = [x[:, :].bitcast(F16) for x in bank]

        consts_set = sem("consts_set")
        small_in = sem("small_in")
        wqkv_in = sem("wqkv_in")
        wbd_in = sem("wbd_in")
        wp_in = sem("wp_in")
        prep = sem("prep")
        bmean_ready = sem("bmean_ready")
        wo_in = sem("wo_in")
        blocks_zero = sem("blocks_zero")
        stage_in = [sem(f"stage_in{b}") for b in range(3)]
        split_in = [sem(f"split_in{b}") for b in range(3)]
        split = sem("split")
        shared_in = sem("shared_in")
        experts_in = sem("experts_in")
        last_in = sem("last_in")
        block = ctx.enter_context(nc.Block())
        EARLY = 5
        FIRST = 6

        patch_in = [sem(f"patch_in{b}") for b in range(2)]
        embedded = sem("embedded")
        emb_read = sem("emb_read")
        ln1_dve = sem("ln1_dve")
        ln1_stat = sem("ln1_stat")
        ln1_act = sem("ln1_act")
        x1_ready = sem("x1_ready")
        x1T_ps = sem("x1T_ps")
        x1T_ready = sem("x1T_ready")

        class Pass:
            def __init__(self, name, product=True, consumed=True):
                if product:
                    self.y_ps = sem(f"{name}_y_ps")
                    self.y_sq = sem(f"{name}_y_sq")
                    self.y_out = sem(f"{name}_y_out")
                    self.sums = sem(f"{name}_sums")
                    self.var_out = sem(f"{name}_var_out")
                self.rb_ps = sem(f"{name}_rb_ps")
                self.z_out = sem(f"{name}_z_out")
                self.g_out = sem(f"{name}_g_out")
                if consumed:
                    self.next_out = sem(f"{name}_next_out")

        k_f = sem("k_proj_ps"), sem("k_exp"), sem("k_min"), sem("k_map"), sem("k_pooled")
        q_f = sem("q_proj_ps"), sem("q_exp"), sem("q_min"), sem("q_map")
        ks = [Pass("k0"), Pass("k1"), Pass("k2", consumed=False)]
        es = [Pass("e0", product=False, consumed=False), Pass("e1", consumed=False), Pass("e2")]
        rchain = sem("rchain")
        r_ready = sem("r_ready")
        r_log = sem("r_log")
        r_exp = sem("r_exp")
        k_main = sem("k_main")
        v_ps = sem("v_ps")
        v_out = sem("v_out")
        xp_out = sem("xp_out")
        vfree = sem("vfree")

        def bias_of(s):
            return bcen[:, s:s + 1]

        def gain_of(s):
            return vecs[:, 6 + s:7 + s]

        def shift_of(s):
            return vecs[:, 12 + s:13 + s]


        def f_pe(pe, P, src, w, n, c, p, first_wait):
            first_wait()
            pe.wait_ge(P.y_out, c * PAIRS + p + 1)
            pe.wait_ge(P.y_sq, c * PAIRS + p + 1)
            pe.matmul(bank[3 + p % 3][:, 0:n], w, src, start=True, stop=True).then_inc(P.y_ps, 1)

        def s_pe(pe, P, n, c, p):
            pe.wait_ge(P.y_sq, c * PAIRS + p + 4)
            if p == 0:
                pe.wait_ge(P.var_out, c + 1)
            pe.matmul(bank[6][0:96, 0:n], ind[:, 96 * p:96 * p + 96], sqb[:, p % 3, 0:n],
                      start=(p == 0), stop=(p == PAIRS - 1)).then_inc(P.sums, 1)

        def f_act(act, P, s, n, c, p):
            act.wait_ge(P.y_ps, c * PAIRS + p + 1)
            act.wait_ge(P.sums, c * PAIRS + p + 1)
            act.activation(sqb[:, p % 3, 0:n], bank[3 + p % 3][:, 0:n], ACT.Square,
                           bias=bias_of(s)).then_inc(P.y_sq, 1)

        def f_dve(dve, P, s, dst, n, c, p):
            dve.wait_ge(P.y_sq, c * PAIRS + p + 4)
            dve.tensor_scalar(dst, bank[3 + p % 3][:, 0:n], bias_of(s), None,
                              ALU.add).then_inc(P.y_out, 1)

        def var_dve(dve, P, n, c):
            dve.wait_ge(P.sums, c * PAIRS + PAIRS + 3)
            dve.tensor_copy(var[:, ds(c * n, n)], bank[6][0:96, 0:n]).then_inc(P.var_out, 1)

        def r_act(act, P, chunks, length, n):
            act.preload_act_table_set(LN_EXP_TABLES)
            act.wait_ge(P.var_out, chunks + 1)
            act.activation(var[:, 0:length], var[:, 0:length], ACT.Ln, bias=eps[0:96, :]).then_inc(r_log, 1)
            act.wait_ge(r_log, n + 1)
            act.activation(rstd[:, 0:length], var[:, 0:length], ACT.Exp, scale=-0.5).then_inc(r_exp, 1)

        def split_dve(dve, src, dst, length, chain, n):
            dve.tensor_copy(dst[:, 0:length], src[:, 0:length]).then_inc(chain, 1)
            dve.wait_ge(chain, n + 1)
            dve.tensor_tensor(src[:, 0:length], src[:, 0:length], dst[:, 0:length],
                              ALU.subtract).then_inc(chain, 1)
            dve.wait_ge(chain, n + 2)
            dve.tensor_copy(dst[32:64, 0:length], src[32:64, 0:length]).then_inc(chain, 1)
            dve.tensor_copy(dst[64:96, 0:length], src[64:96, 0:length]).then_inc(chain, 1)
            dve.wait_ge(chain, n + 4)
            return dve.tensor_tensor(dst[64:96, 0:length], src[64:96, 0:length], dst[64:96, 0:length],
                                     ALU.subtract)

        def r_dve(dve, length, n):
            dve.wait_ge(r_exp, n + 1)
            split_dve(dve, rstd, rsplit, length, rchain, 4 * n).then_inc(r_ready, 1)

        def b_pe(pe, P, n, c, p):
            pe.wait_ge(P.z_out, c * PAIRS + p + 1)
            pe.matmul(bank[p % 3][:, 0:n], sel[:, p, :], rsplit[:, ds(c * n, n)],
                      start=True, stop=True).then_inc(P.rb_ps, 1)

        def z_dve(dve, P, src, n, c, p):
            dve.wait_ge(P.rb_ps, c * PAIRS + p + 1)
            dve.wait_ge(P.g_out, c * PAIRS + p + 1)
            dve.tensor_tensor(zb[:, p % 3, 0:n], src, bank[p % 3][:, 0:n], ALU.mult).then_inc(P.z_out, 1)

        def g_act(act, P, s, n, c, p, consumed=True):
            act.wait_ge(P.z_out, c * PAIRS + p + 4)
            if consumed:
                act.wait_ge(P.next_out, c * PAIRS + p + 1)
            act.activation(gb[:, p % 3, 0:n], zb[:, p % 3, 0:n], ACT.Gelu, bias=shift_of(s),
                           scale=gain_of(s)).then_inc(P.g_out, 1)

        def chunks_with_ends(eng, body):
            body(0, False, True)
            with eng.Fori(1, CHUNKS - 1) as c:
                body(c, True, True)
            body(CHUNKS - 1, True, False)

        KSTAGE = [(kp1, CHUNK, K1 // CHUNK), (kp2, K2 // 2, 2), (kc3, K3, 1)]

        def loop(eng, n, body):
            if n == 1:
                body(0)
            else:
                with eng.Fori(0, n) as c:
                    body(c)

        core_kv = sem("core_kv")
        core_vw = sem("core_vw")
        core_vw_out = sem("core_vw_out")
        core_s = sem("core_s")
        core_sm = sem("core_sm")
        core_den = sem("core_den")
        core_chain = sem("core_chain")
        core_r = sem("core_r")
        core_rb = sem("core_rb")
        core_sn = sem("core_sn")
        core_y = sem("core_y")
        core_sq = sem("core_sq")
        core_y_out = sem("core_y_out")
        core_sum = sem("core_sum")
        core_var = sem("core_var")

        mv_out = sem("mv_out")
        wo_read = sem("wo_read")
        ln2_chain = sem("ln2_chain")
        ln2_log = sem("ln2_log")
        ln2_r = sem("ln2_r")
        x2_out = sem("x2_out")
        x2T_ps = sem("x2T_ps")
        x2T_out = sem("x2T_out")
        logit_ps = sem("logit_ps")
        logit_out = sem("logit_out")
        rt_step = sem("rt_step")
        zrow_set = sem("zrow_set")
        rt_abs = sem("rt_abs")
        rt_exp = sem("rt_exp")
        rt_ln = sem("rt_ln")
        rt_sp = sem("rt_sp")
        rt_sqrt = sem("rt_sqrt")
        rt_masks = sem("rt_masks")
        rt_prefix = sem("rt_prefix")
        prefix_read = sem("prefix_read")
        tab_ready = sem("tab_ready")
        slots_ready = sem("slots_ready")
        scattered = sem("scattered")
        zeroed = sem("zeroed")
        row_in = [sem(f"row_in{b}") for b in range(2)]
        row_used = sem("row_used")
        xT_ps = sem("xT_ps")
        xT_out = sem("xT_out")
        gu_ps = sem("gu_ps")
        silu_out = sem("silu_out")
        up_out = sem("up_out")
        hid_parts = sem("hid_parts")
        hid_out = sem("hid_out")
        hidT_ps = sem("hidT_ps")
        hidT_out = sem("hidT_out")
        y_ps = sem("y_ps")
        y_read = sem("y_read")
        y_stored = [sem(f"y_stored{b}") for b in range(2)]
        gathered = [sem(f"gathered{b}") for b in range(3)]
        comb = sem("comb")
        comb_step = sem("comb_step")
        stored = [sem(f"stored{b}") for b in range(3)]

        KB = PATCH_DIM // 128

        @block.sync
        def _(sp):
            def load_patch(t, b):
                sp.dma_start(patches[:, b], dram["patches"][ds(t, 1)].rearrange("a p k n -> p (a k) n")
                             ).then_inc(patch_in[b], 16)
            load_patch(0, 0)
            load_patch(1, 1)
            with sp.Fori(0, TILES // 2 - 1) as it:
                for b in range(2):
                    sp.wait_ge(embedded, it * 2 + b + 1)
                    load_patch(it * 2 + 2 + b, b)

            sp.wait_ge(consts_set, N_CONST)
            for a in range(2):
                sp.dma_start(wbd[64 * a:64 * a + 64, :, 64 * a:64 * a + 64], dram["maps"]).then_inc(wbd_in, 16)
            def load_chunk(e, q, after=0):
                b = q % 3
                if q < C13:
                    sp.dma_start(stage[0:HALF, b, :], dram["w13"][after:, :, :][ds(e, 1), :, q * STAGE:(q + 1) * STAGE].rearrange(
                        "a p n -> p (a n)")).then_inc(stage_in[b], 16)
                else:
                    r = q - C13
                    sp.dma_start(stage[:, b, 0:STAGE2], dram["w2"][after:, :, :][ds(e, 1), :, r * STAGE2:(r + 1) * STAGE2].rearrange(
                        "a p n -> p (a n)")).then_inc(stage_in[b], 16)

            def store_chunk(e, q):
                b = q % 3
                if q < C13:
                    rows, n, first, rest = HALF, STAGE, q * STAGE, W13
                else:
                    rows, n, first, rest = 128, STAGE2, 2 * W13 + (q - C13) * STAGE2, W2
                for part, at in ((values, first), (rests, first + rest)):
                    sp.dma_start(dram["parts"][ds(e, 1), 0:rows, at:at + n].rearrange("a p n -> p (a n)"),
                                 part[0:rows, b, 0:n]).then_inc(split_in[b], 16)

            def weights_to_dram(k0, count, e0):
                for q in range(2):
                    if k0:
                        sp.wait_ge(split_in[q % 3], 32 * (k0 // 3))
                    load_chunk(e0, q)

                def expert(e, more):
                    k = e * CHUNKS_W
                    for q in range(CHUNKS_W):
                        nxt = q + 2
                        if more or nxt < CHUNKS_W:
                            rounds = e * (CHUNKS_W // 3) + nxt // 3
                            if not isinstance(rounds, int) or rounds > 0:
                                sp.wait_ge(split_in[nxt % 3], rounds * 32)
                            load_chunk(e, nxt % CHUNKS_W, nxt // CHUNKS_W)
                        sp.wait_ge(split, (k + q) * 3 + 3)
                        store_chunk(e, q)
                if e0 == 0:
                    expert(0, True)
                with sp.Fori(max(e0, 1), e0 + count - 1) as e:
                    expert(e, True)
                expert(e0 + count - 1, False)
            weights_to_dram(0, FIRST, 0)
            sp.wait_ge(q_f[3], CHUNKS * PAIRS + 3)
            sp.dma_start(wo, dram["wo"]).then_inc(wo_in, 16)
            def load_expert(place, e, what, done):
                if what == "w13":
                    dst, n, rows, first = w13_all, 2 * W13, HALF, 0
                else:
                    dst, n, rows, first = w2_all, 2 * W2, 128, 2 * W13
                sp.dma_start(dst[:, ds(place * n, n)], dram["parts"][ds(e, 1), 0:rows, first:first + n].rearrange(
                    "a p n -> p (a n)")).then_inc(done, 16)

            weights_to_dram(FIRST * CHUNKS_W, EXPERTS + 1 - FIRST, FIRST)
            sp.wait_ge(core_y_out, 2 * GROUPS + 2)
            for b in range(3):
                sp.wait_ge(split_in[b], 32 * (EXPERTS + 1) * CHUNKS_W // 3)
            load_expert(SHARED, EXPERTS, "w13", shared_in)
            load_expert(SHARED, EXPERTS, "w2", shared_in)
            for e in range(EARLY, SHARED):
                load_expert(e, e, "w13", experts_in)
            sp.wait_ge(wo_read, TILES + 3)
            with sp.Fori(0, EARLY) as e:
                load_expert(e, e, "w13", experts_in)
            with sp.Fori(0, SHARED) as e:
                load_expert(e, e, "w2", experts_in)

            def load_row(m, b):
                sp.dma_start(xrow16[:, b, :], dram["slots"][ds(m * TILE, TILE), :]).then_inc(row_in[b], 16)

            def store_tile(m, b):
                sp.wait_ge(y_read, m + TILES + 2)
                sp.dma_start(dram["expert_out"][ds(m * TILE, TILE), :], orow[:, b, :]).then_inc(y_stored[b], 16)
            sp.wait_ge(x2T_ps, TILES)
            sp.wait_ge(scattered, 16 * 2 * TILES)
            for b in range(2):
                load_row(b, b)
            for b in range(2):
                sp.wait_ge(row_used, TILES + b + 1)
                load_row(2 + b, b)
            with sp.Fori(1, ROUTED_TILES // 2 - 1) as it:
                for b in range(2):
                    sp.wait_ge(row_used, it * 2 + b + 1 + TILES)
                    load_row(it * 2 + 2 + b, b)
                    store_tile(it * 2 + b - 2, b)
            for m in range(ROUTED_TILES - 4, ROUTED_TILES):
                store_tile(m, m % 2)

        @block.gpsimd
        def _(pool):
            n_const = [0]

            def const(ins):
                ins.then_inc(consts_set, 1)
                n_const[0] += 1
                pool.wait_ge(consts_set, n_const[0])

            const(pool.memset(eps[:, :], LN_EPS))
            const(pool.memset(ident[:, :], 0.0))
            const(pool.affine_select(out=ident[:, :], in_=ident[:, :], compare_op=ALU.not_equal, fill=1.0,
                                     base=0, pattern=[[-1, 128]], channel_multiplier=1))
            const(pool.memset(ones[:, :], 1.0))
            const(pool.memset(blk64[:, :], 0.0))
            const(pool.memset(scale16[:, :], SCALE))
            const(pool.memset(wbd[:, :, :], 0.0))
            const(pool.memset(ind[:, :], 0.0))
            const(pool.memset(ind_den[:, :], 0.0))
            const(pool.memset(sel[:, :, :], 0.0))
            const(pool.memset(sel_den[:, :, :], 0.0))
            const(pool.memset(mask[:, :], float(POOLED) ** -0.5))
            const(pool.tensor_copy(ident16[:, :], ident[:, :]))
            const(pool.affine_select(out=upper[:, :], in_=ones[:, :], compare_op=ALU.is_ge, fill=0.0,
                                     base=-1, pattern=[[1, 128]], channel_multiplier=-1))
            for a in range(2):
                rows = slice(64 * a, 64 * a + 64)
                const(pool.memset(blk64[rows, 64 * a:64 * a + 64], 1.0 / HEAD_DIM))
                for r in range(3):
                    first = 32 * r + a
                    const(pool.memset(ind[rows, first:first + 98 * (PAIRS - 1) + 1:98], 1.0 / HEAD_DIM))
            for j in range(4):
                for r in range(3):
                    first = 32 * r + j
                    const(pool.memset(ind_den[32 * j:32 * j + 32, first:first + 100 * (QUADS - 1) + 1:100], 1.0))
            for r in range(3):
                rows = slice(32 * r, 32 * r + 32)
                v = sel[rows, :, :].rearrange("k p (h j) -> k p h j", h=2)
                const(pool.affine_select(out=v, in_=v, compare_op=ALU.not_equal, fill=1.0, base=0,
                                         pattern=[[-2, PAIRS], [-1, 2], [0, 64]], channel_multiplier=1))
                v = sel_den[rows, :, :].rearrange("k q (h j) -> k q h j", h=4)
                const(pool.affine_select(out=v, in_=v, compare_op=ALU.not_equal, fill=1.0, base=0,
                                         pattern=[[-4, QUADS], [-1, 4], [0, 32]], channel_multiplier=1))
            for j in range(4):
                m = mask[32 * j:32 * j + 32, :].rearrange("k (i t) -> k i t", i=GROUP_IMAGES)
                const(pool.affine_select(out=m, in_=m, compare_op=ALU.is_ge, fill=0.0, base=0,
                                         pattern=[[-POOLED, GROUP_IMAGES], [0, TOKENS_PER_IMAGE]], channel_multiplier=1))
            for j in range(4):
                m = mask[32 * j:32 * j + 32, :].rearrange("k (i t) -> k i t", i=GROUP_IMAGES)
                const(pool.affine_select(out=m, in_=m, compare_op=ALU.is_ge, fill=0.0, base=POOLED - 1,
                                         pattern=[[POOLED, GROUP_IMAGES], [0, TOKENS_PER_IMAGE]], channel_multiplier=-1))
            const(pool.iota(iota_e[:, :], [[0, TILES], [1, EXPERTS]], base=0, channel_multiplier=0,
                            allow_small_or_imprecise_dtypes=True))
            const(pool.iota(iota_tok[:, :], [[0, EXPERTS], [TILE, TILES]], base=0, channel_multiplier=0,
                            allow_small_or_imprecise_dtypes=True))
            const(pool.iota(iota_tile[:, :, :], [[1, ROUTED_TILES], [0, EXPERTS]], base=0, channel_multiplier=0,
                            allow_small_or_imprecise_dtypes=True))
            assert n_const[0] == N_CONST, n_const[0]

            def split_experts(e0, count):
                def expert(e):
                    for q in range(CHUNKS_W):
                        b, k = q % 3, e * CHUNKS_W + q
                        rows, n = (HALF, STAGE) if q < C13 else (128, STAGE2)
                        if not isinstance(k, int) or k > 0:
                            pool.wait_ge(split, k * 3)
                        pool.wait_ge(stage_in[b], (e * (CHUNKS_W // 3) + q // 3) * 16 + 16)
                        src = stage[0:rows, b, 0:n]
                        scale = scale16[0:rows, 0:1].to_broadcast([rows, n])
                        pool.tensor_tensor(values[0:rows, b, 0:n], src, scale, ALU.mult).then_inc(split, 1)
                        pool.wait_ge(split, k * 3 + 1)
                        pool.tensor_tensor(src, src, scale, ALU.mult).then_inc(split, 1)
                        pool.wait_ge(split, k * 3 + 2)
                        pool.tensor_tensor(rests[0:rows, b, 0:n], src, values[0:rows, b, 0:n],
                                           ALU.subtract).then_inc(split, 1)
                if e0 == 0:
                    expert(0)
                with pool.Fori(max(e0, 1), e0 + count) as e:
                    expert(e)
            split_experts(0, FIRST)
            pool.wait_ge(v_out, PAIRS)
            pool.wait_ge(ks[0].y_ps, 1)
            for blocks in (kblk, vblk, vw):
                pool.memset(blocks, 0.0).then_inc(blocks_zero, 1)
            pool.wait_ge(blocks_zero, 3)
            pool.wait_ge(ks[2].g_out, PAIRS + 3)
            with pool.Fori(0, GROUPS // 2) as it:
                for b in range(2):
                    g = it * 2 + b
                    pool.wait_ge(core_s, g + 1)
                    for src, dst in ((kc3, kblk), (vcT, vblk)):
                        for odd in range(2):
                            for a in range(2):
                                rows = slice(64 * a, 64 * a + 64)
                                first = 64 * odd + 32 * a
                                pool.tensor_copy(
                                    dst[rows, b, odd::2, first:first + GROUP_ROWS],
                                    src[rows, odd::2, ds(g * GROUP_ROWS, GROUP_ROWS)]).then_inc(core_kv, 1)
            pool.wait_ge(core_kv, 8 * GROUPS)
            split_experts(FIRST, EXPERTS + 1 - FIRST)
            pool.wait_ge(wo_read, TILES + 3)
            pool.memset(zrow, 0.0).then_inc(zrow_set, 1)
            pool.wait_ge(zrow_set, 1)
            n0 = 8 * TILE
            for z in range(6):
                lo, hi = z * n0, min((z + 1) * n0, ROUTED_TILES * TILE)
                k = (hi - lo) // TILE
                pool.dma_start(dram["slots"][lo:hi, :].rearrange("(p a) d -> p (a d)", p=128),
                               zrow[:, 0:k * DIM].bitcast(F16)).then_inc(zeroed, 16)
            pool.wait_ge(zeroed, 16 * 6)
            pool.wait_ge(slots_ready, 1)
            for t in range(TILES):
                for k in range(2):
                    pool.indirect_dma_start(dram["slots"][:, :], bass.IndirectOffsetOnAxis(slot[:, k, t:t + 1], 0),
                                            x2c[:, t, :, :].rearrange("p a d -> p (a d)"), None).then_inc(scattered, 16)
            pool.wait_ge(y_ps, TILES * UNITS)
            for dst, rows, first, n in ((w13_all, HALF, 0, 2 * W13), (w2_all, 128, 2 * W13, 2 * W2)):
                pool.dma_start(dst[:, SHARED * n:(SHARED + 1) * n],
                               dram["parts"][SHARED, 0:rows, first:first + n]).then_inc(last_in, 16)
            for b in range(2):
                pool.wait_ge(y_stored[b], 16 * (ROUTED_TILES // 2))
            for t in range(TILES):
                b = t % 3
                if t >= 3:
                    pool.wait_ge(comb, t - 2)
                for k in range(2):
                    pool.indirect_dma_start(gath[:, b, k, :], None, dram["expert_out"][:, :],
                                            bass.IndirectOffsetOnAxis(slot[:, k, t:t + 1], 0)).then_inc(gathered[b], 16)

        @block.tensor
        def _(pe):
            pe.wait_ge(wp_in, 16)
            def embed(it, b):
                t = it * 2 + b
                pe.wait_ge(patch_in[b], (it + 1) * 16)
                pe.wait_ge(emb_read, t + 1)
                for k in range(KB):
                    mm = pe.matmul(bank[b][:, 0:DIM], patches[:, b, k, :], wp[:, k, :],
                                   start=(k == 0), stop=(k == KB - 1))
                mm.then_inc(embedded, 1)

            def turn_x1(it, b):
                t = it * 2 + b
                pe.wait_ge(x1_ready, t + 1)
                pe.wait_ge(x1T_ready, t + 1)
                for h in range(2):
                    mm = pe.transpose(bank[2 + b][0:HALF, h * TILE:(h + 1) * TILE],
                                      xrow[:, b, h * HALF:(h + 1) * HALF], ident[:, :])
                mm.then_inc(x1T_ps, 1)

            embed(0, 0)
            pe.wait_ge(consts_set, 3)
            with pe.Fori(0, TILES // 2 - 1) as it:
                embed(it, 1)
                turn_x1(it, 0)
                embed(it + 1, 0)
                turn_x1(it, 1)
            embed(TILES // 2 - 1, 1)
            turn_x1(TILES // 2 - 1, 0)
            turn_x1(TILES // 2 - 1, 1)

            pe.wait_ge(consts_set, N_CONST)
            pe.wait_ge(small_in, 16 * SMALL_LOADS)
            pe.matmul(bank[7][:, 0:2 * STAGES], blk64[:, :], vecs[:, 0:2 * STAGES], start=True,
                      stop=True).then_inc(bmean_ready, 1)
            pe.wait_ge(x1T_ready, TILES + 2)
            pe.wait_ge(wqkv_in, 48)
            pe.wait_ge(xp_out, 2)
            xpf = xp.rearrange("p (h i) r -> p h (i r)", h=2)
            for p in range(PAIRS):
                if p >= 2:
                    pe.wait_ge(v_out, p - 1)
                for h in range(2):
                    mm = pe.matmul(bank[4 + p % 2][:, 0:K3], wv[0:HALF, h, p * 128:(p + 1) * 128],
                                   xpf[0:HALF, h, :], start=(h == 0), stop=(h == 1))
                mm.then_inc(v_ps, 1)
            def project(w, ps_sem, free_sem, c, p):
                pe.wait_ge(free_sem, c * PAIRS + p + 1)
                for h in range(2):
                    mm = pe.matmul(bank[p % 3][:, 0:CHUNK], w[0:HALF, h, p * 128:(p + 1) * 128],
                                   x1T[0:HALF, h, ds(c * CHUNK, CHUNK)], start=(h == 0), stop=(h == 1))
                mm.then_inc(ps_sem, 1)
            pe.wait_ge(emb_read, TILES + 2)
            with pe.Fori(0, CHUNKS) as c:
                for p in range(PAIRS):
                    project(wk, k_f[0], k_f[3], c, p)
            pe.wait_ge(prep, PREP)
            for i in range(STAGES):
                buf, n, chunks = KSTAGE[i]
                if i == 0:
                    pe.wait_ge(k_f[4], CHUNKS * PAIRS + 3)
                    pe.wait_ge(v_out, PAIRS)
                else:
                    pe.wait_ge(ks[i - 1].next_out, 3 + KSTAGE[i - 1][2] * PAIRS)

                def f_body(c):
                    for p in range(PAIRS):
                        f_pe(pe, ks[i], buf[:, p, ds(c * n, n)], wbd[:, i, :], n, c, p, lambda: None)
                        if p:
                            s_pe(pe, ks[i], n, c, p - 1)
                    s_pe(pe, ks[i], n, c, PAIRS - 1)
                loop(pe, chunks, f_body)
                pe.wait_ge(r_ready, i + 1)

                def g_body(c):
                    for p in range(PAIRS):
                        b_pe(pe, ks[i], n, c, p)
                loop(pe, chunks, g_body)
            pe.wait_ge(ks[2].z_out, 3 + PAIRS)
            with pe.Fori(0, CHUNKS) as c:
                for p in range(PAIRS):
                    project(wq, q_f[0], q_f[3], c, p)
            pe.wait_ge(q_f[3], 3 + CHUNKS * PAIRS)

            def core_a(it, b):
                g = it * 2 + b
                pe.wait_ge(core_kv, (g + 1) * 8)
                pe.wait_ge(core_vw_out, g * 2 + 2)
                for p in range(PAIRS):
                    mm = pe.matmul(bank[0][:, (p // 2) * 128:(p // 2) * 128 + 128], vblk[:, b, p, :],
                                   wbd[:, 2 * STAGES - 1, :], start=(p % 2 == 0), stop=(p % 2 == 1))
                mm.then_inc(core_vw, 1)
                pe.wait_ge(core_sm, g + 1)
                for p in range(PAIRS):
                    mm = pe.matmul(bank[1][:, (p // 2) * GROUP:(p // 2 + 1) * GROUP], kblk[:, b, p, :],
                                   q_y[:, p, ds(g * GROUP, GROUP)], start=(p % 2 == 0), stop=(p % 2 == 1))
                mm.then_inc(core_s, 1)

            def core_d(it, b):
                g = it * 2 + b
                pe.wait_ge(core_sm, g + 2)
                pe.wait_ge(core_chain, g * 6 + 1)
                for q in range(QUADS):
                    mm = pe.matmul(bank[2][0:96, 0:GROUP], ind_den[:, 96 * q:96 * q + 96], sm[:, b, q, :],
                                   start=(q == 0), stop=(q == QUADS - 1))
                mm.then_inc(core_den, 1)

            def core_b(it, b):
                g = it * 2 + b
                pe.wait_ge(core_r, g + 1)
                pe.wait_ge(core_sn, g + 1)
                for q in range(QUADS):
                    mm = pe.matmul(bank[3][:, q * GROUP:(q + 1) * GROUP], sel_den[:, q, :], dsplit[:, :],
                                   start=True, stop=True)
                mm.then_inc(core_rb, 1)

            def core_yy(it, b):
                g = it * 2 + b
                pe.wait_ge(core_sn, g + 2)
                pe.wait_ge(core_vw_out, g * 2 + 4)
                pe.wait_ge(core_y_out, g * 2 + 2)
                pe.wait_ge(core_sq, g * 2 + 2)
                for p in range(PAIRS):
                    mm = pe.matmul(bank[4 + p // 3][:, (p % 3) * GROUP:(p % 3 + 1) * GROUP],
                                   vw[:, b, p, :], sn[:, b, p // 2, :], start=True, stop=True)
                mm.then_inc(core_y, 1)

            def core_st(it, b):
                g = it * 2 + b
                pe.wait_ge(core_sq, g * 2 + 4)
                pe.wait_ge(core_var, g + 1)
                for p in range(PAIRS):
                    mm = pe.matmul(bank[6][0:96, 0:GROUP], ind[:, 96 * p:96 * p + 96], sq[:, p, :],
                                   start=(p == 0), stop=(p == PAIRS - 1))
                mm.then_inc(core_sum, 1)

            def core_step(it, b, last=False):
                core_b(it, b)
                if not last:
                    core_a(it + b, 1 - b)
                core_yy(it, b)
                if not last:
                    core_d(it + b, 1 - b)
                core_st(it, b)
            core_a(0, 0)
            core_d(0, 0)
            with pe.Fori(0, GROUPS // 2 - 1) as it:
                core_step(it, 0)
                core_step(it, 1)
            core_step(GROUPS // 2 - 1, 0)
            core_step(GROUPS // 2 - 1, 1, last=True)

            for i in range(STAGES - 1):
                G, Fn = es[i], es[i + 1]
                pe.wait_ge(r_ready, STAGES + i + 1)

                def gf_body(c, before, more):
                    for p in range(PAIRS):
                        if p + 2 < PAIRS:
                            b_pe(pe, G, CHUNK, c, p + 2)
                        elif more:
                            b_pe(pe, G, CHUNK, c + 1, p + 2 - PAIRS)
                        f_pe(pe, Fn, gb[:, p % 3, :], wbd[:, 2 * STAGES - 2 - i, :], CHUNK, c, p,
                             lambda: pe.wait_ge(G.g_out, c * PAIRS + p + 4))
                        if p:
                            s_pe(pe, Fn, CHUNK, c, p - 1)
                        elif before:
                            s_pe(pe, Fn, CHUNK, c - 1, PAIRS - 1)
                b_pe(pe, G, CHUNK, 0, 0)
                b_pe(pe, G, CHUNK, 0, 1)
                chunks_with_ends(pe, gf_body)
                s_pe(pe, Fn, CHUNK, CHUNKS - 1, PAIRS - 1)
            pe.wait_ge(r_ready, 2 * STAGES)
            G = es[2]
            pe.wait_ge(wo_in, 16)
            pe.wait_ge(G.y_out, 3 + CHUNKS * PAIRS)

            def go_body(c, more):
                for p in range(PAIRS):
                    if p + 2 < PAIRS:
                        b_pe(pe, G, CHUNK, c, p + 2)
                    elif more:
                        b_pe(pe, G, CHUNK, c + 1, p + 2 - PAIRS)
                    pe.wait_ge(G.g_out, c * PAIRS + p + 4)
                    for j in range(3):
                        if p == 0:
                            pe.wait_ge(wo_read, c * 3 + j + 1)
                        mm = pe.matmul(bank[3 + j][:, 0:DIM], gb[:, p % 3, j * TILE:(j + 1) * TILE], wo[:, p, :],
                                       start=(p == 0), stop=(p == PAIRS - 1))
                    mm.then_inc(G.next_out, 1)
            b_pe(pe, G, CHUNK, 0, 0)
            b_pe(pe, G, CHUNK, 0, 1)
            with pe.Fori(0, CHUNKS - 1) as c:
                go_body(c, True)
            go_body(CHUNKS - 1, False)

            pe.wait_ge(G.z_out, 3 + CHUNKS * PAIRS)
            pe.wait_ge(wo_read, 3 + TILES)
            with pe.Fori(0, TILES // 2) as it:
                for b in range(2):
                    t = it * 2 + b
                    pe.wait_ge(x2_out, t * 3 + 1)
                    pe.wait_ge(x2T_out, t + 1)
                    for h in range(2):
                        mm = pe.transpose(bank[b][0:HALF, h * TILE:(h + 1) * TILE],
                                          xrow[:, b, h * HALF:(h + 1) * HALF], ident[:, :])
                    mm.then_inc(x2T_ps, 1)
                    pe.wait_ge(x2T_out, t + 3)
                    pe.wait_ge(logit_out, t + 1)
                    for h in range(2):
                        mm = pe.matmul(bank[2 + b][:, 0:EXPERTS], xT[:, b, h, :], gatew[:, h, :],
                                       start=(h == 0), stop=(h == 1))
                    mm.then_inc(logit_ps, 1)
            pe.wait_ge(rt_masks, 1)
            pe.matmul(bank[0][:, 0:N144], upper[:, :], rt[:, 7, :], start=True, stop=True)
            pe.matmul(bank[1][:, 0:N144], ones[:, :], rt[:, 7, :], start=True, stop=True).then_inc(rt_prefix, 1)

            def turn_row(rows):
                for k in range(4):
                    mm = pe.transpose(bank16[7][0:HALF, k * TILE:(k + 1) * TILE], rows[:, k * HALF:(k + 1) * HALF],
                                      ident16[:, :])
                mm.then_inc(row_used, 1)

            def turn_shared(n):
                turn_row(x2c[:, ds(n, 1), :, :].rearrange("p t a d -> p (t a d)"))

            def turn_routed(b, k):
                pe.wait_ge(row_in[b], k * 16)
                turn_row(xrow16[:, b, :])

            def gate_up(n, b, u, e):
                if u == 0:
                    pe.wait_ge(xT_out, n + 1)
                pe.wait_ge(up_out, n * UNITS + u + 1)
                parts = [(x, w, h) for x, w in ((0, 0), (0, 1), (1, 0)) for h in range(2)]
                for i in range(6):
                    x, w, h = parts[i]
                    mm = pe.matmul(bank[u][:, :], xT16[:, b, 2 * x + h, :],
                                   w13_all[:, ds(e * 2 * W13 + w * W13 + h * 2 * HIDDEN + u * 512, 512)],
                                   start=(i == 0), stop=(i == 5))
                mm.then_inc(gu_ps, 1)

            def turn_hid(n, u):
                pe.wait_ge(hid_out, n * UNITS + u + 1)
                pe.wait_ge(hidT_out, n * UNITS + u + 1)
                for k in range(4):
                    mm = pe.transpose(bank16[3 + u][:, k * 128:(k + 1) * 128],
                                      hsplit[:, u, k // 2, (k % 2) * 128:(k % 2 + 1) * 128], ident16[:, :])
                mm.then_inc(hidT_ps, 1)

            def down(n, u, e):
                pe.wait_ge(hidT_out, n * UNITS + u + 4)
                if u == 0:
                    pe.wait_ge(y_read, n + 1)
                for x, w in ((0, 0), (0, 1), (1, 0)):
                    for j in range(2):
                        mm = pe.matmul(bank[6][:, 0:DIM], hidT[:, u, 2 * x + j, :],
                                       w2_all[:, ds(e * 2 * W2 + w * W2 + (2 * u + j) * DIM, DIM)],
                                       start=(u == 0 and x + w + j == 0),
                                       stop=(u == UNITS - 1 and x == 1 and j == 1))
                mm.then_inc(y_ps, 1)

            def tile(n, b, e, before, turn_next, load_next=None):
                for u in range(UNITS):
                    gate_up(n, b, u, e)
                    if callable(before):
                        before = before()
                    if u == 1 and load_next is not None:
                        load_next()
                    if u == 0 and turn_next is not None:
                        turn_next()
                    if u == 2:
                        turn_hid(n, 0)
                    elif before is not None:
                        turn_hid(n - 1, u + 1)
                    if before is not None:
                        down(n - 1, u, before)

            pe.wait_ge(shared_in, 32)
            pe.wait_ge(prefix_read, 1)
            turn_shared(0)
            tile(0, 0, SHARED, None, lambda: turn_shared(1))
            tile(1, 1, SHARED, SHARED, lambda: turn_shared(2))
            with pe.Fori(1, TILES // 2 - 1) as it:
                for b in range(2):
                    n = it * 2 + b
                    tile(n, b, SHARED, SHARED, lambda: turn_shared(n + 1))
            tile(TILES - 2, 0, SHARED, SHARED, lambda: turn_shared(TILES - 1))
            tile(TILES - 1, 1, SHARED, SHARED, lambda: turn_routed(0, 1))
            pe.wait_ge(tab_ready, 1)
            pe.wait_ge(experts_in, 16 * 2 * SHARED)

            def expert_of(j):
                return pe.value_load(tab[0:1, ds(j, 1)], min_val=0, max_val=EXPERTS - 1)
            first = expert_of(1)
            tile(TILES, 0, first, SHARED, lambda: turn_routed(1, 1))
            tile(TILES + 1, 1, expert_of(2), first, lambda: turn_routed(0, 2))
            pe.wait_ge(last_in, 32)
            with pe.Fori(1, ROUTED_TILES // 2 - 1) as it:
                e = [expert_of(it * 2 + 1)]
                tile(it * 2 + TILES, 0, e[0], lambda: expert_of(it * 2), lambda: turn_routed(1, it + 1),
                     lambda: e.append(expert_of(it * 2 + 2)))
                tile(it * 2 + TILES + 1, 1, e[1], e[0], lambda: turn_routed(0, it + 2))
            n = TILES + ROUTED_TILES - 2
            e0, e1 = expert_of(ROUTED_TILES - 1), expert_of(ROUTED_TILES)
            tile(n, 0, e0, expert_of(ROUTED_TILES - 2), lambda: turn_routed(1, ROUTED_TILES // 2))
            tile(n + 1, 1, e1, e0, None)
            turn_hid(n + 1, 1)
            down(n + 1, 0, e1)
            turn_hid(n + 1, 2)
            down(n + 1, 1, e1)
            down(n + 1, 2, e1)

        @block.scalar
        def _(act):
            act.dma_start(wp, dram["wp"]).then_inc(wp_in, 16)
            for dst, name in ((bproj, "bproj"), (bo, "bo"), (vecs, "vecs"), (gbias, "gbias")):
                act.dma_start(dst[:, :], dram[name]).then_inc(small_in, 16)
            act.dma_start(gatew[:, :, :], dram["gatew"]).then_inc(small_in, 16)
            act.dma_start(wv[0:HALF], dram["wv"]).then_inc(wqkv_in, 16)
            act.dma_start(wk[0:HALF], dram["wk"]).then_inc(wqkv_in, 16)
            act.dma_start(wq[0:HALF], dram["wq"]).then_inc(wqkv_in, 16)
            act.wait_ge(consts_set, 1)
            act.sem_inc(x1T_ready, 2)
            act.sem_inc(core_vw_out, 2)
            act.sem_inc(core_sq, 2)
            for P in ks + es[1:]:
                act.sem_inc(P.y_sq, 3)
            for P in ks + es:
                act.sem_inc(P.g_out, 3)
            act.sem_inc(x2T_out, 2)
            act.sem_inc(hidT_out, 3)
            act.sem_inc(silu_out, 3)

            act.preload_act_table_set(LN_EXP_TABLES)

            def norm1(t, b):
                act.wait_ge(ln1_stat, t + 1)
                act.activation(lnv[:, b:b + 1], mv1[:, b, 1:2], ACT.Ln, bias=eps[:, :]).then_inc(ln1_act, 1)
                act.wait_ge(ln1_act, t * 2 + 1)
                act.activation(rs1[:, b:b + 1], lnv[:, b:b + 1], ACT.Exp, scale=-0.5).then_inc(ln1_act, 1)

            with act.Fori(0, TILES // 2) as it:
                for b in range(2):
                    t = it * 2 + b
                    norm1(t, b)
                    act.wait_ge(x1T_ps, t + 1)
                    act.activation(x1T[0:HALF, :, ds(t * TILE, TILE)],
                                   bank[2 + b][0:HALF, 0:2 * TILE].rearrange("p (h t) -> p h t", h=2),
                                   ACT.Copy).then_inc(x1T_ready, 1)
            for p in range(PAIRS):
                act.wait_ge(v_ps, p + 1)
                act.activation(vcT[:, p, :], bank[4 + p % 2][:, 0:K3], ACT.Copy, scale=1.0 / 8).then_inc(v_out, 1)

            def exp_unit(S, used, c, p):
                act.wait_ge(S[0], c * PAIRS + p + 1)
                act.wait_ge(used, c * PAIRS + p + 1)
                act.activation(gb[:, p % 3, :], bank[p % 3][:, 0:CHUNK], ACT.Exp).then_inc(S[1], 1)
            with act.Fori(0, CHUNKS) as c:
                for p in range(PAIRS):
                    exp_unit(k_f, k_f[4], c, p)
            for i in range(STAGES):
                buf, n, chunks = KSTAGE[i]
                act.wait_ge(prep, PREP)
                act.preload_act_table(ACT.Gelu)

                def f_body(c):
                    for p in range(PAIRS):
                        f_act(act, ks[i], i, n, c, p)
                loop(act, chunks, f_body)
                r_act(act, ks[i], chunks, n * chunks, i)
                act.preload_act_table(ACT.Gelu)

                def g_body(c):
                    for p in range(PAIRS):
                        if i < 2:
                            g_act(act, ks[i], i, n, c, p)
                        else:
                            act.wait_ge(ks[i].z_out, c * PAIRS + p + 4)
                            act.activation(kc3[:, p, :], zb[:, p % 3, 0:n], ACT.Gelu, bias=shift_of(i),
                                           scale=gain_of(i)).then_inc(ks[i].g_out, 1)
                loop(act, chunks, g_body)
            act.preload_act_table(ACT.Exp)
            with act.Fori(0, CHUNKS) as c:
                for p in range(PAIRS):
                    exp_unit(q_f, q_f[3], c, p)

            act.wait_ge(blocks_zero, 3)

            def vw_copy(it, b):
                g = it * 2 + b
                act.wait_ge(core_vw, g + 1)
                act.wait_ge(core_y, g + 1)
                for odd in range(2):
                    rows = slice(64 * odd, 64 * odd + 64)
                    act.activation(vw[rows, b, odd::2, :],
                                   bank[0][rows, 0:QUADS * 128].rearrange("p (q e) -> p q e", q=QUADS),
                                   ACT.Copy).then_inc(core_vw_out, 1)

            def square(it, b):
                g = it * 2 + b
                act.wait_ge(core_y, g + 3)
                act.wait_ge(core_sum, g + 1)
                for q in range(2):
                    act.activation(sq[:, 3 * q:3 * q + 3, :],
                                         bank[4 + q][:, 0:3 * GROUP].rearrange("p (a t) -> p a t", a=3),
                                         ACT.Square, bias=bias_of(2 * STAGES - 1)).then_inc(core_sq, 1)
            vw_copy(0, 0)
            with act.Fori(0, GROUPS // 2 - 1) as it:
                vw_copy(it, 1)
                square(it, 0)
                vw_copy(it + 1, 0)
                square(it, 1)
            vw_copy(GROUPS // 2 - 1, 1)
            square(GROUPS // 2 - 1, 0)
            square(GROUPS // 2 - 1, 1)
            act.preload_act_table_set(LN_EXP_TABLES)
            act.wait_ge(core_var, GROUPS + 1)
            act.activation(var[:, :], var[:, :], ACT.Ln, bias=eps[0:96, :]).then_inc(r_log, 1)
            act.wait_ge(r_log, STAGES + 1)
            act.activation(rstd[:, :], var[:, :], ACT.Exp, scale=-0.5).then_inc(r_exp, 1)
            for i in range(STAGES):
                G = es[i]
                s = 2 * STAGES - 1 - i
                act.preload_act_table(ACT.Gelu)

                def gf_body(c, before, more):
                    for p in range(PAIRS):
                        g_act(act, G, s, CHUNK, c, p, consumed=(i == STAGES - 1))
                        if i < STAGES - 1:
                            if p:
                                f_act(act, es[i + 1], s - 1, CHUNK, c, p - 1)
                            elif before:
                                f_act(act, es[i + 1], s - 1, CHUNK, c - 1, PAIRS - 1)
                if i < STAGES - 1:
                    chunks_with_ends(act, gf_body)
                    f_act(act, es[i + 1], s - 1, CHUNK, CHUNKS - 1, PAIRS - 1)
                    r_act(act, es[i + 1], CHUNKS, TOKENS, STAGES + 1 + i)
                else:
                    with act.Fori(0, CHUNKS) as c:
                        gf_body(c, False, False)

            act.preload_act_table_set(LN_EXP_TABLES)
            act.wait_ge(mv_out, TILES)
            act.activation(ln2[:, :], mv2[:, :, 1], ACT.Ln, bias=eps[:, :]).then_inc(ln2_log, 1)
            act.wait_ge(ln2_log, 1)
            act.activation(rs2[:, :], ln2[:, :], ACT.Exp, scale=-0.5).then_inc(ln2_r, 1)
            with act.Fori(0, TILES // 2) as it:
                for b in range(2):
                    t = it * 2 + b
                    act.wait_ge(x2T_ps, t + 1)
                    act.wait_ge(logit_ps, t + 1)
                    act.activation(xT[:, b, :, :],
                                   bank[b][0:HALF, 0:2 * TILE].rearrange("p (h t) -> p h t", h=2),
                                   ACT.Copy).then_inc(x2T_out, 1)
            act.wait_ge(rt_abs, 1)
            act.activation(rt[:, 2, :], rt[:, 1, :], ACT.Exp, scale=-1.0).then_inc(rt_exp, 1)
            act.wait_ge(rt_exp, 1)
            act.activation(rt[:, 3, :], rt[:, 2, :], ACT.Ln, bias=1.0).then_inc(rt_ln, 1)
            act.wait_ge(rt_sp, 1)
            act.activation(rt[:, 2, :], rt[:, 1, :], ACT.Sqrt).then_inc(rt_sqrt, 1)

            def turned(n, b):
                act.wait_ge(row_used, n + 1)
                act.wait_ge(gu_ps, n * UNITS - 3) if not isinstance(n, int) or n >= 2 else None
                act.activation(xT16[:, b, :, :],
                               bank16[7][0:HALF, 0:4 * TILE].rearrange("p (k t) -> p k t", k=4),
                               ACT.Copy).then_inc(xT_out, 1)

            def silu(n, u):
                act.wait_ge(gu_ps, n * UNITS + u + 1)
                act.wait_ge(hid_out, n * UNITS + u - 2) if not isinstance(n, int) or n >= 1 else None
                act.activation(sgate[:, u, :], bank[u][:, 0:UNIT], ACT.Silu, scale=1.0 / SCALE).then_inc(silu_out, 1)

            def hid_copy(n, u):
                act.wait_ge(hidT_ps, n * UNITS + u + 1)
                act.wait_ge(y_ps, n * UNITS + u - 2) if not isinstance(n, int) or n >= 1 else None
                act.activation(hidT[:, u, :, :], bank16[3 + u][:, 0:512].rearrange("p (k t) -> p k t", k=4),
                               ACT.Copy).then_inc(hidT_out, 1)

            def tile(n, b, first=False, more=True):
                for u in range(UNITS):
                    silu(n, u)
                    if u == 0 and more:
                        turned(n + 1, 1 - b)
                    if u == 2:
                        hid_copy(n, 0)
                    elif not first:
                        hid_copy(n - 1, u + 1)
            turned(0, 0)
            tile(0, 0, first=True)
            tile(1, 1)
            with act.Fori(1, (TILES + ROUTED_TILES) // 2 - 1) as it:
                for b in range(2):
                    tile(it * 2 + b, b)
            n = TILES + ROUTED_TILES - 2
            tile(n, 0)
            tile(n + 1, 1, more=False)
            hid_copy(n + 1, 1)
            hid_copy(n + 1, 2)

            for t in range(TILES):
                act.wait_ge(comb, t + 1)
                act.dma_start(out[t * TILE:(t + 1) * TILE, :], orow[:, t % 3, :]).then_inc(stored[t % 3], 16)
            for b in range(3):
                act.wait_ge(stored[b], 16 * (TILES // 3))

        @block.vector
        def _(dve):
            def routing():
                count = [0]

                def step(ins, signal=None):
                    if signal is None:
                        count[0] += 1
                        ins.then_inc(rt_step, 1)
                        dve.wait_ge(rt_step, count[0])
                    else:
                        ins.then_inc(signal, 1)
                        dve.wait_ge(signal, 1)

                def by_token(x):
                    return x.rearrange("p (t e) -> p t e", t=TILES)

                def over_experts(x):
                    return x.unsqueeze(2).to_broadcast([128, TILES, EXPERTS])

                L, A, E, LN, SC, R, TMP, M, M1, M2, SA, SB = (rt[:, k, :] for k in range(12))
                s1, s2, w1, w2, inv, pos = (small[:, k, :] for k in range(6))
                step(dve.scalar_tensor_tensor(out=A, in0=L, scalar=-1.0, in1=L, op0=ALU.mult, op1=ALU.max), rt_abs)
                dve.wait_ge(rt_ln, 1)
                step(dve.tensor_scalar(SC, E, -1.0 / 6, None, ALU.mult))
                for c in (1.0 / 5, -1.0 / 4, 1.0 / 3, -1.0 / 2, 1.0):
                    step(dve.scalar_tensor_tensor(out=SC, in0=SC, scalar=c, in1=E, op0=ALU.add, op1=ALU.mult))
                step(dve.tensor_tensor(SC, SC, LN, ALU.subtract))
                step(dve.scalar_tensor_tensor(out=SC, in0=E, scalar=0.06, in1=SC, op0=ALU.is_lt, op1=ALU.mult))
                step(dve.tensor_tensor(LN, LN, SC, ALU.add))
                step(dve.scalar_tensor_tensor(out=A, in0=L, scalar=0.0, in1=LN, op0=ALU.max, op1=ALU.add))
                step(dve.tensor_scalar(A, A, 1e-30, None, ALU.max), rt_sp)
                dve.wait_ge(rt_sqrt, 1)
                step(dve.reciprocal(LN, E))
                step(dve.scalar_tensor_tensor(out=LN, in0=A, scalar=0.5, in1=LN, op0=ALU.mult, op1=ALU.mult))
                step(dve.scalar_tensor_tensor(out=SC, in0=E, scalar=0.5, in1=LN, op0=ALU.mult, op1=ALU.add))
                step(dve.tensor_tensor(by_token(R), by_token(SC),
                                       gbias[:, :].unsqueeze(1).to_broadcast([128, TILES, EXPERTS]), ALU.add))
                for mk in (M1, M2):
                    step(dve.tensor_reduce(s1, by_token(R), AX.X, ALU.max))
                    step(dve.tensor_tensor(by_token(TMP), by_token(R), over_experts(s1), ALU.is_equal))
                    step(dve.scalar_tensor_tensor(out=TMP, in0=TMP, scalar=-100.0, in1=iota_e[:, :], op0=ALU.mult,
                                                  op1=ALU.add))
                    step(dve.tensor_reduce(s2, by_token(TMP), AX.X, ALU.min))
                    step(dve.tensor_scalar(TMP, iota_e[:, :], -100.0, None, ALU.add))
                    step(dve.tensor_tensor(by_token(mk), by_token(TMP), over_experts(s2), ALU.is_equal))
                    if mk is M1:
                        step(dve.scalar_tensor_tensor(out=R, in0=M1, scalar=-1e30, in1=R, op0=ALU.mult, op1=ALU.add))
                step(dve.tensor_tensor(M, M1, M2, ALU.add), rt_masks)
                for mk, s in ((M1, s1), (M2, s2)):
                    step(dve.tensor_tensor(TMP, mk, SC, ALU.mult))
                    step(dve.tensor_reduce(s, by_token(TMP), AX.X, ALU.add))
                step(dve.tensor_tensor(inv, s1, s2, ALU.add))
                step(dve.tensor_scalar(inv, inv, 1e-6, None, ALU.max))
                step(dve.reciprocal(pos, inv))
                for w, s in ((w1, s1), (w2, s2)):
                    step(dve.scalar_tensor_tensor(out=w, in0=s, scalar=1.0 / (SCALE * SCALE), in1=pos, op0=ALU.mult,
                                                  op1=ALU.mult))
                dve.wait_ge(rt_prefix, 1)
                step(dve.tensor_copy(L, bank[1][:, 0:N144]))
                step(dve.tensor_copy(A, bank[0][:, 0:N144]), prefix_read)
                src, dst = L, SA
                shift = 1
                while shift < TILES:
                    n = shift * EXPERTS
                    step(dve.tensor_copy(dst[:, 0:n], src[:, 0:n]))
                    step(dve.tensor_tensor(dst[:, n:N144], src[:, n:N144], src[:, 0:N144 - n], ALU.add))
                    src, dst = dst, (SB if dst is SA else SA)
                    shift *= 2
                total = ecount[:, 0, :]
                step(dve.tensor_copy(total, src[:, N144 - EXPERTS:N144]))
                step(dve.tensor_tensor(TMP, src, L, ALU.subtract))
                step(dve.tensor_tensor(TMP, TMP, A, ALU.add))
                tiles = ecount[:, 1, :]
                by_expert = SA.rearrange("p (e j) -> p e j", e=EXPERTS)
                step(dve.tensor_tensor(by_expert, iota_tok[:, :].rearrange("p (e j) -> p e j", e=EXPERTS),
                                       total.unsqueeze(2).to_broadcast([128, EXPERTS, TILES]), ALU.is_lt))
                step(dve.tensor_reduce(tiles, by_expert, AX.X, ALU.add))
                step(dve.tensor_copy(ecount[:, 2, :], tiles))
                src, dst = ecount[:, 2, :], ecount[:, 3, :]
                for n in (1, 2, 4):
                    step(dve.tensor_copy(dst[:, 0:n], src[:, 0:n]))
                    step(dve.tensor_tensor(dst[:, n:EXPERTS], src[:, n:EXPERTS], src[:, 0:EXPERTS - n], ALU.add))
                    src, dst = dst, src
                ends = src
                step(dve.tensor_tensor(cmp_tile[:, :, :], iota_tile[:, :, :],
                                       ends[0:1, :].unsqueeze(1).to_broadcast([1, ROUTED_TILES, EXPERTS]), ALU.is_ge))
                step(dve.tensor_reduce(tile_expert[:, :], cmp_tile[:, :, :], AX.X, ALU.add))
                step(dve.memset(tab[:, 0:1], SHARED))
                step(dve.tensor_scalar(tab[:, 1:1 + ROUTED_TILES], tile_expert[:, :], float(EXPERTS - 1), None,
                                       ALU.min), tab_ready)
                step(dve.tensor_tensor(dst, ends, tiles, ALU.subtract))
                step(dve.tensor_scalar(dst, dst, float(TILE), None, ALU.mult))
                step(dve.tensor_tensor(by_token(TMP), by_token(TMP),
                                       dst.unsqueeze(1).to_broadcast([128, TILES, EXPERTS]), ALU.add))
                for k, mk in enumerate((M1, M2)):
                    step(dve.tensor_tensor(R, mk, TMP, ALU.mult))
                    step(dve.tensor_reduce(pos, by_token(R), AX.X, ALU.add))
                    step(dve.tensor_copy(slot[:, k, :], pos), slots_ready if k else None)

            dve.sem_inc(emb_read, 2)
            for P in ks + es[1:]:
                dve.sem_inc(P.y_out, 3)
                dve.sem_inc(P.var_out, 1)
                dve.sem_inc(P.sums, 3)
            for P in ks + es:
                dve.sem_inc(P.z_out, 3)
            for P in (ks[0], ks[1], es[2]):
                dve.sem_inc(P.next_out, 3)
            for s in (k_f[3], q_f[3], k_f[4]):
                dve.sem_inc(s, 3)
            dve.sem_inc(core_s, 2)
            dve.sem_inc(core_sm, 1)
            dve.sem_inc(core_chain, 1)
            dve.sem_inc(core_sn, 1)
            dve.sem_inc(core_y, 2)
            dve.sem_inc(core_y_out, 2)
            dve.sem_inc(core_sum, 1)
            dve.sem_inc(core_var, 1)
            dve.sem_inc(wo_read, 3)
            dve.sem_inc(logit_out, 2)
            dve.sem_inc(logit_ps, 2)
            dve.sem_inc(up_out, 3)
            dve.sem_inc(y_read, 1)
            dve.wait_ge(small_in, 16 * SMALL_LOADS)
            dve.tensor_tensor(bboth[:, :], bproj[:, :], bo[:, :], ALU.add).then_inc(prep, 1)
            dve.wait_ge(prep, 1)

            with dve.Fori(0, TILES // 2) as it:
                for b in range(2):
                    t = it * 2 + b
                    dve.wait_ge(embedded, t + 1)
                    dve.tensor_tensor(hrow[:, b, :], bank[b][:, 0:DIM], bproj[:, :], ALU.add).then_inc(ln1_dve, 1)
                    dve.wait_ge(ln1_dve, t * 2 + 1)
                    dve.bn_stats(stats[:, b, :], hrow[:, b, :]).then_inc(ln1_dve, 1)
                    dve.wait_ge(ln1_dve, t * 2 + 2)
                    dve.tensor_tensor(resid[:, ds(t, 1), :], bank[b][:, 0:DIM].unsqueeze(1), bboth[:, :].unsqueeze(1),
                                      ALU.add).then_inc(emb_read, 1)
                    dve.bn_aggr(mv1[:, b, :], stats[:, b, :]).then_inc(ln1_stat, 1)
                    dve.wait_ge(ln1_act, t * 2 + 2)
                    dve.wait_ge(ln1_stat, t + 1)
                    dve.tensor_scalar(xrow[:, b, :], hrow[:, b, :], mv1[:, b, 0:1], rs1[:, b:b + 1],
                                      ALU.subtract, ALU.mult).then_inc(x1_ready, 1)
            dve.wait_ge(x1T_ready, TILES + 2)
            xv = x1T[0:HALF].rearrange("p h (i t) -> p (h i) t", t=TOKENS_PER_IMAGE)
            dve.tensor_reduce(xp[0:HALF, :, 0:4], xv[:, :, 0:32].rearrange("p i (r t) -> p i r t", t=8), AX.X,
                              ALU.add).then_inc(xp_out, 1)
            dve.tensor_reduce(xp[0:HALF, :, 4:5], xv[:, :, 32:36].unsqueeze(2), AX.X, ALU.add).then_inc(xp_out, 1)

            dve.wait_ge(wbd_in, 32)
            dve.tensor_reduce(wsum[:, :], wbd[:, :, :], AX.X, ALU.add).then_inc(prep, 1)
            dve.wait_ge(prep, 2)
            dve.tensor_scalar(wmean[:, :], wsum[:, :], 1.0 / HEAD_DIM, None, ALU.mult).then_inc(prep, 1)
            dve.wait_ge(prep, 3)
            for a in range(2):
                rows, cols = slice(64 * a, 64 * a + 64), slice(64 * a, 64 * a + 64)
                dve.tensor_tensor(wbd[rows, :, cols], wbd[rows, :, cols],
                                  wmean[rows, :].unsqueeze(2).to_broadcast([64, 2 * STAGES, 64]),
                                  ALU.subtract).then_inc(prep, 1)
            dve.wait_ge(prep, 5)
            dve.tensor_scalar(wbd[:, 0:STAGES, :], wbd[:, 0:STAGES, :], 0.5, None, ALU.mult).then_inc(prep, 1)
            dve.wait_ge(bmean_ready, 1)
            dve.tensor_tensor(bcen[:, :], vecs[:, 0:2 * STAGES], bank[7][:, 0:2 * STAGES],
                              ALU.subtract).then_inc(prep, 1)
            dve.wait_ge(prep, PREP)

            def feature_map(S, dst, c, p):
                dve.wait_ge(S[1], c * PAIRS + p + 1)
                dve.tensor_scalar(gb[:, p % 3, :], gb[:, p % 3, :], 1.0, None, ALU.min).then_inc(S[2], 1)
                dve.wait_ge(S[2], c * PAIRS + p + 1)
                dve.scalar_tensor_tensor(out=dst, in0=bank[p % 3][:, 0:CHUNK], scalar=1.0, in1=gb[:, p % 3, :],
                                         op0=ALU.add, op1=ALU.max).then_inc(S[3], 1)
            with dve.Fori(0, CHUNKS) as c:
                for p in range(PAIRS):
                    feature_map(k_f, gb[:, p % 3, :], c, p)
                    dve.wait_ge(k_f[3], c * PAIRS + p + 4)
                    dve.tensor_tensor(kp1[:, p, ds(c * (CHUNK // 2), CHUNK // 2)], gb[:, p % 3, 0::2],
                                      gb[:, p % 3, 1::2], ALU.add).then_inc(k_f[4], 1)
            for i in range(STAGES):
                buf, n, chunks = KSTAGE[i]
                P = ks[i]

                def f_body(c):
                    for p in range(PAIRS):
                        f_dve(dve, P, i, buf[:, p, ds(c * n, n)], n, c, p)
                    var_dve(dve, P, n, c)
                loop(dve, chunks, f_body)
                r_dve(dve, n * chunks, i)

                def g_body(c):
                    def pool_pair(p):
                        dve.wait_ge(P.g_out, c * PAIRS + p + 4)
                        if i == 0:
                            dve.tensor_tensor(kp2[:, p, ds(c * (n // 2), n // 2)], gb[:, p % 3, 0:n:2],
                                              gb[:, p % 3, 1:n:2], ALU.add).then_inc(P.next_out, 1)
                        elif i == 1:
                            rows = gb[:, p % 3, 0:n].rearrange("p (i r) -> p i r", r=9)
                            dst = kc3[:, p, ds(c * (K3 // 2), K3 // 2)].rearrange("p (i r) -> p i r", r=POOLED)
                            dve.tensor_tensor(dst[:, :, 0:4], rows[:, :, 0:8:2], rows[:, :, 1:8:2],
                                              ALU.add).then_inc(k_main, 1)
                            dve.wait_ge(k_main, c * PAIRS + p + 1)
                            dve.tensor_copy(dst[:, :, 4:5], rows[:, :, 8:9]).then_inc(P.next_out, 1)
                    for p in range(PAIRS):
                        z_dve(dve, P, buf[:, p, ds(c * n, n)], n, c, p)
                        if p and i < 2:
                            pool_pair(p - 1)
                    if i < 2:
                        pool_pair(PAIRS - 1)
                loop(dve, chunks, g_body)
            with dve.Fori(0, CHUNKS) as c:
                for p in range(PAIRS):
                    feature_map(q_f, q_y[:, p, ds(c * CHUNK, CHUNK)], c, p)

            def masked(it, b):
                g = it * 2 + b
                dve.wait_ge(core_s, g + 3)
                dve.tensor_tensor(sm[:, b, :, :], bank[1][:, 0:QUADS * GROUP].rearrange("p (q t) -> p q t", q=QUADS),
                                  mask[:, :].unsqueeze(1).to_broadcast([128, QUADS, GROUP]), ALU.mult).then_inc(core_sm, 1)

            def inverse(it, b):
                g = it * 2 + b
                dve.wait_ge(core_den, g + 1)
                dve.wait_ge(core_rb, g) if not isinstance(g, int) or g > 0 else None
                dve.tensor_scalar(den[:, :], bank[2][0:96, 0:GROUP], DEN_EPS, None, ALU.add).then_inc(core_chain, 1)
                dve.wait_ge(core_chain, g * 6 + 2)
                dve.reciprocal(rden[:, :], den[:, :]).then_inc(core_chain, 1)
                dve.wait_ge(core_chain, g * 6 + 3)
                split_dve(dve, rden, dsplit, GROUP, core_chain, g * 6 + 3).then_inc(core_r, 1)

            def normalised(it, b):
                g = it * 2 + b
                dve.wait_ge(core_rb, g + 1)
                dve.tensor_tensor(sn[:, b, :, :], sm[:, b, :, :],
                                  bank[3][:, 0:QUADS * GROUP].rearrange("p (q t) -> p q t", q=QUADS),
                                  ALU.mult).then_inc(core_sn, 1)

            def y_copy(it, b):
                g = it * 2 + b
                dve.wait_ge(core_sq, g * 2 + 4)
                for q in range(2):
                    dve.tensor_scalar(q_y[:, 3 * q:3 * q + 3, ds(g * GROUP, GROUP)],
                                            bank[4 + q][:, 0:3 * GROUP].rearrange("p (a t) -> p a t", a=3),
                                            bias_of(2 * STAGES - 1), None, ALU.add).then_inc(core_y_out, 1)
                dve.wait_ge(core_sum, g + 2)
                dve.tensor_copy(var[:, ds(g * GROUP, GROUP)], bank[6][0:96, 0:GROUP]).then_inc(core_var, 1)

            def core_step(it, b, last=False):
                normalised(it, b)
                if not last:
                    masked(it + b, 1 - b)
                    inverse(it + b, 1 - b)
                y_copy(it, b)
            masked(0, 0)
            inverse(0, 0)
            with dve.Fori(0, GROUPS // 2 - 1) as it:
                core_step(it, 0)
                core_step(it, 1)
            core_step(GROUPS // 2 - 1, 0)
            core_step(GROUPS // 2 - 1, 1, last=True)
            r_dve(dve, TOKENS, STAGES)
            rows = [hrow[:, 0, :], hrow[:, 1, :], xrow[:, 0, :]]
            for i in range(STAGES):
                G = es[i]
                s = 2 * STAGES - 1 - i

                def z(c, p):
                    z_dve(dve, G, q_y[:, p, ds(c * CHUNK, CHUNK)], CHUNK, c, p)

                def to_sbuf(c, p):
                    f_dve(dve, es[i + 1], s - 1, q_y[:, p, ds(c * CHUNK, CHUNK)], CHUNK, c, p)

                def residual(c):
                    dve.wait_ge(G.next_out, c * PAIRS + PAIRS + 3)
                    for j in range(3):
                        dve.tensor_tensor(rows[j], bank[3 + j][:, 0:DIM],
                                          resid[:, ds(c * 3 + j, 1), :].rearrange("p a d -> p (a d)"),
                                          ALU.add).then_inc(ln2_chain, 1)
                    dve.wait_ge(ln2_chain, c * 9 + 3)
                    for j in range(3):
                        dve.bn_stats(stats[:, j, :], rows[j]).then_inc(ln2_chain, 1)
                    dve.wait_ge(ln2_chain, c * 9 + 6)
                    for j in range(3):
                        dve.tensor_tensor(resid[:, ds(c * 3 + j, 1), :], bank[3 + j][:, 0:DIM].unsqueeze(1),
                                          resid[:, ds(c * 3 + j, 1), :], ALU.add).then_inc(wo_read, 1)

                def aggregate(c):
                    for j in range(3):
                        dve.bn_aggr(mv1[:, j, :], stats[:, j, :]).then_inc(ln2_chain, 1)
                    dve.wait_ge(ln2_chain, c * 9 + 9)
                    for j in range(3):
                        dve.tensor_scalar(mv2[:, ds(c * 3 + j, 1), :], mv1[:, j, :].unsqueeze(1), 1.0, None,
                                          ALU.mult).then_inc(mv_out, 1)

                def gf_body(c, before, more):
                    for p in range(PAIRS):
                        if p + 1 < PAIRS:
                            z(c, p + 1)
                        elif more:
                            z(c + 1, 0)
                        if i < STAGES - 1:
                            if p == 0 and before:
                                to_sbuf(c - 1, PAIRS - 1)
                            if p == 1 and before:
                                var_dve(dve, es[i + 1], CHUNK, c - 1)
                            if p:
                                to_sbuf(c, p - 1)
                        elif before and p == 0:
                            residual(c - 1)
                        elif before and p == 1:
                            aggregate(c - 1)
                z(0, 0)
                chunks_with_ends(dve, gf_body)
                if i < STAGES - 1:
                    to_sbuf(CHUNKS - 1, PAIRS - 1)
                    var_dve(dve, es[i + 1], CHUNK, CHUNKS - 1)
                    r_dve(dve, TOKENS, STAGES + 1 + i)
                else:
                    residual(CHUNKS - 1)
                    aggregate(CHUNKS - 1)
            dve.wait_ge(ln2_r, 1)
            dve.wait_ge(wo_read, TILES + 3)
            def x2(it, b):
                t = it * 2 + b
                for dst in (xrow[:, b, :].unsqueeze(1), x2c[:, ds(t, 1), 0, :]):
                    dve.tensor_scalar(dst, resid[:, ds(t, 1), :], mv2[:, ds(t, 1), 0], rs2[:, ds(t, 1)],
                                      ALU.subtract, ALU.mult).then_inc(x2_out, 1)
                dve.wait_ge(x2_out, t * 3 + 2)
                dve.tensor_tensor(x2c[:, ds(t, 1), 1, :], xrow[:, b, :].unsqueeze(1), x2c[:, ds(t, 1), 0, :],
                                  ALU.subtract).then_inc(x2_out, 1)

            def logits(it, b):
                t = it * 2 + b
                dve.wait_ge(logit_ps, t + 3)
                dve.tensor_copy(rt[:, 0, ds(t * EXPERTS, EXPERTS)], bank[2 + b][:, 0:EXPERTS]).then_inc(logit_out, 1)
            x2(0, 0)
            with dve.Fori(0, TILES // 2 - 1) as it:
                x2(it, 1)
                logits(it, 0)
                x2(it + 1, 0)
                logits(it, 1)
            x2(TILES // 2 - 1, 1)
            logits(TILES // 2 - 1, 0)
            logits(TILES // 2 - 1, 1)
            dve.wait_ge(logit_out, TILES + 2)
            routing()

            def hidden(n, u):
                dve.wait_ge(silu_out, n * UNITS + u + 4)
                dve.tensor_scalar(sup[:, u, :], bank[u][:, UNIT:2 * UNIT], LIMIT * SCALE, -LIMIT * SCALE, ALU.min,
                                  ALU.max).then_inc(up_out, 1)
                dve.wait_ge(up_out, n * UNITS + u + 4)
                dve.wait_ge(hidT_ps, n * UNITS + u - 2) if not isinstance(n, int) or n >= 1 else None
                for dst in (hsplit[:, u, 0, :], hid[:, u, :]):
                    dve.scalar_tensor_tensor(out=dst, in0=sgate[:, u, :], scalar=SILU_LIMIT, in1=sup[:, u, :],
                                             op0=ALU.min, op1=ALU.mult).then_inc(hid_parts, 1)
                dve.wait_ge(hid_parts, (n * UNITS + u) * 2 + 2)
                dve.tensor_tensor(hsplit[:, u, 1, :], hid[:, u, :], hsplit[:, u, 0, :],
                                  ALU.subtract).then_inc(hid_out, 1)

            def finish(n, b, shared, m=None):
                dve.wait_ge(y_ps, (n + 1) * UNITS)
                if shared:
                    dve.scalar_tensor_tensor(out=resid[:, ds(n, 1), :], in0=bank[6][:, 0:DIM].unsqueeze(1),
                                             scalar=1.0 / (SCALE * SCALE), in1=resid[:, ds(n, 1), :], op0=ALU.mult,
                                             op1=ALU.add).then_inc(y_read, 1)
                else:
                    dve.wait_ge(y_stored[b], m * 16) if not isinstance(m, int) or m > 0 else None
                    dve.tensor_copy(orow[:, b, :], bank[6][:, 0:DIM]).then_inc(y_read, 1)

            def tile(n, finish_before=None):
                for u in range(UNITS):
                    hidden(n, u)
                if finish_before is not None:
                    finish_before()
            dve.wait_ge(zeroed, 16 * 6)
            tile(0)
            tile(1, lambda: finish(0, 0, True))
            with dve.Fori(1, TILES // 2) as it:
                for b in range(2):
                    tile(it * 2 + b, lambda: finish(it * 2 + b - 1, 1 - b, True))
            tile(TILES, lambda: finish(TILES - 1, 1, True))
            tile(TILES + 1, lambda: finish(TILES, 0, False, 0))
            tile(TILES + 2, lambda: finish(TILES + 1, 1, False, 0))
            tile(TILES + 3, lambda: finish(TILES + 2, 0, False, 1))
            with dve.Fori(2, ROUTED_TILES // 2) as it:
                n = it * 2 + TILES
                tile(n, lambda: finish(n - 1, 1, False, it - 1))
                tile(n + 1, lambda: finish(n, 0, False, it))
            finish(TILES + ROUTED_TILES - 1, 1, False, ROUTED_TILES // 2 - 1)

            for b in range(2):
                dve.wait_ge(y_stored[b], 16 * (ROUTED_TILES // 2))
            for t in range(TILES):
                b = t % 3
                dve.wait_ge(gathered[b], 32 * (t // 3 + 1))
                if t >= 3:
                    dve.wait_ge(stored[b], 16 * (t // 3))
                dve.scalar_tensor_tensor(out=resid[:, t, :], in0=gath[:, b, 0, :], scalar=small[:, 2, t:t + 1],
                                         in1=resid[:, t, :], op0=ALU.mult, op1=ALU.add).then_inc(comb_step, 1)
                dve.wait_ge(comb_step, t + 1)
                dve.scalar_tensor_tensor(out=orow[:, b, :], in0=gath[:, b, 1, :], scalar=small[:, 3, t:t + 1],
                                         in1=resid[:, t, :], op0=ALU.mult, op1=ALU.add).then_inc(comb, 1)


def kernel(**inputs):
    import numpy as np
    import concourse.bacc as bacc
    from concourse.bass_utils import run_bass_kernel_spmd as run

    a = {k: np.asarray(v) for k, v in inputs.items()}
    P = 16
    x = a["x"].reshape(IMAGES, 3, 6, P, 6, P).transpose(0, 2, 4, 1, 3, 5).reshape(TILES, TILE, PATCH_DIM // 128, 128)

    def halves(w):
        return w.reshape(2, HALF, -1).transpose(1, 0, 2)

    w1 = np.concatenate([a["L0_ffn_w1"], a["L0_ffn_w1s"][None]])
    w3 = np.concatenate([a["L0_ffn_w3"], a["L0_ffn_w3s"][None]])
    w2 = np.concatenate([a["L0_ffn_w2"], a["L0_ffn_w2s"][None]])
    w13 = np.stack([w1.reshape(EXPERTS + 1, 2, HALF, UNITS, UNIT), w3.reshape(EXPERTS + 1, 2, HALF, UNITS, UNIT)], 4)
    vecs = np.concatenate([a["L0_attn_" + k + v] for v in ("_b", "_g", "_be") for k in ("pool", "exp")])
    arrays = {
        "patches": x.transpose(0, 3, 2, 1),
        "wp": a["L0_tok_W_proj"].reshape(DIM, PATCH_DIM // 128, 128).transpose(2, 1, 0),
        "bproj": np.broadcast_to(a["L0_tok_b_proj"], (128, DIM)),
        "bo": np.broadcast_to(a["L0_attn_bo"], (128, DIM)),
        "vecs": np.concatenate([vecs.T, vecs.T]),
        "gbias": np.broadcast_to(a["L0_ffn_gate_bias"], (128, EXPERTS)),
        "gatew": halves(a["L0_ffn_gate_w"]),
        "wq": halves(a["L0_attn_Wq"]),
        "wk": halves(a["L0_attn_Wk"]),
        "wv": halves(a["L0_attn_Wv"]),
        "wo": a["L0_attn_Wo"].reshape(PAIRS, 128, DIM).transpose(1, 0, 2),
        "maps": np.concatenate([a["L0_attn_pool_W"], a["L0_attn_exp_W"]]).transpose(1, 0, 2),
        "w13": w13.transpose(0, 2, 1, 3, 4, 5).reshape(EXPERTS + 1, HALF, W13),
        "w2": w2.reshape(EXPERTS + 1, HIDDEN // 128, 128, DIM).transpose(0, 2, 1, 3).reshape(EXPERTS + 1, 128, W2),
    }
    nc = bacc.Bacc("TRN2", target_bir_lowering=False, num_devices=1)
    arrays = {k: np.ascontiguousarray(v) for k, v in arrays.items()}
    dram = {k: nc.dram_tensor(f"in_{k}", v.shape, F32, kind="ExternalInput").ap() for k, v in arrays.items()}
    dram["slots"] = nc.dram_tensor("slots", (ROUTED_TILES * TILE, 2 * DIM), F16).ap()
    dram["parts"] = nc.dram_tensor("parts", (EXPERTS + 1, 128, 2 * (W13 + W2)), F16).ap()
    dram["expert_out"] = nc.dram_tensor("expert_out", (ROUTED_TILES * TILE, DIM), F32).ap()
    out = nc.dram_tensor("out", (TOKENS, DIM), F32, kind="ExternalOutput").ap()
    build(nc, dram, out)
    r = run(nc, [{f"in_{k}": v for k, v in arrays.items()}], core_ids=[0])
    return r.results[0]["out"].reshape(IMAGES, TOKENS_PER_IMAGE, DIM)
```

```python
from contextlib import ExitStack

import concourse.bass as bass
from concourse import mybir

F32 = mybir.dt.float32
BF16 = mybir.dt.bfloat16
F16 = mybir.dt.float16
I32 = mybir.dt.int32
U32 = mybir.dt.uint32
ALU = mybir.AluOpType
ACT = mybir.ActivationFunctionType
AX = mybir.AxisListType
ds = bass.ds

IMAGES, TOKENS_PER_IMAGE = 64, 36
TOKENS = IMAGES * TOKENS_PER_IMAGE
PATCH_DIM, DIM, HEADS, HEAD_DIM = 768, 192, 12, 64
HALF = DIM // 2
STAGES = 3
PAIRS = HEADS // 2
TILE = 128
TILES = TOKENS // TILE
CHUNK = 384
CHUNKS = TOKENS // CHUNK
HEAD = 2
GROUP_IMAGES = 4
GROUP = GROUP_IMAGES * TOKENS_PER_IMAGE
GROUPS = IMAGES // GROUP_IMAGES
POOLED = 5
GROUP_ROWS = GROUP_IMAGES * POOLED
K1, K2, K3 = TOKENS // 2, TOKENS // 4, IMAGES * POOLED
LN_EPS = 1e-5
DEN_EPS = 1e-6
QUADS = HEADS // 4
EXPERTS, HIDDEN = 8, 768
LIMIT = 10.0
LN_EXP_TABLES = "natural_log_exp_and_others"
SILU_LIMIT = 9.999546021312976
UNITS = 3
UNIT = HIDDEN // UNITS
W13 = 2 * 2 * HIDDEN
W2 = (HIDDEN // 128) * DIM
SCALE = 16.0
STAGE = 512
STAGE2 = 384
C13, C2 = W13 // STAGE, W2 // STAGE2
CHUNKS_W = C13 + C2
SHARED = EXPERTS - 1
ROUTED_TILES = 44
ROW = 2 * DIM + 2
N144 = TILES * EXPERTS


def build(nc, dram, out):
    ctx = ExitStack()
    with ctx:
        def sb(name, shape, dt=F32):
            return ctx.enter_context(nc.sbuf_tensor(name, shape, dt))

        def sem(name):
            return ctx.enter_context(nc.semaphore(name))

        resid = sb("resid", [128, TILES, DIM])
        arena = sb("arena", [128, EXPERTS * (W13 + W2)])
        ARENA_B = 8256 + TILES
        arena_b = sb("arena_b", [128, ARENA_B])
        w13_cols = EXPERTS * W13
        w13_all = arena[:, 0:w13_cols].bitcast(F16)
        w2_all = arena[:, w13_cols:w13_cols + EXPERTS * W2].bitcast(F16)
        PREP, SMALL_LOADS, N_CONST = 7, 5, 51

        def view(base, start, shape):
            n = 1
            for s in shape:
                n *= s
            v = base[:, start:start + n]
            if len(shape) == 1:
                return v
            names = "abc"[:len(shape)]
            return v.rearrange(f"p ({' '.join(names)}) -> p {' '.join(names)}",
                               **{names[i]: shape[i] for i in range(1, len(shape))})

        q_y = view(arena, 0, [PAIRS, TOKENS])
        kp1 = view(arena, 0, [PAIRS, K1])
        kp2 = view(arena, PAIRS * K1, [PAIRS, K2])
        o = PAIRS * TOKENS
        x1T = view(arena, o, [2, TOKENS]); o += 2 * TOKENS
        wo = view(arena, PAIRS * TOKENS, [PAIRS, DIM])
        wq = view(arena, o, [2, HEADS * HEAD_DIM]); o += 2 * HEADS * HEAD_DIM
        wk = view(arena, o, [2, HEADS * HEAD_DIM])
        vw = view(arena, o, [2, PAIRS, 128]); o += 2 * HEADS * HEAD_DIM
        wv = view(arena, o, [2, HEADS * HEAD_DIM])
        vblk = view(arena, o, [2, PAIRS, 128]); o += 2 * HEADS * HEAD_DIM
        patches = view(arena, o, [2, PATCH_DIM // 128, TILE])
        kblk = view(arena, o, [2, PAIRS, 128]); o += 2 * PATCH_DIM
        assert o <= EXPERTS * W13
        o = w13_cols
        var = arena[0:96, o:o + TOKENS]; o += TOKENS
        rstd = arena[0:96, o:o + TOKENS]; o += TOKENS
        rsplit = arena[0:96, o:o + TOKENS // 2].bitcast(BF16); o += TOKENS // 2
        ind = arena[:, o:o + (PAIRS + 1) * 96]; o += (PAIRS + 1) * 96
        wbd = view(arena, o, [2 * STAGES, 128]); o += 2 * STAGES * 128
        kc3_at = w13_cols + EXPERTS * W2 - PAIRS * K3
        assert o <= kc3_at <= w13_cols + (EXPERTS - 1) * W2
        kc3 = view(arena, kc3_at, [PAIRS, K3])
        gath = view(arena, 0, [2, TILES, DIM])
        o = 0
        vcT = view(arena_b, o, [PAIRS, K3]); o += PAIRS * K3
        xp = view(arena_b, o, [2 * IMAGES, POOLED]); o += 2 * IMAGES * POOLED
        sqb = view(arena_b, o, [3, CHUNK]); o += 3 * CHUNK
        zb = view(arena_b, o, [3, CHUNK]); o += 3 * CHUNK
        gb = view(arena_b, o, [3, CHUNK]); o += 3 * CHUNK
        wp = view(arena_b, o, [PATCH_DIM // 128, DIM]); o += (PATCH_DIM // 128) * DIM
        ind_den = arena_b[:, o:o + (QUADS + 1) * 96]; o += (QUADS + 1) * 96
        mask = arena_b[:, o:o + GROUP]; o += GROUP
        den = arena_b[0:96, o:o + GROUP]; o += GROUP
        rden = arena_b[0:96, o:o + GROUP]; o += GROUP
        dsplit = arena_b[0:96, o:o + GROUP // 2].bitcast(BF16); o += GROUP // 2
        sel_den = arena_b[0:96, o:o + QUADS * 64].bitcast(BF16).rearrange("p (q n) -> p q n", q=QUADS)
        o += QUADS * 64
        assert o <= ARENA_B
        sm = view(arena_b, PAIRS * K3 + 2 * IMAGES * POOLED, [2, QUADS, GROUP])
        sn = view(arena_b, PAIRS * K3 + 2 * IMAGES * POOLED + 3 * CHUNK, [2, QUADS, GROUP])
        sq = view(arena_b, PAIRS * K3 + 2 * IMAGES * POOLED + 6 * CHUNK, [PAIRS, GROUP])
        o = 0
        x2rows = arena_b[:, o:o + TILES * ROW // 2].bitcast(F16).rearrange("p (t r) -> p t r", t=TILES)
        row_dest = arena_b[:, o:o + TILES * ROW // 2].bitcast(I32).rearrange("p (t r) -> p t r", t=TILES)[:, :, DIM]
        o += TILES * ROW // 2

        SEGMENTS = ((0, TILE, 0), (TILE, DIM - TILE, 2 * TILE))

        def x2part(t, a, first, n, at):
            return x2rows[:, ds(t, 1), at + a * n:at + (a + 1) * n]
        sgate = view(arena_b, o, [3, UNIT]); o += 3 * UNIT
        sup = view(arena_b, o, [3, UNIT]); o += 3 * UNIT
        hid = view(arena_b, o, [3, UNIT]); o += 3 * UNIT
        PAD = 8
        pad_rows = arena_b[:, o + 3 * UNIT - PAD * ROW // 2:o + 3 * UNIT]
        hsplit = arena_b[:, o:o + 3 * UNIT].bitcast(F16).rearrange("p (u a n) -> p u a n", u=3, a=2)
        o += 3 * UNIT
        rt = view(arena_b, o, [12, N144]); o += 12 * N144
        assert o <= ARENA_B

        vecs = sb("vecs", [128, 6 * STAGES])
        bcen = sb("bcen", [128, 2 * STAGES])
        wsum = sb("wsum", [128, 2 * STAGES])
        wmean = sb("wmean", [128, 2 * STAGES])
        bproj = sb("bproj", [128, DIM])
        bo = sb("bo", [128, DIM])
        bboth = sb("bboth", [128, DIM])
        gbias = sb("gbias", [128, EXPERTS])
        gatew = sb("gatew", [HALF, 2, EXPERTS])
        ident = sb("ident", [128, 128])
        ones = sb("ones", [128, 128])
        upper = sb("upper", [128, 128])
        blk64 = sb("blk64", [128, 128])
        sel = sb("sel", [96, PAIRS, 128], BF16)
        eps = sb("eps", [128, 1])
        hrow = sb("hrow", [128, 2, DIM])
        xrow = sb("xrow", [128, 2, DIM])
        xT = sb("xT", [128, 2, 2, TILE])
        xrow16 = xrow[:, :, :].bitcast(F16)
        xT16 = xT[:, :, :, :].rearrange("p b h t -> p (b h t)").bitcast(F16).rearrange(
            "p (b k t) -> p b k t", b=2, k=4)
        hidT = sb("hidT", [128, 3, 4, 128], F16)
        stage = sb("stage", [128, 3, STAGE])
        scale16 = sb("scale16", [128, 1])
        values = hidT[:, :, :, :].rearrange("p u k t -> p u (k t)")
        rests = stage[:, :, :].rearrange("p b n -> p (b n)").bitcast(F16).rearrange(
            "p (b n) -> p b n", b=3)
        ident16 = sb("ident16", [128, 128], F16)
        stats = sb("stats", [128, 3, 6])
        mv1 = sb("mv1", [128, 3, 2])
        lnv = sb("lnv", [128, 2])
        rs1 = sb("rs1", [128, 2])
        mv2 = sb("mv2", [128, TILES, 2])
        ln2 = sb("ln2", [128, TILES])
        rs2 = sb("rs2", [128, TILES])
        tab = sb("tab", [1, ROUTED_TILES + 1], I32)
        small = sb("small", [128, 12, TILES])
        iota_e = sb("iota_e", [128, N144])
        iota_tok = sb("iota_tok", [128, N144])
        iota_tile = sb("iota_tile", [1, ROUTED_TILES, EXPERTS])
        cmp_tile = sb("cmp_tile", [1, ROUTED_TILES, EXPERTS])
        tile_expert = sb("tile_expert", [1, ROUTED_TILES])
        ecount = sb("ecount", [128, 6, EXPERTS])
        slot = sb("slot", [128, 2, TILES], U32)
        orow = sb("orow", [128, 2, DIM])
        dest = sb("dest", [128, ROUTED_TILES], U32)

        x2_ring = [xrow[:, 0, :], xrow[:, 1, :], hrow[:, 0, :]]
        x2T_ring = [xT[0:HALF, 0, :, :], xT[0:HALF, 1, :, :],
                    orow[0:HALF, :, :].rearrange("p b d -> p (b d)")[:, 0:2 * TILE].rearrange("p (h t) -> p h t", h=2)]

        bank = [ctx.enter_context(nc.psum_tensor(f"bank{i}", [128, 512], F32)) for i in range(8)]
        bank16 = [x[:, :].bitcast(F16) for x in bank]

        consts_set = sem("consts_set")
        small_in = sem("small_in")
        wqkv_in = sem("wqkv_in")
        wbd_in = sem("wbd_in")
        wp_in = sem("wp_in")
        prep = sem("prep")
        bmean_ready = sem("bmean_ready")
        wo_in = sem("wo_in")
        blocks_zero = sem("blocks_zero")
        stage_in = [sem(f"stage_in{b}") for b in range(3)]
        split_in = [sem(f"split_in{b}") for b in range(3)]
        split = sem("split")
        shared_in = sem("shared_in")
        experts_in = sem("experts_in")
        last_in = sem("last_in")
        block = ctx.enter_context(nc.Block())
        PADS = -(-ROUTED_TILES // PAD)
        EARLY = 5
        FIRST = 6

        patch_in = [sem(f"patch_in{b}") for b in range(2)]
        embedded = sem("embedded")
        emb_read = sem("emb_read")
        ln1_dve = sem("ln1_dve")
        ln1_stat = sem("ln1_stat")
        ln1_act = sem("ln1_act")
        x1_ready = sem("x1_ready")
        x1T_ps = sem("x1T_ps")
        x1T_ready = sem("x1T_ready")

        class Pass:
            def __init__(self, name, product=True, consumed=True):
                if product:
                    self.y_ps = sem(f"{name}_y_ps")
                    self.y_sq = sem(f"{name}_y_sq")
                    self.y_out = sem(f"{name}_y_out")
                    self.sums = sem(f"{name}_sums")
                    self.var_out = sem(f"{name}_var_out")
                self.rb_ps = sem(f"{name}_rb_ps")
                self.z_out = sem(f"{name}_z_out")
                self.g_out = sem(f"{name}_g_out")
                if consumed:
                    self.next_out = sem(f"{name}_next_out")

        k_f = sem("k_proj_ps"), sem("k_exp"), sem("k_min"), sem("k_map"), sem("k_pooled")
        q_f = sem("q_proj_ps"), sem("q_exp"), sem("q_min"), sem("q_map")
        ks = [Pass("k0"), Pass("k1"), Pass("k2", consumed=False)]
        es = [Pass("e0", product=False, consumed=False), Pass("e1", consumed=False), Pass("e2")]
        rchain = sem("rchain")
        r_ready = sem("r_ready")
        r_log = sem("r_log")
        r_exp = sem("r_exp")
        k_main = sem("k_main")
        v_ps = sem("v_ps")
        v_out = sem("v_out")
        xp_out = sem("xp_out")

        def bias_of(s):
            return bcen[:, s:s + 1]

        def gain_of(s):
            return vecs[:, 6 + s:7 + s]

        def shift_of(s):
            return vecs[:, 12 + s:13 + s]


        def f_pe(pe, P, src, w, n, c, p, first_wait):
            first_wait()
            pe.wait_ge(P.y_out, c * PAIRS + p + 1)
            pe.wait_ge(P.y_sq, c * PAIRS + p + 1)
            pe.matmul(bank[3 + p % 3][:, 0:n], w, src, start=True, stop=True).then_inc(P.y_ps, 1)

        def s_pe(pe, P, n, c, p):
            pe.wait_ge(P.y_sq, c * PAIRS + p + 4)
            if p == 0:
                pe.wait_ge(P.var_out, c + 1)
            pe.matmul(bank[6][0:96, 0:n], ind[:, 96 * p:96 * p + 96], sqb[:, p % 3, 0:n],
                      start=(p == 0), stop=(p == PAIRS - 1)).then_inc(P.sums, 1)

        def f_act(act, P, s, n, c, p):
            act.wait_ge(P.y_ps, c * PAIRS + p + 1)
            act.wait_ge(P.sums, c * PAIRS + p + 1)
            act.activation(sqb[:, p % 3, 0:n], bank[3 + p % 3][:, 0:n], ACT.Square,
                           bias=bias_of(s)).then_inc(P.y_sq, 1)

        def f_dve(dve, P, s, dst, n, c, p):
            dve.wait_ge(P.y_sq, c * PAIRS + p + 4)
            dve.tensor_scalar(dst, bank[3 + p % 3][:, 0:n], bias_of(s), None,
                              ALU.add).then_inc(P.y_out, 1)

        def var_dve(dve, P, n, c):
            dve.wait_ge(P.sums, c * PAIRS + PAIRS + 3)
            dve.tensor_copy(var[:, ds(c * n, n)], bank[6][0:96, 0:n]).then_inc(P.var_out, 1)

        def r_act(act, var_out, n, parts):
            act.preload_act_table_set(LN_EXP_TABLES)
            for start, end, count in parts:
                act.wait_ge(var_out, count)
                act.activation(var[:, start:end], var[:, start:end], ACT.Ln, bias=eps[0:96, :]).then_inc(r_log, 1)
                n += 1
                act.wait_ge(r_log, n)
                act.activation(rstd[:, start:end], var[:, start:end], ACT.Exp, scale=-0.5).then_inc(r_exp, 1)

        def split_dve(dve, src, dst, length, chain, n):
            dve.tensor_copy(dst[:, 0:length], src[:, 0:length]).then_inc(chain, 1)
            dve.wait_ge(chain, n + 1)
            dve.tensor_tensor(src[:, 0:length], src[:, 0:length], dst[:, 0:length],
                              ALU.subtract).then_inc(chain, 1)
            dve.wait_ge(chain, n + 2)
            dve.tensor_copy(dst[32:64, 0:length], src[32:64, 0:length]).then_inc(chain, 1)
            dve.tensor_copy(dst[64:96, 0:length], src[64:96, 0:length]).then_inc(chain, 1)
            dve.wait_ge(chain, n + 4)
            return dve.tensor_tensor(dst[64:96, 0:length], src[64:96, 0:length], dst[64:96, 0:length],
                                     ALU.subtract)

        def r_dve(dve, length, n):
            dve.wait_ge(r_exp, n + 1)
            split_dve(dve, rstd, rsplit, length, rchain, 4 * n).then_inc(r_ready, 1)

        def r_chunk(dve, i, c):
            n = 4 * (STAGES + i * CHUNKS + c)
            cols = ds(c * CHUNK, CHUNK)
            dve.wait_ge(r_exp, STAGES + 2 * i + (1 if isinstance(c, int) and c < HEAD else 2))
            dve.tensor_scalar(rsplit[:, cols], rstd[:, cols], 1.0, None, ALU.mult).then_inc(rchain, 1)
            dve.wait_ge(rchain, n + 1)
            dve.tensor_tensor(rstd[:, cols], rstd[:, cols], rsplit[:, cols], ALU.subtract).then_inc(rchain, 1)
            dve.wait_ge(rchain, n + 2)
            for rows in (slice(32, 64), slice(64, 96)):
                dve.tensor_scalar(rsplit[rows, cols], rstd[rows, cols], 1.0, None, ALU.mult).then_inc(rchain, 1)
            dve.wait_ge(rchain, n + 4)
            dve.tensor_tensor(rsplit[64:96, cols], rstd[64:96, cols], rsplit[64:96, cols],
                              ALU.subtract).then_inc(r_ready, 1)

        def b_pe(pe, P, n, c, p):
            pe.wait_ge(P.z_out, c * PAIRS + p + 1)
            pe.matmul(bank[p % 3][:, 0:n], sel[:, p, :], rsplit[:, ds(c * n, n)],
                      start=True, stop=True).then_inc(P.rb_ps, 1)

        def z_dve(dve, P, src, n, c, p):
            dve.wait_ge(P.rb_ps, c * PAIRS + p + 1)
            dve.wait_ge(P.g_out, c * PAIRS + p + 1)
            dve.tensor_tensor(zb[:, p % 3, 0:n], src, bank[p % 3][:, 0:n], ALU.mult).then_inc(P.z_out, 1)

        def g_act(act, P, s, n, c, p, consumed=True):
            act.wait_ge(P.z_out, c * PAIRS + p + 4)
            if consumed:
                act.wait_ge(P.next_out, c * PAIRS + p + 1)
            act.activation(gb[:, p % 3, 0:n], zb[:, p % 3, 0:n], ACT.Gelu, bias=shift_of(s),
                           scale=gain_of(s)).then_inc(P.g_out, 1)

        def chunks_with_ends(eng, body):
            body(0, False, True)
            with eng.Fori(1, CHUNKS - 1) as c:
                body(c, True, True)
            body(CHUNKS - 1, True, False)

        KSTAGE = [(kp1, CHUNK, K1 // CHUNK), (kp2, K2 // 2, 2), (kc3, K3, 1)]

        def loop(eng, n, body):
            if n == 1:
                body(0)
            else:
                with eng.Fori(0, n) as c:
                    body(c)

        K_BANKS = (4, 5, 3, 0, 1, 2)

        core_kv = sem("core_kv")
        core_vw = sem("core_vw")
        core_vw_out = sem("core_vw_out")
        core_s = sem("core_s")
        core_sm = sem("core_sm")
        core_den = sem("core_den")
        core_chain = sem("core_chain")
        core_r = sem("core_r")
        core_rb = sem("core_rb")
        core_sn = sem("core_sn")
        core_y = sem("core_y")
        core_sq = sem("core_sq")
        core_y_out = sem("core_y_out")
        core_sum = sem("core_sum")
        core_var = sem("core_var")

        mv_out = sem("mv_out")
        wo_read = sem("wo_read")
        ln2_chain = sem("ln2_chain")
        ln2_log = sem("ln2_log")
        ln2_r = sem("ln2_r")
        x2_out = sem("x2_out")
        x2_values = sem("x2_values")
        x2_rests = sem("x2_rests")
        x2T_ps = sem("x2T_ps")
        x2T_out = sem("x2T_out")
        logit_ps = sem("logit_ps")
        logit_out = sem("logit_out")
        rt_step = sem("rt_step")
        pad_set = sem("pad_set")
        rt_abs = sem("rt_abs")
        rt_act = sem("rt_act")
        rt_sp = sem("rt_sp")
        rt_masks = sem("rt_masks")
        rt_prefix = sem("rt_prefix")
        prefix_read = sem("prefix_read")
        tab_ready = sem("tab_ready")
        slots_ready = sem("slots_ready")
        scattered = sem("scattered")
        zeroed = sem("zeroed")
        row_in = [sem(f"row_in{b}") for b in range(2)]
        row_used = sem("row_used")
        xT_out = sem("xT_out")
        gu_ps = sem("gu_ps")
        silu_out = sem("silu_out")
        up_out = sem("up_out")
        hid_parts = sem("hid_parts")
        hid_out = sem("hid_out")
        hidT_ps = sem("hidT_ps")
        hidT_out = sem("hidT_out")
        y_ps = sem("y_ps")
        y_read = sem("y_read")
        y_stored = [sem(f"y_stored{b}") for b in range(2)]
        dest_in = sem("dest_in")
        returned = [sem(f"returned{c}") for c in range(CHUNKS)]
        comb = sem("comb")
        comb_step = sem("comb_step")
        stored = sem("stored")

        KB = PATCH_DIM // 128

        @block.sync
        def _(sp):
            def load_patch(t, b):
                sp.dma_start(patches[:, b], dram["patches"][ds(t, 1)].rearrange("a p k n -> p (a k) n")
                             ).then_inc(patch_in[b], 16)
            load_patch(0, 0)
            load_patch(1, 1)
            with sp.Fori(0, TILES // 2 - 1) as it:
                for b in range(2):
                    sp.wait_ge(embedded, it * 2 + b + 1)
                    load_patch(it * 2 + 2 + b, b)

            sp.wait_ge(consts_set, N_CONST)
            for a in range(2):
                sp.dma_start(wbd[64 * a:64 * a + 64, :, 64 * a:64 * a + 64], dram["maps"]).then_inc(wbd_in, 16)
            def load_chunk(e, q, after=0):
                b = q % 3
                if q < C13:
                    sp.dma_start(stage[:, b, :], dram["w13"][after:, :, :][ds(e, 1), :, q * STAGE:(q + 1) * STAGE].rearrange(
                        "a p n -> p (a n)")).then_inc(stage_in[b], 16)
                else:
                    r = q - C13
                    sp.dma_start(stage[:, b, 0:STAGE2], dram["w2"][after:, :, :][ds(e, 1), :, r * STAGE2:(r + 1) * STAGE2].rearrange(
                        "a p n -> p (a n)")).then_inc(stage_in[b], 16)

            def store_chunk(e, q):
                b = q % 3
                if q < C13:
                    rows, n, first, rest = 128, STAGE, q * STAGE, W13
                else:
                    rows, n, first, rest = 128, STAGE2, 2 * W13 + (q - C13) * STAGE2, W2
                for part, at in ((values, first), (rests, first + rest)):
                    sp.dma_start(dram["parts"][ds(e, 1), 0:rows, at:at + n].rearrange("a p n -> p (a n)"),
                                 part[0:rows, b, 0:n]).then_inc(split_in[b], 16)

            def weights_to_dram(k0, count, e0):
                for q in range(2):
                    if k0:
                        sp.wait_ge(split_in[q % 3], 32 * (k0 // 3))
                    load_chunk(e0, q)

                def expert(e, more):
                    k = e * CHUNKS_W
                    for q in range(CHUNKS_W):
                        nxt = q + 2
                        if more or nxt < CHUNKS_W:
                            rounds = e * (CHUNKS_W // 3) + nxt // 3
                            if not isinstance(rounds, int) or rounds > 0:
                                sp.wait_ge(split_in[nxt % 3], rounds * 32)
                            load_chunk(e, nxt % CHUNKS_W, nxt // CHUNKS_W)
                        sp.wait_ge(split, (k + q) * 3 + 3)
                        store_chunk(e, q)
                if e0 == 0:
                    expert(0, True)
                with sp.Fori(max(e0, 1), e0 + count - 1) as e:
                    expert(e, True)
                expert(e0 + count - 1, False)
            weights_to_dram(0, FIRST, 0)
            sp.wait_ge(q_f[3], CHUNKS * PAIRS + 3)
            sp.dma_start(wo, dram["wo"]).then_inc(wo_in, 16)
            def load_expert(place, e, what, done):
                if what == "w13":
                    dst, n, rows, first = w13_all, 2 * W13, 128, 0
                else:
                    dst, n, rows, first = w2_all, 2 * W2, 128, 2 * W13
                sp.dma_start(dst[:, ds(place * n, n)], dram["parts"][ds(e, 1), 0:rows, first:first + n].rearrange(
                    "a p n -> p (a n)")).then_inc(done, 16)

            weights_to_dram(FIRST * CHUNKS_W, EXPERTS + 1 - FIRST, FIRST)
            sp.wait_ge(core_y_out, 2 * GROUPS + 2)
            for b in range(3):
                sp.wait_ge(split_in[b], 32 * (EXPERTS + 1) * CHUNKS_W // 3)
            load_expert(SHARED, EXPERTS, "w13", shared_in)
            load_expert(SHARED, EXPERTS, "w2", shared_in)
            for e in range(EARLY, SHARED):
                load_expert(e, e, "w13", experts_in)
            sp.wait_ge(wo_read, TILES + 3)
            with sp.Fori(0, EARLY) as e:
                load_expert(e, e, "w13", experts_in)
            with sp.Fori(0, SHARED) as e:
                load_expert(e, e, "w2", experts_in)

            def load_row(m, b):
                sp.dma_start(xrow16[:, b, :], dram["slots"][ds(m * TILE, TILE), 0:2 * DIM]).then_inc(row_in[b], 16)

            sp.wait_ge(x2T_ps, TILES)
            sp.wait_ge(scattered, 16 * 2 * TILES)
            for b in range(2):
                load_row(b, b)
            sp.dma_start(dest[:, :].bitcast(F16).rearrange("p (m w) -> p m w", w=2),
                         dram["slots"][:, 2 * DIM:ROW].rearrange("(m p) w -> p m w", p=TILE)).then_inc(dest_in, 16)
            with sp.Fori(0, ROUTED_TILES // 2 - 1) as it:
                for b in range(2):
                    sp.wait_ge(row_used, it * 2 + b + 1 + TILES)
                    load_row(it * 2 + 2 + b, b)
            for b in range(2):
                sp.wait_ge(y_stored[b], 16 * (ROUTED_TILES // 2))
            for c in range(CHUNKS):
                for k in range(2):
                    first = k * TOKENS + c * CHUNK
                    sp.dma_start(gath[:, k, c * 3:c * 3 + 3, :], dram["expert_out"][first:first + CHUNK, :].rearrange(
                        "(t p) d -> p t d", p=TILE)).then_inc(returned[c], 16)

        @block.gpsimd
        def _(pool):
            n_const = [0]

            def const(ins):
                ins.then_inc(consts_set, 1)
                n_const[0] += 1
                pool.wait_ge(consts_set, n_const[0])

            const(pool.memset(eps[:, :], LN_EPS))
            const(pool.memset(ident[:, :], 0.0))
            const(pool.affine_select(out=ident[:, :], in_=ident[:, :], compare_op=ALU.not_equal, fill=1.0,
                                     base=0, pattern=[[-1, 128]], channel_multiplier=1))
            const(pool.memset(ones[:, :], 1.0))
            const(pool.memset(blk64[:, :], 0.0))
            const(pool.memset(scale16[:, :], SCALE))
            const(pool.memset(wbd[:, :, :], 0.0))
            const(pool.memset(ind[:, :], 0.0))
            const(pool.memset(ind_den[:, :], 0.0))
            const(pool.memset(sel[:, :, :], 0.0))
            const(pool.memset(sel_den[:, :, :], 0.0))
            const(pool.memset(mask[:, :], float(POOLED) ** -0.5))
            const(pool.tensor_copy(ident16[:, :], ident[:, :]))
            const(pool.affine_select(out=upper[:, :], in_=ones[:, :], compare_op=ALU.is_ge, fill=0.0,
                                     base=-1, pattern=[[1, 128]], channel_multiplier=-1))
            for a in range(2):
                rows = slice(64 * a, 64 * a + 64)
                const(pool.memset(blk64[rows, 64 * a:64 * a + 64], 1.0 / HEAD_DIM))
                for r in range(3):
                    first = 32 * r + a
                    const(pool.memset(ind[rows, first:first + 98 * (PAIRS - 1) + 1:98], 1.0 / HEAD_DIM))
            for j in range(4):
                for r in range(3):
                    first = 32 * r + j
                    const(pool.memset(ind_den[32 * j:32 * j + 32, first:first + 100 * (QUADS - 1) + 1:100], 1.0))
            for r in range(3):
                rows = slice(32 * r, 32 * r + 32)
                v = sel[rows, :, :].rearrange("k p (h j) -> k p h j", h=2)
                const(pool.affine_select(out=v, in_=v, compare_op=ALU.not_equal, fill=1.0, base=0,
                                         pattern=[[-2, PAIRS], [-1, 2], [0, 64]], channel_multiplier=1))
                v = sel_den[rows, :, :].rearrange("k q (h j) -> k q h j", h=4)
                const(pool.affine_select(out=v, in_=v, compare_op=ALU.not_equal, fill=1.0, base=0,
                                         pattern=[[-4, QUADS], [-1, 4], [0, 32]], channel_multiplier=1))
            for j in range(4):
                m = mask[32 * j:32 * j + 32, :].rearrange("k (i t) -> k i t", i=GROUP_IMAGES)
                const(pool.affine_select(out=m, in_=m, compare_op=ALU.is_ge, fill=0.0, base=0,
                                         pattern=[[-POOLED, GROUP_IMAGES], [0, TOKENS_PER_IMAGE]], channel_multiplier=1))
            for j in range(4):
                m = mask[32 * j:32 * j + 32, :].rearrange("k (i t) -> k i t", i=GROUP_IMAGES)
                const(pool.affine_select(out=m, in_=m, compare_op=ALU.is_ge, fill=0.0, base=POOLED - 1,
                                         pattern=[[POOLED, GROUP_IMAGES], [0, TOKENS_PER_IMAGE]], channel_multiplier=-1))
            const(pool.iota(iota_e[:, :], [[0, TILES], [1, EXPERTS]], base=0, channel_multiplier=0,
                            allow_small_or_imprecise_dtypes=True))
            const(pool.iota(iota_tok[:, :], [[0, EXPERTS], [TILE, TILES]], base=0, channel_multiplier=0,
                            allow_small_or_imprecise_dtypes=True))
            const(pool.iota(iota_tile[:, :, :], [[1, ROUTED_TILES], [0, EXPERTS]], base=0, channel_multiplier=0,
                            allow_small_or_imprecise_dtypes=True))
            assert n_const[0] == N_CONST, n_const[0]

            def split_experts(e0, count):
                def expert(e):
                    for q in range(CHUNKS_W):
                        b, k = q % 3, e * CHUNKS_W + q
                        rows, n = 128, STAGE if q < C13 else STAGE2
                        if not isinstance(k, int) or k > 0:
                            pool.wait_ge(split, k * 3)
                        pool.wait_ge(stage_in[b], (e * (CHUNKS_W // 3) + q // 3) * 16 + 16)
                        src = stage[0:rows, b, 0:n]
                        scale = scale16[0:rows, 0:1].to_broadcast([rows, n])
                        pool.tensor_tensor(values[0:rows, b, 0:n], src, scale, ALU.mult).then_inc(split, 1)
                        pool.wait_ge(split, k * 3 + 1)
                        pool.tensor_tensor(src, src, scale, ALU.mult).then_inc(split, 1)
                        pool.wait_ge(split, k * 3 + 2)
                        pool.tensor_tensor(rests[0:rows, b, 0:n], src, values[0:rows, b, 0:n],
                                           ALU.subtract).then_inc(split, 1)
                if e0 == 0:
                    expert(0)
                with pool.Fori(max(e0, 1), e0 + count) as e:
                    expert(e)
            split_experts(0, FIRST)
            pool.wait_ge(v_out, PAIRS)
            for blocks in (kblk, vblk, vw):
                pool.memset(blocks, 0.0).then_inc(blocks_zero, 1)
            pool.wait_ge(blocks_zero, 3)
            pool.wait_ge(ks[2].g_out, PAIRS + 3)
            with pool.Fori(0, GROUPS // 2) as it:
                for b in range(2):
                    g = it * 2 + b
                    pool.wait_ge(core_vw, g + 1)
                    for src, dst in ((kc3, kblk), (vcT, vblk)):
                        for odd in range(2):
                            for a in range(2):
                                rows = slice(64 * a, 64 * a + 64)
                                first = 64 * odd + 32 * a
                                pool.tensor_copy(
                                    dst[rows, b, odd::2, first:first + GROUP_ROWS],
                                    src[rows, odd::2, ds(g * GROUP_ROWS, GROUP_ROWS)]).then_inc(core_kv, 1)
            pool.wait_ge(core_kv, 8 * GROUPS)
            split_experts(FIRST, EXPERTS + 1 - FIRST)
            pool.wait_ge(wo_read, TILES + 3)
            pool.memset(pad_rows, 0.0).then_inc(pad_set, 1)
            pool.wait_ge(pad_set, 1)
            pool.iota(pad_rows.bitcast(I32).rearrange("p (a r) -> p a r", a=PAD)[:, :, DIM], [[0, PAD]],
                      base=2 * TOKENS, channel_multiplier=1).then_inc(pad_set, 1)
            pool.wait_ge(pad_set, 2)
            for m in range(0, ROUTED_TILES, PAD):
                n = min(PAD, ROUTED_TILES - m)
                pool.dma_start(dram["slots"][m * TILE:(m + n) * TILE, :].rearrange("(a p) r -> p a r", p=128),
                               pad_rows.bitcast(F16).rearrange("p (a r) -> p a r", a=PAD)[:, 0:n, :]).then_inc(zeroed, 16)
            pool.wait_ge(zeroed, 16 * PADS)
            for k in range(2):
                pool.iota(row_dest, [[TILE, TILES]], base=k * TOKENS, channel_multiplier=1).then_inc(pad_set, 1)
                pool.wait_ge(pad_set, 3 + k)
                pool.wait_ge(slots_ready, 1)
                for t in range(TILES):
                    pool.indirect_dma_start(dram["slots"][:, :], bass.IndirectOffsetOnAxis(slot[:, k, t:t + 1], 0),
                                            x2rows[:, t, :], None).then_inc(scattered, 16)
                pool.wait_ge(scattered, 16 * TILES * (k + 1))
            pool.wait_ge(y_ps, TILES * UNITS)
            for dst, rows, first, n in ((w13_all, 128, 0, 2 * W13), (w2_all, 128, 2 * W13, 2 * W2)):
                pool.dma_start(dst[:, SHARED * n:(SHARED + 1) * n],
                               dram["parts"][SHARED, 0:rows, first:first + n]).then_inc(last_in, 16)
            pool.wait_ge(dest_in, 16)
            for m in range(ROUTED_TILES):
                pool.wait_ge(y_read, m + TILES + 2)
                if m:
                    pool.wait_ge(y_stored[(m - 1) % 2], 16 * ((m + 1) // 2))
                pool.indirect_dma_start(dram["expert_out"][:, :], bass.IndirectOffsetOnAxis(dest[:, m:m + 1], 0),
                                        orow[:, m % 2, :], None).then_inc(y_stored[m % 2], 16)

        @block.tensor
        def _(pe):
            pe.wait_ge(wp_in, 16)
            def embed(it, b):
                t = it * 2 + b
                pe.wait_ge(patch_in[b], (it + 1) * 16)
                pe.wait_ge(emb_read, t + 1)
                for k in range(KB):
                    mm = pe.matmul(bank[b][:, 0:DIM], patches[:, b, k, :], wp[:, k, :],
                                   start=(k == 0), stop=(k == KB - 1))
                mm.then_inc(embedded, 1)

            def turn_x1(it, b):
                t = it * 2 + b
                pe.wait_ge(x1_ready, t + 1)
                pe.wait_ge(x1T_ready, t + 1)
                for h in range(2):
                    mm = pe.transpose(bank[2 + b][0:HALF, h * TILE:(h + 1) * TILE],
                                      xrow[:, b, h * HALF:(h + 1) * HALF], ident[:, :])
                mm.then_inc(x1T_ps, 1)

            embed(0, 0)
            pe.wait_ge(consts_set, 3)
            with pe.Fori(0, TILES // 2 - 1) as it:
                embed(it, 1)
                turn_x1(it, 0)
                embed(it + 1, 0)
                turn_x1(it, 1)
            embed(TILES // 2 - 1, 1)
            turn_x1(TILES // 2 - 1, 0)

            def project(w, ps_sem, to, c, p):
                for h in range(2):
                    mm = pe.matmul(bank[to][:, 0:CHUNK], w[0:HALF, h, p * 128:(p + 1) * 128],
                                   x1T[0:HALF, h, ds(c * CHUNK, CHUNK)], start=(h == 0), stop=(h == 1))
                mm.then_inc(ps_sem, 1)
            pe.wait_ge(wqkv_in, 48)
            pe.wait_ge(x1T_ready, CHUNK // TILE + 2)
            for p in range(2):
                project(wk, k_f[0], K_BANKS[p], 0, p)
            turn_x1(TILES // 2 - 1, 1)
            pe.wait_ge(consts_set, N_CONST)
            pe.wait_ge(small_in, 16 * SMALL_LOADS)
            pe.matmul(bank[7][:, 0:2 * STAGES], blk64[:, :], vecs[:, 0:2 * STAGES], start=True,
                      stop=True).then_inc(bmean_ready, 1)
            pe.wait_ge(x1T_ready, TILES + 2)
            pe.wait_ge(emb_read, TILES + 2)
            for p in range(2, PAIRS):
                project(wk, k_f[0], K_BANKS[p], 0, p)
            with pe.Fori(1, CHUNKS) as c:
                for p in range(PAIRS):
                    pe.wait_ge(k_f[3], (c - 1) * PAIRS + p + 4)
                    project(wk, k_f[0], K_BANKS[p], c, p)
            def pooled_values():
                pe.wait_ge(ks[0].y_out, 3 + KSTAGE[0][2] * PAIRS)
                pe.wait_ge(xp_out, 4)
                xpf = xp.rearrange("p (h i) r -> p h (i r)", h=2)
                for p in range(PAIRS):
                    if p >= 2:
                        pe.wait_ge(v_out, p - 1)
                    for h in range(2):
                        mm = pe.matmul(bank[4 + p % 2][:, 0:K3], wv[0:HALF, h, p * 128:(p + 1) * 128],
                                       xpf[0:HALF, h, :], start=(h == 0), stop=(h == 1))
                    mm.then_inc(v_ps, 1)
            pe.wait_ge(prep, PREP)
            for i in range(STAGES):
                buf, n, chunks = KSTAGE[i]
                if i == 0:
                    pe.wait_ge(k_f[3], (CHUNKS - 1) * PAIRS + 3 + 3)
                if i == 1:
                    pe.wait_ge(v_out, PAIRS)

                def f_body(c):
                    if i == 0:
                        pe.wait_ge(k_f[4], (c + 1) * 2 * PAIRS + 3)
                    elif i == 1:
                        pe.wait_ge(ks[0].next_out, c * PAIRS + 2 * PAIRS + 3)
                    else:
                        pe.wait_ge(ks[1].next_out, 2 * PAIRS + 3)
                    for p in range(PAIRS):
                        f_pe(pe, ks[i], buf[:, p, ds(c * n, n)], wbd[:, i, :], n, c, p, lambda: None)
                        if p:
                            s_pe(pe, ks[i], n, c, p - 1)
                    s_pe(pe, ks[i], n, c, PAIRS - 1)
                loop(pe, chunks, f_body)
                if i == 0:
                    pooled_values()
                pe.wait_ge(r_ready, i + 1)

                def g_body(c):
                    for p in range(PAIRS):
                        b_pe(pe, ks[i], n, c, p)
                loop(pe, chunks, g_body)
            pe.wait_ge(ks[2].z_out, 3 + PAIRS)
            with pe.Fori(0, CHUNKS) as c:
                for p in range(PAIRS):
                    pe.wait_ge(q_f[3], c * PAIRS + p + 1)
                    project(wq, q_f[0], p % 3, c, p)
            pe.wait_ge(q_f[3], 3 + CHUNKS * PAIRS)

            def core_a(it, b):
                g = it * 2 + b
                pe.wait_ge(core_kv, (g + 1) * 8)
                pe.wait_ge(core_sm, g + 1)
                for p in range(PAIRS):
                    mm = pe.matmul(bank[1][:, (p // 2) * GROUP:(p // 2 + 1) * GROUP], kblk[:, b, p, :],
                                   q_y[:, p, ds(g * GROUP, GROUP)], start=(p % 2 == 0), stop=(p % 2 == 1))
                mm.then_inc(core_s, 1)

            def core_v(it, b):
                g = it * 2 + b
                pe.wait_ge(core_vw_out, g * 2 + 2)
                for p in range(PAIRS):
                    mm = pe.matmul(bank[0][:, (p // 2) * 128:(p // 2) * 128 + 128], vblk[:, b, p, :],
                                   wbd[:, 2 * STAGES - 1, :], start=(p % 2 == 0), stop=(p % 2 == 1))
                mm.then_inc(core_vw, 1)

            def core_d(it, b):
                g = it * 2 + b
                pe.wait_ge(core_sm, g + 2)
                pe.wait_ge(core_chain, g * 6 + 1)
                for q in range(QUADS):
                    mm = pe.matmul(bank[2][0:96, 0:GROUP], ind_den[:, 96 * q:96 * q + 96], sm[:, b, q, :],
                                   start=(q == 0), stop=(q == QUADS - 1))
                mm.then_inc(core_den, 1)

            def core_b(it, b):
                g = it * 2 + b
                pe.wait_ge(core_r, g + 1)
                pe.wait_ge(core_sn, g + 1)
                for q in range(QUADS):
                    mm = pe.matmul(bank[3][:, q * GROUP:(q + 1) * GROUP], sel_den[:, q, :], dsplit[:, :],
                                   start=True, stop=True)
                mm.then_inc(core_rb, 1)

            def core_yy(it, b):
                g = it * 2 + b
                pe.wait_ge(core_sn, g + 2)
                pe.wait_ge(core_vw_out, g * 2 + 4)
                pe.wait_ge(core_y_out, g * 2 + 2)
                pe.wait_ge(core_sq, g * 2 + 2)
                for p in range(PAIRS):
                    mm = pe.matmul(bank[4 + p // 3][:, (p % 3) * GROUP:(p % 3 + 1) * GROUP],
                                   vw[:, b, p, :], sn[:, b, p // 2, :], start=True, stop=True)
                mm.then_inc(core_y, 1)

            def core_st(it, b):
                g = it * 2 + b
                pe.wait_ge(core_sq, g * 2 + 4)
                pe.wait_ge(core_var, g + 1)
                for p in range(PAIRS):
                    mm = pe.matmul(bank[6][0:96, 0:GROUP], ind[:, 96 * p:96 * p + 96], sq[:, p, :],
                                   start=(p == 0), stop=(p == PAIRS - 1))
                mm.then_inc(core_sum, 1)

            def core_step(it, b, last=False):
                core_b(it, b)
                if not last:
                    core_a(it + b, 1 - b)
                core_yy(it, b)
                if not last:
                    core_d(it + b, 1 - b)
                    core_v(it + b, 1 - b)
                core_st(it, b)
            core_a(0, 0)
            core_d(0, 0)
            core_v(0, 0)
            with pe.Fori(0, GROUPS // 2 - 1) as it:
                core_step(it, 0)
                core_step(it, 1)
            core_step(GROUPS // 2 - 1, 0)
            core_step(GROUPS // 2 - 1, 1, last=True)

            for i in range(STAGES - 1):
                G, Fn = es[i], es[i + 1]
                pe.wait_ge(r_ready, STAGES + i * CHUNKS + 1)

                def gf_body(c, before, more):
                    for p in range(PAIRS):
                        if p + 2 < PAIRS:
                            b_pe(pe, G, CHUNK, c, p + 2)
                        elif more:
                            if p + 2 == PAIRS:
                                pe.wait_ge(r_ready, STAGES + i * CHUNKS + c + 2)
                            b_pe(pe, G, CHUNK, c + 1, p + 2 - PAIRS)
                        f_pe(pe, Fn, gb[:, p % 3, :], wbd[:, 2 * STAGES - 2 - i, :], CHUNK, c, p,
                             lambda: pe.wait_ge(G.g_out, c * PAIRS + p + 4))
                        if p:
                            s_pe(pe, Fn, CHUNK, c, p - 1)
                        elif before:
                            s_pe(pe, Fn, CHUNK, c - 1, PAIRS - 1)
                b_pe(pe, G, CHUNK, 0, 0)
                b_pe(pe, G, CHUNK, 0, 1)
                chunks_with_ends(pe, gf_body)
                s_pe(pe, Fn, CHUNK, CHUNKS - 1, PAIRS - 1)
            pe.wait_ge(r_ready, STAGES + (STAGES - 1) * CHUNKS + 1)
            G = es[2]
            pe.wait_ge(wo_in, 16)
            pe.wait_ge(G.y_out, 3 + CHUNKS * PAIRS)

            def go_body(c, more):
                for p in range(PAIRS):
                    if p + 2 < PAIRS:
                        b_pe(pe, G, CHUNK, c, p + 2)
                    elif more:
                        if p + 2 == PAIRS:
                            pe.wait_ge(r_ready, STAGES + (STAGES - 1) * CHUNKS + c + 2)
                        b_pe(pe, G, CHUNK, c + 1, p + 2 - PAIRS)
                    pe.wait_ge(G.g_out, c * PAIRS + p + 4)
                    for j in range(3):
                        if p == 0:
                            pe.wait_ge(wo_read, c * 3 + j + 1)
                        mm = pe.matmul(bank[3 + j][:, 0:DIM], gb[:, p % 3, j * TILE:(j + 1) * TILE], wo[:, p, :],
                                       start=(p == 0), stop=(p == PAIRS - 1))
                    mm.then_inc(G.next_out, 1)
            b_pe(pe, G, CHUNK, 0, 0)
            b_pe(pe, G, CHUNK, 0, 1)
            with pe.Fori(0, CHUNKS - 1) as c:
                go_body(c, True)
            go_body(CHUNKS - 1, False)

            pe.wait_ge(G.z_out, 3 + CHUNKS * PAIRS)
            pe.wait_ge(wo_read, 3 + TILES)
            def turn_x2(t, j):
                pe.wait_ge(x2_out, t + 1)
                pe.wait_ge(x2T_out, t + 1)
                for h in range(2):
                    mm = pe.transpose(bank[j][0:HALF, h * TILE:(h + 1) * TILE],
                                      x2_ring[j][:, h * HALF:(h + 1) * HALF], ident[:, :])
                mm.then_inc(x2T_ps, 1)

            def logits_pe(c, before, more):
                for j in range(3):
                    t = c * 3 + j
                    if more or j < 2:
                        turn_x2(t + 1, (j + 1) % 3)
                    pe.wait_ge(x2T_out, t + 4)
                    pe.wait_ge(logit_out, t + 1)
                    for h in range(2):
                        mm = pe.matmul(bank[3 + j][:, 0:EXPERTS], x2T_ring[j][:, h, :], gatew[:, h, :],
                                       start=(h == 0), stop=(h == 1))
                    mm.then_inc(logit_ps, 1)
            turn_x2(0, 0)
            chunks_with_ends(pe, logits_pe)
            pe.wait_ge(rt_masks, 1)
            pe.matmul(bank[0][:, 0:N144], upper[:, :], rt[:, 7, :], start=True, stop=True)
            pe.matmul(bank[1][:, 0:N144], ones[:, :], rt[:, 7, :], start=True, stop=True).then_inc(rt_prefix, 1)

            def turn_row(rows):
                for k in range(3):
                    mm = pe.transpose(bank16[7][:, k * TILE:(k + 1) * TILE], rows[:, k * TILE:(k + 1) * TILE],
                                      ident16[:, :])
                mm.then_inc(row_used, 1)

            def turn_shared(n):
                turn_row(x2rows[:, ds(n, 1), :].rearrange("p t r -> p (t r)"))

            def turn_routed(b, k):
                pe.wait_ge(row_in[b], k * 16)
                turn_row(xrow16[:, b, :])

            def gate_up(n, b, u, e):
                if u == 0:
                    pe.wait_ge(xT_out, n + 1)
                pe.wait_ge(up_out, n * UNITS + u + 1)
                parts = ((0, 0, 0), (1, 0, 0), (0, 0, 1), (2, 1, 0), (2, 1, 1))
                for k, h, w in parts:
                    mm = pe.matmul(bank[u][:, :], xT16[:, b, k, :],
                                   w13_all[:, ds(e * 2 * W13 + w * W13 + h * 2 * HIDDEN + u * 512, 512)],
                                   start=(k, h, w) == parts[0], stop=(k, h, w) == parts[-1])
                mm.then_inc(gu_ps, 1)

            def turn_hid(n, u):
                pe.wait_ge(hid_out, n * UNITS + u + 1)
                pe.wait_ge(hidT_out, n * UNITS + u + 1)
                for k in range(4):
                    mm = pe.transpose(bank16[3 + u][:, k * 128:(k + 1) * 128],
                                      hsplit[:, u, k // 2, (k % 2) * 128:(k % 2 + 1) * 128], ident16[:, :])
                mm.then_inc(hidT_ps, 1)

            def down(n, u, e):
                pe.wait_ge(hidT_out, n * UNITS + u + 4)
                if u == 0:
                    pe.wait_ge(y_read, n + 1)
                for x, w in ((0, 0), (0, 1), (1, 0)):
                    for j in range(2):
                        mm = pe.matmul(bank[6][:, 0:DIM], hidT[:, u, 2 * x + j, :],
                                       w2_all[:, ds(e * 2 * W2 + w * W2 + (2 * u + j) * DIM, DIM)],
                                       start=(u == 0 and x + w + j == 0),
                                       stop=(u == UNITS - 1 and x == 1 and j == 1))
                mm.then_inc(y_ps, 1)

            def tile(n, b, e, before, turn_next, load_next=None):
                for u in range(UNITS):
                    gate_up(n, b, u, e)
                    if callable(before):
                        before = before()
                    if u == 1 and load_next is not None:
                        load_next()
                    if u == 0 and turn_next is not None:
                        turn_next()
                    if u == 2:
                        turn_hid(n, 0)
                    elif before is not None:
                        turn_hid(n - 1, u + 1)
                    if before is not None:
                        down(n - 1, u, before)

            pe.wait_ge(shared_in, 32)
            pe.wait_ge(prefix_read, 1)
            turn_shared(0)
            tile(0, 0, SHARED, None, lambda: turn_shared(1))
            tile(1, 1, SHARED, SHARED, lambda: turn_shared(2))
            with pe.Fori(1, TILES // 2 - 1) as it:
                for b in range(2):
                    n = it * 2 + b
                    tile(n, b, SHARED, SHARED, lambda: turn_shared(n + 1))
            tile(TILES - 2, 0, SHARED, SHARED, lambda: turn_shared(TILES - 1))
            tile(TILES - 1, 1, SHARED, SHARED, lambda: turn_routed(0, 1))
            pe.wait_ge(tab_ready, 1)
            pe.wait_ge(experts_in, 16 * 2 * SHARED)

            def expert_of(j):
                return pe.value_load(tab[0:1, ds(j, 1)], min_val=0, max_val=EXPERTS - 1)
            first = expert_of(1)
            tile(TILES, 0, first, SHARED, lambda: turn_routed(1, 1))
            tile(TILES + 1, 1, expert_of(2), first, lambda: turn_routed(0, 2))
            pe.wait_ge(last_in, 32)
            assert ROUTED_TILES % 4 == 0
            with pe.Fori(0, ROUTED_TILES // 4 - 1) as it:
                m = it * 4 + 2
                e = [expert_of(m + 1)]
                for i in range(4):
                    tile(m + TILES + i, i % 2, e[i], e[i - 1] if i else lambda: expert_of(m),
                         lambda: turn_routed(1 - i % 2, it * 2 + 2 + (i + 1) // 2),
                         (lambda: e.append(expert_of(m + 2 + i))) if i < 3 else None)
            n = TILES + ROUTED_TILES - 2
            e0, e1 = expert_of(ROUTED_TILES - 1), expert_of(ROUTED_TILES)
            tile(n, 0, e0, expert_of(ROUTED_TILES - 2), lambda: turn_routed(1, ROUTED_TILES // 2))
            tile(n + 1, 1, e1, e0, None)
            turn_hid(n + 1, 1)
            down(n + 1, 0, e1)
            turn_hid(n + 1, 2)
            down(n + 1, 1, e1)
            down(n + 1, 2, e1)

        @block.scalar
        def _(act):
            act.dma_start(wp, dram["wp"]).then_inc(wp_in, 16)
            for dst, name in ((bproj, "bproj"), (bo, "bo"), (vecs, "vecs"), (gbias, "gbias")):
                act.dma_start(dst[:, :], dram[name]).then_inc(small_in, 16)
            act.dma_start(gatew[:, :, :], dram["gatew"]).then_inc(small_in, 16)
            act.dma_start(wv[0:HALF], dram["wv"]).then_inc(wqkv_in, 16)
            act.dma_start(wk[0:HALF], dram["wk"]).then_inc(wqkv_in, 16)
            act.dma_start(wq[0:HALF], dram["wq"]).then_inc(wqkv_in, 16)
            act.wait_ge(consts_set, 1)
            act.sem_inc(x1T_ready, 2)
            act.sem_inc(core_vw_out, 2)
            act.sem_inc(core_sq, 2)
            for P in ks + es[1:]:
                act.sem_inc(P.y_sq, 3)
            for P in ks + es:
                act.sem_inc(P.g_out, 3)
            act.sem_inc(x2T_out, 3)
            act.sem_inc(hidT_out, 3)
            act.sem_inc(silu_out, 3)

            act.preload_act_table_set(LN_EXP_TABLES)

            def norm1(t, b):
                act.wait_ge(ln1_stat, t + 1)
                act.activation(lnv[:, b:b + 1], mv1[:, b, 1:2], ACT.Ln, bias=eps[:, :]).then_inc(ln1_act, 1)
                act.wait_ge(ln1_act, t * 2 + 1)
                act.activation(rs1[:, b:b + 1], lnv[:, b:b + 1], ACT.Exp, scale=-0.5).then_inc(ln1_act, 1)

            with act.Fori(0, TILES // 2) as it:
                for b in range(2):
                    t = it * 2 + b
                    norm1(t, b)
                    act.wait_ge(x1T_ps, t + 1)
                    act.activation(x1T[0:HALF, :, ds(t * TILE, TILE)],
                                   bank[2 + b][0:HALF, 0:2 * TILE].rearrange("p (h t) -> p h t", h=2),
                                   ACT.Copy).then_inc(x1T_ready, 1)
            def exp_unit(S, used, src, c, p):
                act.wait_ge(S[0], c * PAIRS + p + 1)
                act.wait_ge(used, c * PAIRS + p + 1)
                act.activation(gb[:, p % 3, :], bank[src][:, 0:CHUNK], ACT.Exp).then_inc(S[1], 1)
            with act.Fori(0, CHUNKS) as c:
                for p in range(PAIRS):
                    exp_unit(k_f, k_f[4], K_BANKS[p], c, p)
            for i in range(STAGES):
                buf, n, chunks = KSTAGE[i]
                act.wait_ge(prep, PREP)
                act.preload_act_table(ACT.Gelu)

                def f_body(c):
                    for p in range(PAIRS):
                        f_act(act, ks[i], i, n, c, p)
                loop(act, chunks, f_body)
                r_act(act, ks[i].var_out, i, ((0, n * chunks, chunks + 1),))
                if i == 0:
                    for p in range(PAIRS):
                        act.wait_ge(v_ps, p + 1)
                        act.activation(vcT[:, p, :], bank[4 + p % 2][:, 0:K3], ACT.Copy, scale=1.0 / 8).then_inc(v_out, 1)
                act.preload_act_table(ACT.Gelu)

                def g_body(c):
                    for p in range(PAIRS):
                        if i < 2:
                            g_act(act, ks[i], i, n, c, p)
                        else:
                            act.wait_ge(ks[i].z_out, c * PAIRS + p + 4)
                            act.activation(kc3[:, p, :], zb[:, p % 3, 0:n], ACT.Gelu, bias=shift_of(i),
                                           scale=gain_of(i)).then_inc(ks[i].g_out, 1)
                loop(act, chunks, g_body)
            act.preload_act_table(ACT.Exp)
            with act.Fori(0, CHUNKS) as c:
                for p in range(PAIRS):
                    exp_unit(q_f, q_f[3], p % 3, c, p)

            act.wait_ge(blocks_zero, 3)

            def vw_copy(it, b):
                g = it * 2 + b
                act.wait_ge(core_vw, g + 3)
                act.wait_ge(core_y, g + 1)
                for odd in range(2):
                    rows = slice(64 * odd, 64 * odd + 64)
                    act.activation(vw[rows, b, odd::2, :],
                                   bank[0][rows, 0:QUADS * 128].rearrange("p (q e) -> p q e", q=QUADS),
                                   ACT.Copy).then_inc(core_vw_out, 1)

            def square(it, b):
                g = it * 2 + b
                act.wait_ge(core_y, g + 3)
                act.wait_ge(core_sum, g + 1)
                for q in range(2):
                    act.activation(sq[:, 3 * q:3 * q + 3, :],
                                         bank[4 + q][:, 0:3 * GROUP].rearrange("p (a t) -> p a t", a=3),
                                         ACT.Square, bias=bias_of(2 * STAGES - 1)).then_inc(core_sq, 1)
            vw_copy(0, 0)
            with act.Fori(0, GROUPS // 2 - 1) as it:
                square(it, 0)
                vw_copy(it, 1)
                square(it, 1)
                vw_copy(it + 1, 0)
            square(GROUPS // 2 - 1, 0)
            vw_copy(GROUPS // 2 - 1, 1)
            square(GROUPS // 2 - 1, 1)
            r_act(act, core_var, STAGES, ((0, HEAD * CHUNK, -(-HEAD * CHUNK // GROUP) + 1),
                                            (HEAD * CHUNK, TOKENS, GROUPS + 1)))
            for i in range(STAGES):
                G = es[i]
                s = 2 * STAGES - 1 - i
                act.preload_act_table(ACT.Gelu)

                def gf_body(c, before, more):
                    for p in range(PAIRS):
                        g_act(act, G, s, CHUNK, c, p, consumed=(i == STAGES - 1))
                        if i < STAGES - 1:
                            if p:
                                f_act(act, es[i + 1], s - 1, CHUNK, c, p - 1)
                            elif before:
                                f_act(act, es[i + 1], s - 1, CHUNK, c - 1, PAIRS - 1)
                if i < STAGES - 1:
                    chunks_with_ends(act, gf_body)
                    f_act(act, es[i + 1], s - 1, CHUNK, CHUNKS - 1, PAIRS - 1)
                    r_act(act, es[i + 1].var_out, STAGES + 2 * (i + 1),
                          ((0, HEAD * CHUNK, HEAD + 1), (HEAD * CHUNK, TOKENS, CHUNKS + 1)))
                else:
                    with act.Fori(0, CHUNKS) as c:
                        gf_body(c, False, False)

            act.preload_act_table_set(LN_EXP_TABLES)
            act.wait_ge(mv_out, TILES)
            act.activation(ln2[:, :], mv2[:, :, 1], ACT.Ln, bias=eps[:, :]).then_inc(ln2_log, 1)
            act.wait_ge(ln2_log, 1)
            act.activation(rs2[:, :], ln2[:, :], ACT.Exp, scale=-0.5).then_inc(ln2_r, 1)
            with act.Fori(0, TILES // 3) as it:
                for j in range(3):
                    t = it * 3 + j
                    act.wait_ge(x2_out, t + 1)
                    for seg in SEGMENTS:
                        act.activation(x2part(t, 0, *seg), x2_ring[j][:, seg[0]:seg[0] + seg[1]].unsqueeze(1),
                                       ACT.Copy).then_inc(x2_values, 1)
                    act.wait_ge(x2T_ps, t + 1)
                    act.wait_ge(logit_ps, t + 1)
                    act.activation(x2T_ring[j],
                                   bank[j][0:HALF, 0:2 * TILE].rearrange("p (h t) -> p h t", h=2),
                                   ACT.Copy).then_inc(x2T_out, 1)
            act.wait_ge(rt_abs, 1)
            act.activation(rt[:, 2, :], rt[:, 1, :], ACT.Exp, scale=-1.0).then_inc(rt_act, 1)
            act.wait_ge(rt_act, 1)
            act.activation(rt[:, 3, :], rt[:, 2, :], ACT.Ln, bias=1.0).then_inc(rt_act, 1)
            act.wait_ge(rt_sp, 1)
            act.activation(rt[:, 2, :], rt[:, 1, :], ACT.Sqrt).then_inc(rt_act, 1)

            def turned(n, b):
                act.wait_ge(row_used, n + 1)
                act.wait_ge(gu_ps, n * UNITS - 3) if not isinstance(n, int) or n >= 2 else None
                act.activation(xT16[:, b, 0:3, :],
                               bank16[7][:, 0:3 * TILE].rearrange("p (k t) -> p k t", k=3),
                               ACT.Copy).then_inc(xT_out, 1)

            def silu(n, u):
                act.wait_ge(gu_ps, n * UNITS + u + 1)
                act.wait_ge(hid_out, n * UNITS + u - 2) if not isinstance(n, int) or n >= 1 else None
                act.activation(sgate[:, u, :], bank[u][:, 0:UNIT], ACT.Silu, scale=1.0 / SCALE).then_inc(silu_out, 1)

            def hid_copy(n, u):
                act.wait_ge(hidT_ps, n * UNITS + u + 1)
                act.wait_ge(y_ps, n * UNITS + u - 2) if not isinstance(n, int) or n >= 1 else None
                act.activation(hidT[:, u, :, :], bank16[3 + u][:, 0:512].rearrange("p (k t) -> p k t", k=4),
                               ACT.Copy).then_inc(hidT_out, 1)

            def tile(n, b, first=False, more=True):
                for u in range(UNITS):
                    silu(n, u)
                    if u == 0 and more:
                        turned(n + 1, 1 - b)
                    if u == 2:
                        hid_copy(n, 0)
                    elif not first:
                        hid_copy(n - 1, u + 1)
            turned(0, 0)
            tile(0, 0, first=True)
            tile(1, 1)
            with act.Fori(1, (TILES + ROUTED_TILES) // 2 - 1) as it:
                for b in range(2):
                    tile(it * 2 + b, b)
            n = TILES + ROUTED_TILES - 2
            tile(n, 0)
            tile(n + 1, 1, more=False)
            hid_copy(n + 1, 1)
            hid_copy(n + 1, 2)

            for c in range(CHUNKS):
                act.wait_ge(comb, 3 * c + 3)
                act.dma_start(out[c * CHUNK:(c + 1) * CHUNK, :].rearrange("(t p) d -> p t d", p=TILE),
                              resid[:, c * 3:c * 3 + 3, :]).then_inc(stored, 16)
            act.wait_ge(stored, 16 * CHUNKS)

        @block.vector
        def _(dve):
            def routing():
                count = [0]

                def step(ins, signal=None):
                    if signal is None:
                        count[0] += 1
                        ins.then_inc(rt_step, 1)
                        dve.wait_ge(rt_step, count[0])
                    else:
                        ins.then_inc(signal, 1)
                        dve.wait_ge(signal, 1)

                def by_token(x):
                    return x.rearrange("p (t e) -> p t e", t=TILES)

                def over_experts(x):
                    return x.unsqueeze(2).to_broadcast([128, TILES, EXPERTS])

                L, A, E, LN, SC, R, TMP, M, M1, M2, SA, SB = (rt[:, k, :] for k in range(12))
                s1, s2, w1, w2, inv, pos = (small[:, k, :] for k in range(6))
                step(dve.scalar_tensor_tensor(out=A, in0=L, scalar=-1.0, in1=L, op0=ALU.mult, op1=ALU.max), rt_abs)
                dve.wait_ge(rt_act, 2)
                step(dve.tensor_scalar(SC, E, -1.0 / 6, None, ALU.mult))
                for c in (1.0 / 5, -1.0 / 4, 1.0 / 3, -1.0 / 2, 1.0):
                    step(dve.scalar_tensor_tensor(out=SC, in0=SC, scalar=c, in1=E, op0=ALU.add, op1=ALU.mult))
                step(dve.tensor_tensor(SC, SC, LN, ALU.subtract))
                step(dve.scalar_tensor_tensor(out=SC, in0=E, scalar=0.06, in1=SC, op0=ALU.is_lt, op1=ALU.mult))
                step(dve.tensor_tensor(LN, LN, SC, ALU.add))
                step(dve.scalar_tensor_tensor(out=A, in0=L, scalar=0.0, in1=LN, op0=ALU.max, op1=ALU.add))
                step(dve.tensor_scalar(A, A, 1e-30, None, ALU.max), rt_sp)
                dve.wait_ge(rt_act, 3)
                step(dve.reciprocal(LN, E))
                step(dve.scalar_tensor_tensor(out=LN, in0=A, scalar=0.5, in1=LN, op0=ALU.mult, op1=ALU.mult))
                step(dve.scalar_tensor_tensor(out=SC, in0=E, scalar=0.5, in1=LN, op0=ALU.mult, op1=ALU.add))
                step(dve.tensor_tensor(by_token(R), by_token(SC),
                                       gbias[:, :].unsqueeze(1).to_broadcast([128, TILES, EXPERTS]), ALU.add))
                for mk in (M1, M2):
                    step(dve.tensor_reduce(s1, by_token(R), AX.X, ALU.max))
                    step(dve.tensor_tensor(by_token(TMP), by_token(R), over_experts(s1), ALU.is_equal))
                    step(dve.scalar_tensor_tensor(out=TMP, in0=TMP, scalar=-100.0, in1=iota_e[:, :], op0=ALU.mult,
                                                  op1=ALU.add))
                    step(dve.tensor_reduce(s2, by_token(TMP), AX.X, ALU.min))
                    step(dve.tensor_scalar(TMP, iota_e[:, :], -100.0, None, ALU.add))
                    step(dve.tensor_tensor(by_token(mk), by_token(TMP), over_experts(s2), ALU.is_equal))
                    if mk is M1:
                        step(dve.scalar_tensor_tensor(out=R, in0=M1, scalar=-1e30, in1=R, op0=ALU.mult, op1=ALU.add))
                step(dve.tensor_tensor(M, M1, M2, ALU.add), rt_masks)
                dve.wait_ge(rt_prefix, 1)
                step(dve.tensor_copy(L, bank[1][:, 0:N144]))
                step(dve.tensor_copy(A, bank[0][:, 0:N144]), prefix_read)
                src, dst = L, SA
                shift = 1
                while shift < TILES:
                    n = shift * EXPERTS
                    step(dve.tensor_copy(dst[:, 0:n], src[:, 0:n]))
                    step(dve.tensor_tensor(dst[:, n:N144], src[:, n:N144], src[:, 0:N144 - n], ALU.add))
                    src, dst = dst, (SB if dst is SA else SA)
                    shift *= 2
                total = ecount[:, 0, :]
                step(dve.tensor_copy(total, src[:, N144 - EXPERTS:N144]))
                step(dve.tensor_tensor(TMP, src, L, ALU.subtract))
                step(dve.tensor_tensor(TMP, TMP, A, ALU.add))
                tiles = ecount[:, 1, :]
                by_expert = SA.rearrange("p (e j) -> p e j", e=EXPERTS)
                step(dve.tensor_tensor(by_expert, iota_tok[:, :].rearrange("p (e j) -> p e j", e=EXPERTS),
                                       total.unsqueeze(2).to_broadcast([128, EXPERTS, TILES]), ALU.is_lt))
                step(dve.tensor_reduce(tiles, by_expert, AX.X, ALU.add))
                step(dve.tensor_copy(ecount[:, 2, :], tiles))
                src, dst = ecount[:, 2, :], ecount[:, 3, :]
                for n in (1, 2, 4):
                    step(dve.tensor_copy(dst[:, 0:n], src[:, 0:n]))
                    step(dve.tensor_tensor(dst[:, n:EXPERTS], src[:, n:EXPERTS], src[:, 0:EXPERTS - n], ALU.add))
                    src, dst = dst, src
                ends = src
                step(dve.tensor_tensor(cmp_tile[:, :, :], iota_tile[:, :, :],
                                       ends[0:1, :].unsqueeze(1).to_broadcast([1, ROUTED_TILES, EXPERTS]), ALU.is_ge))
                step(dve.tensor_reduce(tile_expert[:, :], cmp_tile[:, :, :], AX.X, ALU.add))
                step(dve.memset(tab[:, 0:1], SHARED))
                step(dve.tensor_scalar(tab[:, 1:1 + ROUTED_TILES], tile_expert[:, :], float(EXPERTS - 1), None,
                                       ALU.min), tab_ready)
                step(dve.tensor_tensor(dst, ends, tiles, ALU.subtract))
                step(dve.tensor_scalar(dst, dst, float(TILE), None, ALU.mult))
                step(dve.tensor_tensor(by_token(TMP), by_token(TMP),
                                       dst.unsqueeze(1).to_broadcast([128, TILES, EXPERTS]), ALU.add))
                for k, mk in enumerate((M1, M2)):
                    step(dve.tensor_tensor(R, mk, TMP, ALU.mult))
                    step(dve.tensor_reduce(pos, by_token(R), AX.X, ALU.add))
                    step(dve.tensor_copy(slot[:, k, :], pos), slots_ready if k else None)

                def weights():
                    for mk, s in ((M1, s1), (M2, s2)):
                        step(dve.tensor_tensor(TMP, mk, SC, ALU.mult))
                        step(dve.tensor_reduce(s, by_token(TMP), AX.X, ALU.add))
                    step(dve.tensor_tensor(inv, s1, s2, ALU.add))
                    step(dve.tensor_scalar(inv, inv, 1e-6, None, ALU.max))
                    step(dve.reciprocal(pos, inv))
                    for w, s in ((w1, s1), (w2, s2)):
                        step(dve.scalar_tensor_tensor(out=w, in0=s, scalar=1.0 / (SCALE * SCALE), in1=pos, op0=ALU.mult,
                                                      op1=ALU.mult))
                return weights

            dve.sem_inc(emb_read, 2)
            for P in ks + es[1:]:
                dve.sem_inc(P.y_out, 3)
                dve.sem_inc(P.var_out, 1)
                dve.sem_inc(P.sums, 3)
            for P in ks + es:
                dve.sem_inc(P.z_out, 3)
            for P in (ks[0], ks[1], es[2]):
                dve.sem_inc(P.next_out, 3)
            for s in (k_f[3], q_f[3], k_f[4]):
                dve.sem_inc(s, 3)
            dve.sem_inc(core_vw, 2)
            dve.sem_inc(core_sm, 1)
            dve.sem_inc(core_chain, 1)
            dve.sem_inc(core_sn, 1)
            dve.sem_inc(core_y, 2)
            dve.sem_inc(core_y_out, 2)
            dve.sem_inc(core_sum, 1)
            dve.sem_inc(core_var, 1)
            dve.sem_inc(wo_read, 3)
            dve.sem_inc(logit_out, 3)
            dve.sem_inc(logit_ps, 3)
            dve.sem_inc(x2_rests, 6)
            dve.sem_inc(up_out, 3)
            dve.sem_inc(y_read, 1)
            dve.wait_ge(small_in, 16 * SMALL_LOADS)
            dve.tensor_tensor(bboth[:, :], bproj[:, :], bo[:, :], ALU.add).then_inc(prep, 1)
            dve.wait_ge(prep, 1)

            with dve.Fori(0, TILES // 2) as it:
                for b in range(2):
                    t = it * 2 + b
                    dve.wait_ge(embedded, t + 1)
                    dve.tensor_tensor(hrow[:, b, :], bank[b][:, 0:DIM], bproj[:, :], ALU.add).then_inc(ln1_dve, 1)
                    dve.wait_ge(ln1_dve, t * 2 + 1)
                    dve.bn_stats(stats[:, b, :], hrow[:, b, :]).then_inc(ln1_dve, 1)
                    dve.wait_ge(ln1_dve, t * 2 + 2)
                    dve.tensor_tensor(resid[:, ds(t, 1), :], bank[b][:, 0:DIM].unsqueeze(1), bboth[:, :].unsqueeze(1),
                                      ALU.add).then_inc(emb_read, 1)
                    dve.bn_aggr(mv1[:, b, :], stats[:, b, :]).then_inc(ln1_stat, 1)
                    dve.wait_ge(ln1_act, t * 2 + 2)
                    dve.wait_ge(ln1_stat, t + 1)
                    dve.tensor_scalar(xrow[:, b, :], hrow[:, b, :], mv1[:, b, 0:1], rs1[:, b:b + 1],
                                      ALU.subtract, ALU.mult).then_inc(x1_ready, 1)
            def cut_exp(S, c, p):
                dve.wait_ge(S[1], c * PAIRS + p + 1)
                dve.tensor_scalar(gb[:, p % 3, :], gb[:, p % 3, :], 1.0, None, ALU.min).then_inc(S[2], 1)

            def finish_map(S, dst, src, c, p):
                dve.wait_ge(S[2], c * PAIRS + p + 1)
                dve.scalar_tensor_tensor(out=dst, in0=bank[src][:, 0:CHUNK], scalar=1.0, in1=gb[:, p % 3, :],
                                         op0=ALU.add, op1=ALU.max).then_inc(S[3], 1)

            def pool_unit(c, p):
                dve.wait_ge(k_f[3], c * PAIRS + p + 4)
                dve.tensor_tensor(kp1[:, p, ds(c * (CHUNK // 2), CHUNK // 2)], gb[:, p % 3, 0::2],
                                  gb[:, p % 3, 1::2], ALU.add).then_inc(k_f[4], 1)

            def keys(c):
                for p in range(PAIRS):
                    cut_exp(k_f, c, p)
                    if p:
                        pool_unit(c, p - 1)
                    finish_map(k_f, gb[:, p % 3, :], K_BANKS[p], c, p)
                pool_unit(c, PAIRS - 1)
            xv = x1T[0:HALF].rearrange("p h (i t) -> p h i t", t=TOKENS_PER_IMAGE)

            def pooled_rows(h):
                images = slice(h * IMAGES, (h + 1) * IMAGES)
                dve.tensor_reduce(xp[0:HALF, images, 0:4], xv[:, h, :, 0:32].rearrange("p i (r t) -> p i r t", t=8),
                                  AX.X, ALU.add).then_inc(xp_out, 1)
                dve.tensor_reduce(xp[0:HALF, images, 4:5], xv[:, h, :, 32:36].unsqueeze(2), AX.X,
                                  ALU.add).then_inc(xp_out, 1)
            dve.wait_ge(x1T_ready, TILES + 2)
            for c in range(2):
                keys(c)
                pooled_rows(c)
            with dve.Fori(2, CHUNKS - 1) as c:
                keys(c)
            dve.wait_ge(wbd_in, 32)
            dve.tensor_reduce(wsum[:, :], wbd[:, :, :], AX.X, ALU.add).then_inc(prep, 1)
            dve.wait_ge(prep, 2)
            dve.tensor_scalar(wmean[:, :], wsum[:, :], 1.0 / HEAD_DIM, None, ALU.mult).then_inc(prep, 1)
            dve.wait_ge(prep, 3)
            for a in range(2):
                rows, cols = slice(64 * a, 64 * a + 64), slice(64 * a, 64 * a + 64)
                dve.tensor_tensor(wbd[rows, :, cols], wbd[rows, :, cols],
                                  wmean[rows, :].unsqueeze(2).to_broadcast([64, 2 * STAGES, 64]),
                                  ALU.subtract).then_inc(prep, 1)
            dve.wait_ge(prep, 5)
            dve.tensor_scalar(wbd[:, 0:STAGES, :], wbd[:, 0:STAGES, :], 0.5, None, ALU.mult).then_inc(prep, 1)
            dve.wait_ge(bmean_ready, 1)
            dve.tensor_tensor(bcen[:, :], vecs[:, 0:2 * STAGES], bank[7][:, 0:2 * STAGES],
                              ALU.subtract).then_inc(prep, 1)
            dve.wait_ge(prep, PREP)
            keys(CHUNKS - 1)
            for i in range(STAGES):
                buf, n, chunks = KSTAGE[i]
                P = ks[i]

                def f_body(c):
                    for p in range(PAIRS):
                        f_dve(dve, P, i, buf[:, p, ds(c * n, n)], n, c, p)
                    var_dve(dve, P, n, c)
                loop(dve, chunks, f_body)
                r_dve(dve, n * chunks, i)

                def g_body(c):
                    def pool_pair(p):
                        dve.wait_ge(P.g_out, c * PAIRS + p + 4)
                        if i == 0:
                            dve.tensor_tensor(kp2[:, p, ds(c * (n // 2), n // 2)], gb[:, p % 3, 0:n:2],
                                              gb[:, p % 3, 1:n:2], ALU.add).then_inc(P.next_out, 1)
                        elif i == 1:
                            rows = gb[:, p % 3, 0:n].rearrange("p (i r) -> p i r", r=9)
                            dst = kc3[:, p, ds(c * (K3 // 2), K3 // 2)].rearrange("p (i r) -> p i r", r=POOLED)
                            dve.tensor_tensor(dst[:, :, 0:4], rows[:, :, 0:8:2], rows[:, :, 1:8:2],
                                              ALU.add).then_inc(k_main, 1)
                            dve.wait_ge(k_main, c * PAIRS + p + 1)
                            dve.tensor_copy(dst[:, :, 4:5], rows[:, :, 8:9]).then_inc(P.next_out, 1)
                    for p in range(PAIRS):
                        z_dve(dve, P, buf[:, p, ds(c * n, n)], n, c, p)
                        if p and i < 2:
                            pool_pair(p - 1)
                    if i < 2:
                        pool_pair(PAIRS - 1)
                loop(dve, chunks, g_body)
            with dve.Fori(0, CHUNKS) as c:
                for p in range(PAIRS):
                    cut_exp(q_f, c, p)
                    finish_map(q_f, q_y[:, p, ds(c * CHUNK, CHUNK)], p % 3, c, p)

            def masked(it, b):
                g = it * 2 + b
                dve.wait_ge(core_s, g + 1)
                dve.tensor_tensor(sm[:, b, :, :], bank[1][:, 0:QUADS * GROUP].rearrange("p (q t) -> p q t", q=QUADS),
                                  mask[:, :].unsqueeze(1).to_broadcast([128, QUADS, GROUP]), ALU.mult).then_inc(core_sm, 1)

            def inverse(it, b):
                g = it * 2 + b
                dve.wait_ge(core_den, g + 1)
                dve.wait_ge(core_rb, g) if not isinstance(g, int) or g > 0 else None
                dve.tensor_scalar(den[:, :], bank[2][0:96, 0:GROUP], DEN_EPS, None, ALU.add).then_inc(core_chain, 1)
                dve.wait_ge(core_chain, g * 6 + 2)
                dve.reciprocal(rden[:, :], den[:, :]).then_inc(core_chain, 1)
                dve.wait_ge(core_chain, g * 6 + 3)
                split_dve(dve, rden, dsplit, GROUP, core_chain, g * 6 + 3).then_inc(core_r, 1)

            def normalised(it, b):
                g = it * 2 + b
                dve.wait_ge(core_rb, g + 1)
                dve.tensor_tensor(sn[:, b, :, :], sm[:, b, :, :],
                                  bank[3][:, 0:QUADS * GROUP].rearrange("p (q t) -> p q t", q=QUADS),
                                  ALU.mult).then_inc(core_sn, 1)

            def y_copy(it, b):
                g = it * 2 + b
                dve.wait_ge(core_sq, g * 2 + 4)
                for q in range(2):
                    dve.tensor_scalar(q_y[:, 3 * q:3 * q + 3, ds(g * GROUP, GROUP)],
                                            bank[4 + q][:, 0:3 * GROUP].rearrange("p (a t) -> p a t", a=3),
                                            bias_of(2 * STAGES - 1), None, ALU.add).then_inc(core_y_out, 1)
                dve.wait_ge(core_sum, g + 2)
                dve.tensor_copy(var[:, ds(g * GROUP, GROUP)], bank[6][0:96, 0:GROUP]).then_inc(core_var, 1)

            def core_step(it, b, last=False):
                normalised(it, b)
                if not last:
                    masked(it + b, 1 - b)
                    inverse(it + b, 1 - b)
                y_copy(it, b)
            masked(0, 0)
            inverse(0, 0)
            with dve.Fori(0, GROUPS // 2 - 1) as it:
                core_step(it, 0)
                core_step(it, 1)
            core_step(GROUPS // 2 - 1, 0)
            core_step(GROUPS // 2 - 1, 1, last=True)
            rows = [hrow[:, 0, :], hrow[:, 1, :], xrow[:, 0, :]]
            for i in range(STAGES):
                G = es[i]
                s = 2 * STAGES - 1 - i

                def z(c, p):
                    z_dve(dve, G, q_y[:, p, ds(c * CHUNK, CHUNK)], CHUNK, c, p)

                def to_sbuf(c, p):
                    f_dve(dve, es[i + 1], s - 1, q_y[:, p, ds(c * CHUNK, CHUNK)], CHUNK, c, p)

                def residual(c):
                    dve.wait_ge(G.next_out, c * PAIRS + PAIRS + 3)
                    for j in range(3):
                        dve.tensor_tensor(rows[j], bank[3 + j][:, 0:DIM],
                                          resid[:, ds(c * 3 + j, 1), :].rearrange("p a d -> p (a d)"),
                                          ALU.add).then_inc(wo_read, 1)
                    dve.wait_ge(wo_read, c * 3 + 6)
                    for j in range(3):
                        dve.bn_stats(stats[:, j, :], rows[j]).then_inc(ln2_chain, 1)
                    dve.wait_ge(ln2_chain, c * 9 + 3)
                    for j in range(3):
                        dve.tensor_scalar(resid[:, ds(c * 3 + j, 1), :], rows[j].unsqueeze(1), 1.0, None,
                                          ALU.mult).then_inc(ln2_chain, 1)

                def aggregate(c):
                    for j in range(3):
                        dve.bn_aggr(mv1[:, j, :], stats[:, j, :]).then_inc(ln2_chain, 1)
                    dve.wait_ge(ln2_chain, c * 9 + 9)
                    for j in range(3):
                        dve.tensor_scalar(mv2[:, ds(c * 3 + j, 1), :], mv1[:, j, :].unsqueeze(1), 1.0, None,
                                          ALU.mult).then_inc(mv_out, 1)

                def gf_body(c, before, more):
                    for p in range(PAIRS):
                        if p + 1 < PAIRS:
                            z(c, p + 1)
                        elif more:
                            z(c + 1, 0)
                        if p == 2 and more:
                            r_chunk(dve, i, c + 1)
                        if i < STAGES - 1:
                            if p == 0 and before:
                                to_sbuf(c - 1, PAIRS - 1)
                            if p == 1 and before:
                                var_dve(dve, es[i + 1], CHUNK, c - 1)
                            if p:
                                to_sbuf(c, p - 1)
                        elif before and p == 0:
                            residual(c - 1)
                        elif before and p == 1:
                            aggregate(c - 1)
                r_chunk(dve, i, 0)
                z(0, 0)
                chunks_with_ends(dve, gf_body)
                if i < STAGES - 1:
                    to_sbuf(CHUNKS - 1, PAIRS - 1)
                    var_dve(dve, es[i + 1], CHUNK, CHUNKS - 1)
                else:
                    residual(CHUNKS - 1)
                    aggregate(CHUNKS - 1)
            dve.wait_ge(ln2_r, 1)
            dve.wait_ge(wo_read, TILES + 3)
            def x2(t, j):
                dve.wait_ge(x2_rests, t * 2 + 2)
                dve.tensor_scalar(x2_ring[j].unsqueeze(1), resid[:, ds(t, 1), :], mv2[:, ds(t, 1), 0],
                                  rs2[:, ds(t, 1)], ALU.subtract, ALU.mult).then_inc(x2_out, 1)

            def logits(c, before, more):
                for j in range(3):
                    t = c * 3 + j
                    if more or j == 0:
                        x2(t + 2, (j + 2) % 3)
                    dve.wait_ge(x2_values, t * 2 + 2)
                    for seg in SEGMENTS:
                        dve.tensor_tensor(x2part(t, 1, *seg), x2_ring[j][:, seg[0]:seg[0] + seg[1]].unsqueeze(1),
                                          x2part(t, 0, *seg), ALU.subtract).then_inc(x2_rests, 1)
                    dve.wait_ge(logit_ps, t + 4)
                    dve.tensor_copy(rt[:, 0, ds(t * EXPERTS, EXPERTS)], bank[3 + j][:, 0:EXPERTS]).then_inc(logit_out, 1)
            x2(0, 0)
            x2(1, 1)
            chunks_with_ends(dve, logits)
            dve.wait_ge(logit_out, TILES + 3)
            dve.wait_ge(x2_rests, 2 * TILES + 6)
            weights = routing()

            def hidden(n, u, between=None):
                dve.wait_ge(silu_out, n * UNITS + u + 4)
                dve.tensor_scalar(sup[:, u, :], bank[u][:, UNIT:2 * UNIT], LIMIT * SCALE, -LIMIT * SCALE, ALU.min,
                                  ALU.max).then_inc(up_out, 1)
                if between is not None:
                    between()
                dve.wait_ge(up_out, n * UNITS + u + 4)
                dve.wait_ge(hidT_ps, n * UNITS + u - 2) if not isinstance(n, int) or n >= 1 else None
                for dst in (hsplit[:, u, 0, :], hid[:, u, :]):
                    dve.scalar_tensor_tensor(out=dst, in0=sgate[:, u, :], scalar=SILU_LIMIT, in1=sup[:, u, :],
                                             op0=ALU.min, op1=ALU.mult).then_inc(hid_parts, 1)
                dve.wait_ge(hid_parts, (n * UNITS + u) * 2 + 2)
                dve.tensor_tensor(hsplit[:, u, 1, :], hid[:, u, :], hsplit[:, u, 0, :],
                                  ALU.subtract).then_inc(hid_out, 1)

            def finish(n, b, shared, m=None):
                dve.wait_ge(y_ps, (n + 1) * UNITS)
                if shared:
                    dve.scalar_tensor_tensor(out=resid[:, ds(n, 1), :], in0=bank[6][:, 0:DIM].unsqueeze(1),
                                             scalar=1.0 / (SCALE * SCALE), in1=resid[:, ds(n, 1), :], op0=ALU.mult,
                                             op1=ALU.add).then_inc(y_read, 1)
                else:
                    dve.wait_ge(y_stored[b], m * 16) if not isinstance(m, int) or m > 0 else None
                    dve.tensor_copy(orow[:, b, :], bank[6][:, 0:DIM]).then_inc(y_read, 1)

            def tile(n, finish_before=None):
                for u in range(UNITS):
                    hidden(n, u, finish_before if u == UNITS - 1 else None)
            dve.wait_ge(zeroed, 16 * PADS)
            tile(0)
            tile(1, lambda: finish(0, 0, True))
            with dve.Fori(1, TILES // 2) as it:
                for b in range(2):
                    tile(it * 2 + b, lambda: finish(it * 2 + b - 1, 1 - b, True))
            tile(TILES, lambda: finish(TILES - 1, 1, True))
            tile(TILES + 1, lambda: finish(TILES, 0, False, 0))
            tile(TILES + 2, lambda: finish(TILES + 1, 1, False, 0))
            tile(TILES + 3, lambda: finish(TILES + 2, 0, False, 1))
            with dve.Fori(2, ROUTED_TILES // 2) as it:
                n = it * 2 + TILES
                tile(n, lambda: finish(n - 1, 1, False, it - 1))
                tile(n + 1, lambda: finish(n, 0, False, it))
            finish(TILES + ROUTED_TILES - 1, 1, False, ROUTED_TILES // 2 - 1)

            weights()
            for t in range(TILES):
                dve.wait_ge(returned[t // 3], 32)
                for k, done in ((0, comb_step), (1, comb)):
                    dve.scalar_tensor_tensor(out=resid[:, t, :], in0=gath[:, k, t, :], scalar=small[:, 2 + k, t:t + 1],
                                             in1=resid[:, t, :], op0=ALU.mult, op1=ALU.add).then_inc(done, 1)
                    if k == 0:
                        dve.wait_ge(comb_step, t + 1)


def kernel(**inputs):
    import numpy as np
    import concourse.bacc as bacc
    from concourse.bass_utils import run_bass_kernel_spmd as run

    a = {k: np.asarray(v) for k, v in inputs.items()}
    P = 16
    x = a["x"].reshape(IMAGES, 3, 6, P, 6, P).transpose(0, 2, 4, 1, 3, 5).reshape(TILES, TILE, PATCH_DIM // 128, 128)

    def halves(w):
        return w.reshape(2, HALF, -1).transpose(1, 0, 2)

    w1 = np.concatenate([a["L0_ffn_w1"], a["L0_ffn_w1s"][None]])
    w3 = np.concatenate([a["L0_ffn_w3"], a["L0_ffn_w3s"][None]])
    w2 = np.concatenate([a["L0_ffn_w2"], a["L0_ffn_w2s"][None]])
    w13 = np.stack([w.reshape(EXPERTS + 1, DIM, UNITS, UNIT) for w in (w1, w3)], 3).reshape(EXPERTS + 1, DIM, 2 * HIDDEN)
    w13 = np.concatenate([w13[:, :TILE], np.concatenate([w13[:, TILE:], w13[:, TILE:]], 1)], 2)
    vecs = np.concatenate([a["L0_attn_" + k + v] for v in ("_b", "_g", "_be") for k in ("pool", "exp")])
    arrays = {
        "patches": x.transpose(0, 3, 2, 1),
        "wp": a["L0_tok_W_proj"].reshape(DIM, PATCH_DIM // 128, 128).transpose(2, 1, 0),
        "bproj": np.broadcast_to(a["L0_tok_b_proj"], (128, DIM)),
        "bo": np.broadcast_to(a["L0_attn_bo"], (128, DIM)),
        "vecs": np.concatenate([vecs.T, vecs.T]),
        "gbias": np.broadcast_to(a["L0_ffn_gate_bias"], (128, EXPERTS)),
        "gatew": halves(a["L0_ffn_gate_w"]),
        "wq": halves(a["L0_attn_Wq"]),
        "wk": halves(a["L0_attn_Wk"]),
        "wv": halves(a["L0_attn_Wv"]),
        "wo": a["L0_attn_Wo"].reshape(PAIRS, 128, DIM).transpose(1, 0, 2),
        "maps": np.concatenate([a["L0_attn_pool_W"], a["L0_attn_exp_W"]]).transpose(1, 0, 2),
        "w13": w13,
        "w2": w2.reshape(EXPERTS + 1, HIDDEN // 128, 128, DIM).transpose(0, 2, 1, 3).reshape(EXPERTS + 1, 128, W2),
    }
    nc = bacc.Bacc("TRN2", target_bir_lowering=False, num_devices=1)
    arrays = {k: np.ascontiguousarray(v) for k, v in arrays.items()}
    dram = {k: nc.dram_tensor(f"in_{k}", v.shape, F32, kind="ExternalInput").ap() for k, v in arrays.items()}
    dram["slots"] = nc.dram_tensor("slots", (ROUTED_TILES * TILE, ROW), F16).ap()
    dram["parts"] = nc.dram_tensor("parts", (EXPERTS + 1, 128, 2 * (W13 + W2)), F16).ap()
    dram["expert_out"] = nc.dram_tensor("expert_out", (2 * TOKENS + TILE, DIM), F32).ap()
    out = nc.dram_tensor("out", (TOKENS, DIM), F32, kind="ExternalOutput").ap()
    build(nc, dram, out)
    r = run(nc, [{f"in_{k}": v for k, v in arrays.items()}], core_ids=[0])
    return r.results[0]["out"].reshape(IMAGES, TOKENS_PER_IMAGE, DIM)
```
